# Optimizing a Trainium2 kernel written in Bass

```python
import numpy as np
import jax
import jax.numpy as jnp

def _softmax(x, axis=-1):
    return jax.nn.softmax(x, axis=axis)

def _gelu(x):
    return jax.nn.gelu(x, approximate=True)

def _silu(x):
    return jax.nn.silu(x)

def _sigmoid(x):
    return jax.nn.sigmoid(x)

def _layernorm(x, axis=-1, eps=1e-05):
    m = jnp.mean(x, axis=axis, keepdims=True)
    v = jnp.var(x, axis=axis, keepdims=True)
    return (x - m) / jnp.sqrt(v + eps)

def _scatter_add(tgt, idx, src, axis=0):
    return tgt.at[idx].add(src)

def _segment_sum(src, seg, n):
    return jax.ops.segment_sum(src, seg, n)
kernel_name = 'mk_gnn_preln_d2_gnn_r8_2f9de0'

def setup_inputs(seed: int=0):
    np.random.seed(seed)
    _w = jnp.asarray

    def _rec_inputs():
        import jax
        import jax.numpy as jnp
        _gk = jax.random.key(seed)
        x = -0.000202 + 1 * jax.random.normal(jax.random.fold_in(_gk, 1), (6250, 128), jnp.float32)
        _s = jax.random.randint(jax.random.fold_in(_gk, 2), (100000,), 0, 6250, jnp.int32)
        _d = jax.random.randint(jax.random.fold_in(_gk, 3), (100000,), 0, 6250, jnp.int32)
        _loop = jnp.arange(6250, dtype=jnp.int32)
        src = jnp.concatenate([_s, _d, _loop])
        dst = jnp.concatenate([_d, _s, _loop])
        _o = jnp.argsort(dst, stable=True)
        src = src[_o]
        dst = dst[_o]
        return (x, src, dst)
    x, src, dst = _rec_inputs()

    def _L0_gnn_setup():
        import jax, jax.numpy as jnp
        import numpy as np
        N = 6250
        IN_DIM = 128
        OUT_DIM = 128
        HEADS = 2
        EPS = 1e-05
        NEG_SLOPE = 0.2

        def _add_self_loops(edge_index, num_nodes):
            loop = jnp.arange(num_nodes, dtype=edge_index.dtype)
            src = jnp.concatenate([edge_index[0], loop])
            dst = jnp.concatenate([edge_index[1], loop])
            return (src, dst)

        def _layernorm(h, gamma, beta):
            mu = jnp.mean(h, axis=-1, keepdims=True)
            var = jnp.mean(jnp.square(h - mu), axis=-1, keepdims=True)
            return (h - mu) * jax.lax.rsqrt(var + EPS) * gamma + beta

        def _silu(h):
            return h * jax.nn.sigmoid(h)

        def _gcn_conv(x, src, dst, W, b, num_nodes):
            h = x @ W
            deg = jnp.zeros((num_nodes,), h.dtype).at[dst].add(1.0)
            dinv = jnp.where(deg > 0, jax.lax.rsqrt(jnp.maximum(deg, 1.0)), 0.0)
            norm = dinv[src] * dinv[dst]
            msg = h[src] * norm[:, None]
            out = jnp.zeros((num_nodes, h.shape[1]), h.dtype).at[dst].add(msg)
            return out + b

        def _gat_conv(x, src, dst, W, att_src, att_dst, b, num_nodes, heads):
            C = W.shape[1] // heads
            h = (x @ W).reshape(num_nodes, heads, C)
            a_src = jnp.sum(h * att_src, axis=-1)
            a_dst = jnp.sum(h * att_dst, axis=-1)
            e = a_src[src] + a_dst[dst]
            e = jnp.where(e > 0, e, NEG_SLOPE * e)
            m = jax.ops.segment_max(e, dst, num_segments=num_nodes)
            ex = jnp.exp(e - m[dst])
            den = jax.ops.segment_sum(ex, dst, num_segments=num_nodes)
            alpha = ex / den[dst]
            msg = h[src] * alpha[:, :, None]
            out = jnp.zeros((num_nodes, heads, C), h.dtype).at[dst].add(msg)
            return jnp.mean(out, axis=1) + b
        key = jax.random.key(seed)
        ks = jax.random.split(key, 9)
        x = jax.random.normal(ks[0], (N, IN_DIM), dtype=jnp.float32)
        edge_index = jax.random.randint(ks[1], (2, 100000), 0, N, dtype=jnp.int64)
        s = 1.0 / np.sqrt(IN_DIM)
        gcn_w = jax.random.uniform(ks[2], (IN_DIM, OUT_DIM), jnp.float32, -s, s)
        gcn_b = jnp.zeros((OUT_DIM,), jnp.float32)
        so = 1.0 / np.sqrt(OUT_DIM)
        gat_w = jax.random.uniform(ks[3], (OUT_DIM, HEADS * OUT_DIM), jnp.float32, -so, so)
        att_src = jax.random.uniform(ks[4], (HEADS, OUT_DIM), jnp.float32, -so, so)
        att_dst = jax.random.uniform(ks[5], (HEADS, OUT_DIM), jnp.float32, -so, so)
        gat_b = jnp.zeros((OUT_DIM,), jnp.float32)
        ln_gamma = jnp.ones((OUT_DIM,), jnp.float32)
        ln_beta = jnp.zeros((OUT_DIM,), jnp.float32)
        return dict(x=x, edge_index=edge_index, gcn_w=gcn_w, gcn_b=gcn_b, gat_w=gat_w, att_src=att_src, att_dst=att_dst, gat_b=gat_b, ln_gamma=ln_gamma, ln_beta=ln_beta)
    _L0_gnn_all = _L0_gnn_setup()
    _L0_gnn_in = {k: v for k, v in _L0_gnn_all.items() if k in ('gcn_w', 'gcn_b', 'gat_w', 'att_src', 'att_dst', 'gat_b', 'ln_gamma', 'ln_beta')}
    del _L0_gnn_all

    def _L1_gnn_setup():
        import jax, jax.numpy as jnp
        import numpy as np
        BN_EPS = 1e-05

        def _batchnorm(h, gamma, beta):
            mean = jnp.mean(h, axis=0)
            var = jnp.var(h, axis=0)
            return (h - mean) * jax.lax.rsqrt(var + BN_EPS) * gamma + beta
        N, E, D_IN, D_OUT = (6250, 100000, 128, 128)
        key = jax.random.key(seed)
        ks = jax.random.split(key, 6)
        x = jax.random.normal(ks[0], (N, D_IN), dtype=jnp.float32)
        edge_index = jax.random.randint(ks[1], (2, E), 0, N, dtype=jnp.int32)
        lim1 = 1.0 / np.sqrt(2 * D_IN)
        lim2 = 1.0 / np.sqrt(D_OUT)
        W1 = jax.random.uniform(ks[2], (D_OUT, 2 * D_IN), jnp.float32, -lim1, lim1)
        b1 = jax.random.uniform(ks[3], (D_OUT,), jnp.float32, -lim1, lim1)
        W2 = jax.random.uniform(ks[4], (D_OUT, D_OUT), jnp.float32, -lim2, lim2)
        b2 = jax.random.uniform(ks[5], (D_OUT,), jnp.float32, -lim2, lim2)
        g1 = jnp.ones((D_OUT,), jnp.float32)
        be1 = jnp.zeros((D_OUT,), jnp.float32)
        g2 = jnp.ones((D_OUT,), jnp.float32)
        be2 = jnp.zeros((D_OUT,), jnp.float32)
        return {'x': x, 'edge_index': edge_index, 'W1': W1, 'b1': b1, 'g1': g1, 'be1': be1, 'W2': W2, 'b2': b2, 'g2': g2, 'be2': be2}
    _L1_gnn_all = _L1_gnn_setup()
    _L1_gnn_in = {k: v for k, v in _L1_gnn_all.items() if k in ('W1', 'b1', 'g1', 'be1', 'W2', 'b2', 'g2', 'be2')}
    del _L1_gnn_all
    return {'x': x, 'src': src, 'dst': dst, 'L0_gnn_gcn_w': _L0_gnn_in['gcn_w'], 'L0_gnn_gcn_b': _L0_gnn_in['gcn_b'], 'L0_gnn_gat_w': _L0_gnn_in['gat_w'], 'L0_gnn_att_src': _L0_gnn_in['att_src'], 'L0_gnn_att_dst': _L0_gnn_in['att_dst'], 'L0_gnn_gat_b': _L0_gnn_in['gat_b'], 'L0_gnn_ln_gamma': _L0_gnn_in['ln_gamma'], 'L0_gnn_ln_beta': _L0_gnn_in['ln_beta'], 'L1_gnn_W1': _L1_gnn_in['W1'], 'L1_gnn_b1': _L1_gnn_in['b1'], 'L1_gnn_g1': _L1_gnn_in['g1'], 'L1_gnn_be1': _L1_gnn_in['be1'], 'L1_gnn_W2': _L1_gnn_in['W2'], 'L1_gnn_b2': _L1_gnn_in['b2'], 'L1_gnn_g2': _L1_gnn_in['g2'], 'L1_gnn_be2': _L1_gnn_in['be2']}

def reference(x, src, dst, L0_gnn_gcn_w, L0_gnn_gcn_b, L0_gnn_gat_w, L0_gnn_att_src, L0_gnn_att_dst, L0_gnn_gat_b, L0_gnn_ln_gamma, L0_gnn_ln_beta, L1_gnn_W1, L1_gnn_b1, L1_gnn_g1, L1_gnn_be1, L1_gnn_W2, L1_gnn_b2, L1_gnn_g2, L1_gnn_be2):
    import jax
    import jax.numpy as jnp

    def _L0_gnn_ref(x, edge_index, gcn_w, gcn_b, gat_w, att_src, att_dst, gat_b, ln_gamma, ln_beta):
        import jax, jax.numpy as jnp
        import numpy as np
        N = 6250
        IN_DIM = 128
        OUT_DIM = 128
        HEADS = 2
        EPS = 1e-05
        NEG_SLOPE = 0.2

        def _add_self_loops(edge_index, num_nodes):
            loop = jnp.arange(num_nodes, dtype=edge_index.dtype)
            src = jnp.concatenate([edge_index[0], loop])
            dst = jnp.concatenate([edge_index[1], loop])
            return (src, dst)

        def _layernorm(h, gamma, beta):
            mu = jnp.mean(h, axis=-1, keepdims=True)
            var = jnp.mean(jnp.square(h - mu), axis=-1, keepdims=True)
            return (h - mu) * jax.lax.rsqrt(var + EPS) * gamma + beta

        def _silu(h):
            return h * jax.nn.sigmoid(h)

        def _gcn_conv(x, src, dst, W, b, num_nodes):
            h = x @ W
            deg = jnp.zeros((num_nodes,), h.dtype).at[dst].add(1.0)
            dinv = jnp.where(deg > 0, jax.lax.rsqrt(jnp.maximum(deg, 1.0)), 0.0)
            norm = dinv[src] * dinv[dst]
            msg = h[src] * norm[:, None]
            out = jnp.zeros((num_nodes, h.shape[1]), h.dtype).at[dst].add(msg)
            return out + b

        def _gat_conv(x, src, dst, W, att_src, att_dst, b, num_nodes, heads):
            C = W.shape[1] // heads
            h = (x @ W).reshape(num_nodes, heads, C)
            a_src = jnp.sum(h * att_src, axis=-1)
            a_dst = jnp.sum(h * att_dst, axis=-1)
            e = a_src[src] + a_dst[dst]
            e = jnp.where(e > 0, e, NEG_SLOPE * e)
            m = jax.ops.segment_max(e, dst, num_segments=num_nodes)
            ex = jnp.exp(e - m[dst])
            den = jax.ops.segment_sum(ex, dst, num_segments=num_nodes)
            alpha = ex / den[dst]
            msg = h[src] * alpha[:, :, None]
            out = jnp.zeros((num_nodes, heads, C), h.dtype).at[dst].add(msg)
            return jnp.mean(out, axis=1) + b
        num_nodes = x.shape[0]
        src, dst = _add_self_loops(edge_index, num_nodes)
        h = _gcn_conv(x, src, dst, gcn_w, gcn_b, num_nodes)
        h = _silu(_layernorm(h, ln_gamma, ln_beta))
        h = _gat_conv(h, src, dst, gat_w, att_src, att_dst, gat_b, num_nodes, HEADS)
        h = _silu(_layernorm(h, ln_gamma, ln_beta))
        return h

    def _L1_gnn_ref(x, edge_index, W1, b1, g1, be1, W2, b2, g2, be2):
        import jax, jax.numpy as jnp
        import numpy as np
        BN_EPS = 1e-05

        def _batchnorm(h, gamma, beta):
            mean = jnp.mean(h, axis=0)
            var = jnp.var(h, axis=0)
            return (h - mean) * jax.lax.rsqrt(var + BN_EPS) * gamma + beta
        src, dst = (edge_index[0], edge_index[1])
        edge_features = jnp.concatenate([x[src], x[dst]], axis=1)
        h = edge_features @ W1.T + b1
        h = jax.nn.relu(_batchnorm(h, g1, be1))
        h = h @ W2.T + b2
        edge_updates = jax.nn.relu(_batchnorm(h, g2, be2))
        x_out = jax.ops.segment_sum(edge_updates, dst, num_segments=x.shape[0])
        return x_out
    edge_index = jnp.stack([src, dst])
    h = jnp.maximum(_layernorm(x, axis=-1), 0.0)
    x = x + _L0_gnn_ref(h, edge_index, L0_gnn_gcn_w, L0_gnn_gcn_b, L0_gnn_gat_w, L0_gnn_att_src, L0_gnn_att_dst, L0_gnn_gat_b, L0_gnn_ln_gamma, L0_gnn_ln_beta)
    h = jnp.maximum(_layernorm(x, axis=-1), 0.0)
    x = x + _L1_gnn_ref(h, edge_index, L1_gnn_W1, L1_gnn_b1, L1_gnn_g1, L1_gnn_be1, L1_gnn_W2, L1_gnn_b2, L1_gnn_g2, L1_gnn_be2)
    return x

_drawn_inputs = setup_inputs


def setup_inputs(seed=0):
    import zlib

    import numpy as np

    out = dict(_drawn_inputs(seed))
    spreads = {'L0_gnn_gcn_b': (0.0, 0.1),
     'L0_gnn_gat_b': (0.0, 0.1),
     'L0_gnn_ln_gamma': (1.0, 0.2),
     'L0_gnn_ln_beta': (0.0, 0.1),
     'L1_gnn_g1': (1.0, 0.2),
     'L1_gnn_be1': (0.0, 0.1),
     'L1_gnn_g2': (1.0, 0.2),
     'L1_gnn_be2': (0.0, 0.1)}
    factors = {'L0_gnn_att_src': 40.361, 'L0_gnn_att_dst': 64.0, 'L1_gnn_b1': 64.0, 'L1_gnn_b2': 64.0}
    for name, (base, spread) in spreads.items():
        noise = np.random.default_rng([zlib.crc32(name.encode()), seed]).standard_normal(out[name].shape)
        drawn = base * np.exp(spread * noise) if base else spread * noise
        out[name] = jnp.asarray(drawn.astype(out[name].dtype))
    for name, factor in factors.items():
        out[name] = (out[name] * factor).astype(out[name].dtype)
    return out
```

```python
import concourse.bass as bass
from concourse import mybir
from contextlib import ExitStack

f32 = mybir.dt.float32
bf16 = mybir.dt.bfloat16
i32 = mybir.dt.int32
ALU = mybir.AluOpType
ACT = mybir.ActivationFunctionType
AX = mybir.AxisListType

P = 128
F = 128
HEADS = 2
HALF = 8
BODY = 2 * HALF
GROUP = 4
NEG = -1e30
LN_EPS = 1e-5
BN_EPS = 1e-5
SLOPE = 0.2
ROW_H = F + 2 * HEADS
ROW_R = HEADS * F + 2 * HEADS


def gnn_kernel(nc, x, src, dst, gcn_w, gcn_b, gat_w, att_src, att_dst, gat_b, ln_gamma, ln_beta,
               W1, b1, g1, be1, W2, b2, g2, be2, out):
    N = x.shape[0]
    E = src.shape[0]
    NB = -(-N // P)
    NP = NB * P
    PAD = NP - 1
    NLAST = N - (NB - 1) * P
    T = -(-E // (P * BODY)) * BODY
    NI = T // BODY
    W = T + BODY
    ELAST = E - (P - 1) * T
    assert N < NP and 0 < ELAST < T
    GROUPS = [(b, min(b + GROUP, NB)) for b in range(0, NB, GROUP)]
    PAIRS = [(b, min(b + 2, NB)) for b in range(0, NB, 2)]
    SMALL = 11
    SMALL_LOGS = 8
    FAR = 1 << 20

    gcn_table = nc.dram_tensor("gcn_table", (NP, F), f32).ap()
    gat_table = nc.dram_tensor("gat_table", (NP, ROW_H), f32).ap()
    p_table = nc.dram_tensor("p_table", (NP, F), f32).ap()
    q_table = nc.dram_tensor("q_table", (NP, F), f32).ap()
    q_edge = nc.dram_tensor("q_edge", (P * T, F), f32).ap()
    adst_edge = nc.dram_tensor("adst_edge", (P * T, HEADS), f32).ap()
    gcn_run = nc.dram_tensor("gcn_run", (P * T, F), f32).ap()
    gat_run = nc.dram_tensor("gat_run", (P * T, ROW_R), f32).ap()
    mlp_run = nc.dram_tensor("mlp_run", (P * T, F), f32).ap()
    pre_dram = nc.dram_tensor("pre_dram", (NI, P, BODY * P), f32).ap()
    q_edge_pt = q_edge.rearrange("(p t) f -> p t f", t=T)
    gcn_run_pt = gcn_run.rearrange("(p t) f -> p t f", t=T)
    gat_run_pt = gat_run.rearrange("(p t) f -> p t f", t=T)
    mlp_run_pt = mlp_run.rearrange("(p t) f -> p t f", t=T)

    ctx = ExitStack()
    with ctx:
        def sb(name, shape, dt=f32):
            return ctx.enter_context(nc.sbuf_tensor(name, shape, dt))

        def sem(name):
            return ctx.enter_context(nc.semaphore(name))

        src_i = sb("src_i", [P, W], i32)
        keep = sb("keep", [P, W])
        pen = sb("pen", [P, T])
        valid = pen
        adst_e = sb("adst_e", [P, T * HEADS])
        adst_v = adst_e[:, :].rearrange("p (t h) -> p t h", h=HEADS)
        x_n = sb("x_n", [P, NB * F])
        h_n = sb("h_n", [P, NB * F])
        t_n = sb("t_n", [P, NB * F])
        arena = sb("arena", [P, NB * ROW_R])
        a4 = sb("a4", [P, NB * 2 * HEADS])
        small = sb("small", [P, 30 * NB])
        has, dinv, last_f, start_f = (small[:, k * NB:(k + 1) * NB] for k in range(4))
        mu, rs, deg, cum, tot, scr = (small[:, k * NB:(k + 1) * NB] for k in range(4, 10))
        d_rel = small[:, 10 * NB:11 * NB]
        degsrc = small[:, 11 * NB:12 * NB]
        carry5 = small[:, 12 * NB:17 * NB]
        mx2, ss2 = (small[:, (17 + 2 * k) * NB:(19 + 2 * k) * NB] for k in range(2))
        wr2, wc2, ws2, dn2 = (small[:, (21 + 2 * k) * NB:(23 + 2 * k) * NB] for k in range(4))
        pos_i = sb("pos_i", [P, 2 * NB], i32)
        last_i, start_i = pos_i[:, 0:NB], pos_i[:, NB:2 * NB]
        ident = sb("ident", [P, P])
        tri_incl = sb("tri_incl", [P, P])
        low_strict = sb("low_strict", [P, P])
        ones = sb("ones", [P, P])
        iota_f = sb("iota_f", [P, P])
        iota_i = sb("iota_i", [P, P], i32)
        iota_b = sb("iota_b", [P, P], bf16)
        zero_b = sb("zero_b", [P, P], bf16)
        gcn_w_s = sb("gcn_w_s", [P, F])
        gat_w_s = sb("gat_w_s", [P, HEADS * F])
        w1_s = sb("w1_s", [P, 2 * F])
        w1T = sb("w1T", [P, 2 * F])
        w2_s = sb("w2_s", [P, F])
        w2T = sb("w2T", [P, F])
        w2Ts = sb("w2Ts", [P, F])
        att_row = sb("att_row", [P, 4 * F])
        att_v = sb("att_v", [P, 4])
        gcnb_r = sb("gcnb_r", [P, F])
        gatb_r = sb("gatb_r", [P, F])
        gamma_r = sb("gamma_r", [P, F])
        beta_r = sb("beta_r", [P, F])
        cols = sb("cols", [P, 8])
        bn = sb("bn", [P, 16])
        dfirst, dlast, dprev, dnext = (sb(n, [P, 1]) for n in ("dfirst", "dlast", "dprev", "dnext"))
        edge_i = sb("edge_i", [P, 2], i32)
        dfirst_i = sb("dfirst_i", [P, 1], i32)
        ends = sb("ends", [P, 1])
        held = sb("held", [P, 1])
        real_node = sb("real_node", [P, 1])
        mask_qp = sb("mask_qp", [P, P])
        mask_pq = sb("mask_pq", [P, P])
        tmp_a = sb("tmp_a", [P, P])
        mask_w = sb("mask_w", [P, 4 * P])
        shift_row = sb("shift_row", [P, GROUP * F])
        carry_s = sb("carry_s", [P, HEADS * F + 5])
        sel = sb("sel", [P, 2 * GROUP * P])
        stage_t = sb("stage_t", [P, 2 * 512])
        q_init = sb("q_init", [P, ROW_H])
        stage_idx = sb("stage_idx", [P, 2 * HALF], i32)
        stage_keep = sb("stage_keep", [P, 2 * HALF])
        att_s = sb("att_s", [P, 8 * HALF * HEADS])
        att_rw = sb("att_rw", [P, 4 * HALF * HEADS])
        att_m = sb("att_m", [P, 2 * (HALF + 1) * HEADS])
        run = sb("run", [P, BODY * ROW_R])
        banks = [ctx.enter_context(nc.psum_tensor(f"bank{k}", [P, 512], f32)) for k in range(8)]

        def cut(at, n):
            return arena[:, at:at + n]
        G = cut(0, BODY * ROW_H)
        RAW = BODY * ROW_H
        weighted = cut(RAW, BODY * HEADS * F)
        q_load = cut(RAW, BODY * F)
        q_cur = cut(RAW + BODY * F, BODY * F)
        pre_s = cut(RAW + 2 * BODY * F, BODY * P)
        z_s = cut(RAW, BODY * P)
        u_s = cut(RAW + BODY * F, BODY * P)
        assert RAW + 3 * BODY * F <= NB * ROW_R
        dst_i = cut(0, T + 1).bitcast(i32)
        dst_f = cut(T + 8, T + 1)
        hilo_i = cut(2 * T + 16, T).bitcast(i32)
        lo_b = cut(3 * T + 24, T // 2).bitcast(bf16)
        hi_b = cut(3 * T + 24 + T // 2, T // 2).bitcast(bf16)
        HOT = 4 * T + 32
        hot_lo = cut(HOT, BODY * P // 2).bitcast(bf16)
        hot_hi = cut(HOT + BODY * P // 2, BODY * NB // 2).bitcast(bf16)
        zeros = t_n[:, 0:2 * T]
        assert HOT + BODY * (P + NB) // 2 <= NB * ROW_R and 2 * T <= NB * F
        stats = t_n[:, 0:(T // GROUP) * 6]

        x_v = x_n[:, :].rearrange("p (b f) -> p b f", f=F)
        h_v = h_n[:, :].rearrange("p (b f) -> p b f", f=F)
        t_v = t_n[:, :].rearrange("p (b f) -> p b f", f=F)
        R_v = arena[:, :].rearrange("p (b r) -> p b r", r=ROW_R)
        Rf = arena[:, 0:NB * F]
        Rf_v = Rf.rearrange("p (b f) -> p b f", f=F)
        sq_n = arena[:, NB * F:2 * NB * F]

        def wide(a):
            return a.unsqueeze(2).to_broadcast([P, NB, F])

        def rowwise(a, n):
            return a.unsqueeze(1).to_broadcast([P, n, a.shape[-1]])

        names = """const_made x_clear idx_clear x_loaded idx_loaded ends_loaded weights_loaded
        zero_made filled pool_step vec_step
        hilo_ready mask_row mask_T mask_copied w1_T w2_T wT_copied
        hot_hi_made0 hot_hi_made1 hot_lo_made0 hot_lo_made1 hot_used0 hot_used1 hist_done cum_ready cum_done
        var_ready std_ready
        gcn_ready gcn_table_written
        gcn_idx gcn_gathered0 gcn_gathered1 gcn_acc gcn_written0 gcn_written1
        gcn_rows gcn_carry gcn_carry_copied gcn_sel gcn_picked gcn_merged gcn_lin_ready
        gcn_T gcn_T_copied gcn_lin gcn_lin_used
        sig_ready sig_done
        att_lin_ready att_T att_T_copied att_lin att_ready
        gat_table_written held_done adst_scattered adst_loaded adst_init
        gat_idx gat_gathered0 gat_gathered1 gat_small gat_exp gat_weighted gat_acc
        gat_written0 gat_written1
        att_v_done gat_exp_ready2 gat_exp2
        gat_rows gat_mrow_ready gat_mrow gat_wt_ready gat_wt_T gat_wt_copied gat_carry
        gat_carry_copied gat_sel gat_tail gat_comb_ready gat_comb gat_sel2 gat_picked gat_merged
        gat_T gat_T_copied gat_lin gat_lin_used
        mlp_lin_ready mlp_T mlp_T_copied mlp_lin mlp_lin_used mlp_ready mlp_tables_written
        q_scattered q_init_loaded mlp_idx mlp_gathered0 mlp_gathered1
        q_loaded0 q_loaded1 q_acc pre_made0 pre_made1 pre_copied0 pre_copied1 pre_copied2 pre_copied3
        pre_stats0 pre_stats1 pre_stats2 pre_stats3 pre_written0 pre_written1
        bn_var bn_std bn1_ready bn2_ready
        pre2_loaded0 pre2_loaded1 z_made0 z_made1 z_masked0 z_masked1 h2_made0 h2_made1
        bn2_row bn2_row_done
        w2s_ready  u_made0 u_made1 u_made2 u_made3 mlp_acc mlp_written0
        mlp_written1 mlp_rows mlp_carry mlp_carry_copied mlp_sel mlp_picked mlp_merged
        out_ready out_written""".split()
        s = {n: sem(n) for n in names}

        def step(eng, count, ins, name):
            count[name] = count.get(name, 0) + 1
            ins.then_inc(s[name], 1)
            eng.wait_ge(s[name], count[name])

        block = ctx.enter_context(nc.Block())

        @block.sync
        def _(sp):
            sp.wait_ge(s["x_clear"], 1)
            sp.dma_start(x_v[:, 0:NB - 1, :],
                         x[0:(NB - 1) * P, :].rearrange("(b p) f -> p b f", p=P)).then_inc(s["x_loaded"], 16)
            sp.dma_start(x_v[0:NLAST, NB - 1, :], x[(NB - 1) * P:N, :]).then_inc(s["x_loaded"], 16)
            sp.wait_ge(s["idx_clear"], 3)
            for tile, edge in ((dst_i, dst), (src_i, src)):
                sp.dma_start(tile[0:P - 1, 0:T],
                             edge[0:(P - 1) * T].rearrange("(p t) -> p t", t=T)).then_inc(s["idx_loaded"], 16)
                sp.dma_start(tile[P - 1:P, 0:ELAST],
                             edge[(P - 1) * T:E].rearrange("(p t) -> p t", p=1)).then_inc(s["idx_loaded"], 16)
            sp.wait_ge(s["idx_loaded"], 64)
            sp.dma_start(edge_i[1:P, 0:1], dst_i[0:P - 1, T - 1:T]).then_inc(s["ends_loaded"], 16)
            sp.dma_start(edge_i[0:P - 1, 1:2], dst_i[1:P, 0:1]).then_inc(s["ends_loaded"], 16)
            sp.wait_ge(s["zero_made"], 1)
            sp.dma_start(adst_edge.rearrange("(p t) h -> p (t h)", t=T), zeros).then_inc(s["filled"], 16)
            with sp.Fori(0, NI) as i:
                sp.dma_start(q_edge_pt[:, bass.ds(i * BODY, BODY), :],
                             zeros[:, 0:BODY * F].rearrange("p (t f) -> p t f", f=F)).then_inc(s["filled"], 16)
            sp.wait_ge(s["gcn_ready"], 1)
            sp.dma_start(gcn_table.rearrange("(b p) f -> p b f", p=P), h_v).then_inc(s["gcn_table_written"], 16)
            with sp.Fori(0, NI) as i:
                for k in range(2):
                    sp.wait_ge(s["gcn_acc"], i * BODY + (k + 2) * HALF)
                    sp.dma_start(gcn_run_pt[:, bass.ds(i * BODY + k * HALF, HALF), :],
                                 run[:, k * HALF * F:(k + 1) * HALF * F].rearrange("p (t f) -> p t f", f=F)
                                 ).then_inc(s[f"gcn_written{k}"], 16)
            sp.wait_ge(s["att_ready"], 1)
            t_rows = gat_table.rearrange("(b p) f -> p b f", p=P)
            sp.dma_start(t_rows[:, :, 0:F], h_v).then_inc(s["gat_table_written"], 16)
            sp.dma_start(t_rows[:, :, F:ROW_H],
                         a4[:, :].rearrange("p (b c) -> p b c", c=4)).then_inc(s["gat_table_written"], 16)
            sp.wait_ge(s["adst_scattered"], NB * 16)
            sp.dma_start(adst_e[:, :], adst_edge.rearrange("(p t) h -> p (t h)", t=T)).then_inc(s["adst_loaded"], 16)
            with sp.Fori(0, NI) as i:
                for k in range(2):
                    sp.wait_ge(s["gat_acc"], i * (2 * BODY) + (k + 2) * 2 * HALF)
                    sp.dma_start(gat_run_pt[:, bass.ds(i * BODY + k * HALF, HALF), :],
                                 run[:, k * HALF * ROW_R:(k + 1) * HALF * ROW_R].rearrange("p (t f) -> p t f", f=ROW_R)
                                 ).then_inc(s[f"gat_written{k}"], 16)
            sp.wait_ge(s["mlp_ready"], 1)
            sp.dma_start(p_table.rearrange("(b p) f -> p b f", p=P), t_v).then_inc(s["mlp_tables_written"], 16)
            sp.dma_start(q_table.rearrange("(b p) f -> p b f", p=P), Rf_v).then_inc(s["mlp_tables_written"], 16)
            sp.wait_ge(s["q_scattered"], NB * 16)
            sp.wait_ge(s["mlp_tables_written"], 32)
            with sp.Fori(0, NI) as i:
                for k in range(2):
                    sp.wait_ge(s["q_acc"], i * BODY + k * HALF)
                    sp.dma_start(q_load[:, k * HALF * F:(k + 1) * HALF * F].rearrange("p (t f) -> p t f", f=F),
                                 q_edge_pt[:, bass.ds(i * BODY + k * HALF, HALF), :]).then_inc(s[f"q_loaded{k}"], 16)
            sp.wait_ge(s["bn1_ready"], 1)
            with sp.Fori(0, NI) as i:
                for k in range(2):
                    sp.wait_ge(s[f"z_made{k}"], i)
                    sp.dma_start(G[:, k * HALF * P:(k + 1) * HALF * P],
                                 pre_dram[i, :, k * HALF * P:(k + 1) * HALF * P]).then_inc(s[f"pre2_loaded{k}"], 16)
            sp.wait_ge(s["w2s_ready"], 1)
            with sp.Fori(0, NI) as i:
                for k in range(2):
                    sp.wait_ge(s[f"z_made{k}"], i + NI)
                    sp.dma_start(G[:, k * HALF * P:(k + 1) * HALF * P],
                                 pre_dram[i, :, k * HALF * P:(k + 1) * HALF * P]).then_inc(s[f"pre2_loaded{k}"], 16)
            sp.wait_ge(s["out_ready"], 1)
            sp.dma_start(out[0:(NB - 1) * P, :].rearrange("(b p) f -> p b f", p=P),
                         x_v[:, 0:NB - 1, :]).then_inc(s["out_written"], 16)
            sp.dma_start(out[(NB - 1) * P:N, :], x_v[0:NLAST, NB - 1, :]).then_inc(s["out_written"], 16)
            sp.wait_ge(s["out_written"], 32)

        @block.gpsimd
        def _(pool):
            count = {}

            def st(ins):
                step(pool, count, ins, "pool_step")

            st(nc.gpsimd.iota(iota_i[:, :], pattern=[[1, P]], base=0, channel_multiplier=0))
            st(nc.gpsimd.tensor_copy(iota_f[:, :], iota_i[:, :]))
            st(nc.gpsimd.tensor_copy(iota_b[:, :], iota_i[:, :]))
            st(nc.gpsimd.memset(ones[:, :], 1.0))
            st(nc.gpsimd.memset(zero_b[:, :], 0.0))
            st(nc.gpsimd.memset(ident[:, :], 0.0))
            st(nc.gpsimd.affine_select(out=ident[:, :], in_=ident[:, :], compare_op=ALU.not_equal, fill=1.0,
                                       base=0, pattern=[[-1, P]], channel_multiplier=1))
            st(nc.gpsimd.affine_select(out=tri_incl[:, :], in_=ones[:, :], compare_op=ALU.is_ge, fill=0.0,
                                       base=0, pattern=[[1, P]], channel_multiplier=-1))
            st(nc.gpsimd.affine_select(out=low_strict[:, :], in_=ones[:, :], compare_op=ALU.is_gt, fill=0.0,
                                       base=0, pattern=[[-1, P]], channel_multiplier=1))
            nc.gpsimd.affine_select(out=real_node[:, :], in_=ones[:, 0:1], compare_op=ALU.is_gt, fill=0.0,
                                    base=NLAST, pattern=[[0, 1]], channel_multiplier=-1).then_inc(s["const_made"], 1)

            def hold():
                nc.gpsimd.tensor_tensor(held[:, :], ones[:, 0:1], ones[:, 0:1], ALU.add).then_inc(s["held_done"], 1)

            def gather(tile, table, idx):
                return pool.indirect_dma_start(out=tile, out_offset=None, in_=table,
                                               in_offset=bass.IndirectOffsetOnAxis(ap=idx, axis=0))

            def scatter(table, tile, idx):
                return pool.indirect_dma_start(out=table, out_offset=bass.IndirectOffsetOnAxis(ap=idx, axis=0),
                                               in_=tile, in_offset=None, bounds_check=P * T - 1, oob_is_err=False)

            pool.wait_ge(s["gcn_table_written"], 16)
            with pool.Fori(0, NI) as i:
                for k in range(2):
                    pool.wait_ge(s["held_done"], i * 2 + k)
                    pool.wait_ge(s["gcn_idx"], i * 4 + 2 * k + 2)
                    pool.wait_ge(s["gcn_acc"], i * BODY + k * HALF)
                    hold()
                    for j in range(HALF):
                        n = k * HALF + j
                        gather(G[:, n * F:(n + 1) * F], gcn_table, stage_idx[:, n:n + 1]
                               ).then_inc(s[f"gcn_gathered{k}"], 16)
            for k in range(2):
                pool.wait_ge(s[f"gcn_written{k}"], NI * 16)
            for b in range(NB):
                gather(Rf[:, b * F:(b + 1) * F], gcn_run, last_i[:, b:b + 1]).then_inc(s["gcn_rows"], 16)
            pool.wait_ge(s["gat_table_written"], 32)
            pool.wait_ge(s["filled"], (NI + 1) * 16)
            for b in range(NB):
                scatter(adst_edge, a4[:, 4 * b + HEADS:4 * b + 2 * HEADS], start_i[:, b:b + 1]
                        ).then_inc(s["adst_scattered"], 16)
            gather(q_init[:, :], gat_table, dfirst_i[:, 0:1]).then_inc(s["adst_init"], 16)
            with pool.Fori(0, NI) as i:
                for k in range(2):
                    pool.wait_ge(s["held_done"], i * 2 + k + 2 * NI)
                    pool.wait_ge(s["gat_idx"], i * 2 + k + 1)
                    pool.wait_ge(s["gat_acc"], i * (2 * BODY) + k * 2 * HALF)
                    hold()
                    for j in range(HALF):
                        n = k * HALF + j
                        gather(G[:, n * ROW_H:(n + 1) * ROW_H], gat_table, stage_idx[:, n:n + 1]
                               ).then_inc(s[f"gat_gathered{k}"], 16)
            for k in range(2):
                pool.wait_ge(s[f"gat_written{k}"], NI * 16)
            for b in range(NB):
                gather(arena[:, b * ROW_R:(b + 1) * ROW_R], gat_run, last_i[:, b:b + 1]).then_inc(s["gat_rows"], 16)
            pool.wait_ge(s["mlp_tables_written"], 32)
            for b in range(NB):
                scatter(q_edge, Rf[:, b * F:(b + 1) * F], start_i[:, b:b + 1]).then_inc(s["q_scattered"], 16)
            gather(q_init[:, 0:F], q_table, dfirst_i[:, 0:1]).then_inc(s["q_init_loaded"], 16)
            pool.wait_ge(s["q_scattered"], NB * 16)
            with pool.Fori(0, NI) as i:
                for k in range(2):
                    pool.wait_ge(s["held_done"], i * 2 + k + 4 * NI)
                    pool.wait_ge(s["mlp_idx"], i * 4 + 2 * k + 2)
                    pool.wait_ge(s[f"pre_made{k}"], i * 2)
                    hold()
                    for j in range(HALF):
                        n = k * HALF + j
                        gather(G[:, n * F:(n + 1) * F], p_table, stage_idx[:, n:n + 1]
                               ).then_inc(s[f"mlp_gathered{k}"], 16)
            with pool.Fori(0, NI) as i:
                for k in range(2):
                    pool.wait_ge(s["mlp_acc"], i * BODY + (k + 2) * HALF)
                    pool.dma_start(mlp_run_pt[:, bass.ds(i * BODY + k * HALF, HALF), :],
                                   run[:, k * HALF * F:(k + 1) * HALF * F].rearrange("p (t f) -> p t f", f=F)
                                   ).then_inc(s[f"mlp_written{k}"], 16)
            for k in range(2):
                pool.wait_ge(s[f"mlp_written{k}"], NI * 16)
            for b in range(NB):
                gather(Rf[:, b * F:(b + 1) * F], mlp_run, last_i[:, b:b + 1]).then_inc(s["mlp_rows"], 16)

        @block.tensor
        def _(pe):
            mm = nc.tensor.matmul

            def transpose(o, a):
                return mm(o, a, ident[:, :], start=True, stop=True)

            pe.wait_ge(s["const_made"], 1)
            deg_ps = banks[0][:, 0:NB]
            mm(deg_ps, zero_b[:, :], zero_b[:, 0:NB], start=True, stop=False)
            pe.wait_ge(s["weights_loaded"], 16 * 16)
            for c in range(2):
                last = transpose(banks[2][:, c * F:(c + 1) * F], w1_s[:, c * F:(c + 1) * F])
            last.then_inc(s["w1_T"], 1)
            transpose(banks[3][:, 0:F], w2_s[:, :]).then_inc(s["w2_T"], 1)
            pe.wait_ge(s["mask_row"], 1)
            mm(banks[1][:, 0:P], ones[:, :], tmp_a[:, :], start=True, stop=True).then_inc(s["mask_T"], 1)
            pe.wait_ge(s["mask_row"], 2)
            transpose(banks[1][:, P:2 * P], mask_qp[:, :]).then_inc(s["mask_T"], 1)
            with pe.Fori(0, NI) as i:
                for k in range(2):
                    pe.wait_ge(s[f"hot_lo_made{k}"], i + 1)
                    pe.wait_ge(s[f"hot_hi_made{k}"], i + 1)
                    for j in range(HALF):
                        n = k * HALF + j
                        last = mm(deg_ps, hot_lo[:, n * P:(n + 1) * P], hot_hi[:, n * NB:(n + 1) * NB],
                                  start=False, stop=False)
                    last.then_inc(s[f"hot_used{k}"], 1)
            mm(deg_ps, zero_b[:, :], zero_b[:, 0:NB], start=False, stop=True).then_inc(s["hist_done"], 1)
            pe.wait_ge(s["cum_ready"], 1)
            mm(banks[5][:, 0:NB], tri_incl[:, :], deg, start=True, stop=True)
            mm(banks[5][:, NB:2 * NB], ones[:, :], deg, start=True, stop=True).then_inc(s["cum_done"], 1)

            pe.wait_ge(s["gcn_acc"], HALF + T)
            mm(banks[0][:, 0:F], mask_pq[:, :], run[:, (BODY - 1) * F:BODY * F],
               start=True, stop=True).then_inc(s["gcn_carry"], 1)
            pe.wait_ge(s["gcn_carry_copied"], 1)

            def pick(prefix):
                for g, (b0, b1_) in enumerate(GROUPS):
                    pe.wait_ge(s[prefix + "_sel"], b1_)
                    if g >= 2:
                        pe.wait_ge(s[prefix + "_merged"], GROUPS[g - 2][1])
                    for b in range(b0, b1_):
                        last = mm(banks[2 + g % 2][:, (b - b0) * F:(b - b0 + 1) * F],
                                  sel[:, (b % (2 * GROUP)) * P:(b % (2 * GROUP) + 1) * P],
                                  carry_s[:, 0:F], start=True, stop=True)
                    last.then_inc(s[prefix + "_picked"], 1)
            pick("gcn")

            def linear(prefix, source, w, n_out, groups, parts=1):
                width = GROUP // parts
                for g in range(len(groups) + 1):
                    if g < len(groups):
                        b0, b1_ = groups[g]
                        if g >= 2:
                            pe.wait_ge(s[prefix + "_T_copied"], g - 1)
                        for b in range(b0, b1_):
                            for c in range(parts):
                                at = (b - b0) * parts + c
                                last = transpose(banks[4 + g % 2][:, at * P:(at + 1) * P], source(b, c))
                        last.then_inc(s[prefix + "_T"], 1)
                    if g >= 1:
                        b0, b1_ = groups[g - 1]
                        pe.wait_ge(s[prefix + "_T_copied"], g)
                        if g >= 3:
                            pe.wait_ge(s[prefix + "_lin_used"], g - 2)
                        for b in range(b0, b1_):
                            for c in range(parts):
                                at = (b - b0) * parts + c
                                o = banks[6 + (g - 1) % 2][:, (b - b0) * n_out:(b - b0 + 1) * n_out]
                                last = mm(o, stage_t[:, (g - 1) % 2 * 512 + at * P:(g - 1) % 2 * 512 + (at + 1) * P],
                                          w[:, c * n_out:(c + 1) * n_out], start=(c == 0), stop=(c == parts - 1))
                        last.then_inc(s[prefix + "_lin"], 1)

            pe.wait_ge(s["gcn_lin_ready"], 1)
            linear("gcn", lambda b, c: Rf[:, b * F:(b + 1) * F], gcn_w_s, F, GROUPS)
            pe.wait_ge(s["att_lin_ready"], 1)
            for g in range(len(GROUPS) + 1):
                if g < len(GROUPS):
                    b0, b1_ = GROUPS[g]
                    if g >= 2:
                        pe.wait_ge(s["att_T_copied"], g - 1)
                    for b in range(b0, b1_):
                        last = transpose(banks[4 + g % 2][:, (b - b0) * P:(b - b0 + 1) * P],
                                         h_n[:, b * F:(b + 1) * F])
                    last.then_inc(s["att_T"], 1)
                if g >= 1:
                    b0, b1_ = GROUPS[g - 1]
                    pe.wait_ge(s["att_T_copied"], g)
                    for b in range(b0, b1_):
                        at = (g - 1) % 2 * 512 + (b - b0) * P
                        last = mm(banks[6][:, b * 4:(b + 1) * 4], stage_t[:, at:at + P], att_v[:, :],
                                  start=True, stop=True)
                    last.then_inc(s["att_lin"], 1)

            pe.wait_ge(s["gat_acc"], 2 * (HALF + T))
            tail = (BODY - 1) * ROW_R
            for c in range(HEADS):
                pe.wait_ge(s["gat_mrow_ready"], c + 1)
                mm(banks[0][:, c * P:(c + 1) * P], ones[:, :], tmp_a[:, :],
                   start=True, stop=True).then_inc(s["gat_mrow"], 1)
            for c in range(HEADS):
                pe.wait_ge(s["gat_wt_ready"], c + 1)
                transpose(banks[1][:, c * P:(c + 1) * P], mask_w[:, c * P:(c + 1) * P]).then_inc(s["gat_wt_T"], 1)
            pe.wait_ge(s["gat_wt_copied"], HEADS)
            for c in range(HEADS):
                wt = mask_w[:, (2 + c) * P:(3 + c) * P]
                mm(banks[2][:, c * F:(c + 1) * F], wt, run[:, tail + c * F:tail + (c + 1) * F], start=True, stop=True)
                last = mm(banks[3][:, c:c + 1], wt, run[:, tail + HEADS * F + c:tail + HEADS * F + c + 1],
                          start=True, stop=True)
            last.then_inc(s["gat_carry"], 1)
            pe.wait_ge(s["gat_carry_copied"], 1)
            for g, (b0, b1_) in enumerate(GROUPS):
                pe.wait_ge(s["gat_sel"], b1_)
                for b in range(b0, b1_):
                    last = mm(banks[0][:, b * 5:(b + 1) * 5], sel[:, (b % (2 * GROUP)) * P:(b % (2 * GROUP) + 1) * P],
                              carry_s[:, HEADS * F:HEADS * F + 5], start=True, stop=True)
                last.then_inc(s["gat_tail"], 1)
            for g, (b0, b1_) in enumerate(PAIRS):
                pe.wait_ge(s["gat_sel2"], b1_)
                if g >= 2:
                    pe.wait_ge(s["gat_merged"], PAIRS[g - 2][1])
                for b in range(b0, b1_):
                    last = mm(banks[2 + g % 2][:, (b - b0) * HEADS * F:(b - b0 + 1) * HEADS * F],
                              sel[:, (b % (2 * GROUP)) * P:(b % (2 * GROUP) + 1) * P],
                              carry_s[:, 0:HEADS * F], start=True, stop=True)
                last.then_inc(s["gat_picked"], 1)
            pe.wait_ge(s["gat_merged"], NB)
            linear("gat", lambda b, c: arena[:, b * ROW_R + c * F:b * ROW_R + (c + 1) * F], gat_w_s, F, PAIRS, HEADS)
            pe.wait_ge(s["mlp_lin_ready"], 1)
            linear("mlp", lambda b, c: h_n[:, b * F:(b + 1) * F], w1T, 2 * F, PAIRS)

            with pe.Fori(0, NI) as i:
                for k in range(2):
                    pe.wait_ge(s[f"mlp_gathered{k}"], i * (16 * HALF) + 16 * HALF)
                    for g in range(2):
                        n0 = k * HALF + g * GROUP
                        pe.wait_ge(s["q_acc"], i * BODY + n0 + GROUP + HALF)
                        bank = banks[2 * k + g]
                        pe.wait_ge(s[f"pre_copied{2 * k + g}"], i)
                        for j in range(GROUP):
                            n = n0 + j
                            mm(bank[:, j * P:(j + 1) * P], G[:, n * F:(n + 1) * F], ident[:, :],
                               start=True, stop=False)
                            last = mm(bank[:, j * P:(j + 1) * P], q_cur[:, n * F:(n + 1) * F], ident[:, :],
                                      start=False, stop=True)
                        last.then_inc(s[f"pre_made{k}"], 1)
            with pe.Fori(0, NI) as i:
                for k in range(2):
                    pe.wait_ge(s[f"z_masked{k}"], i + 1)
                    for g in range(2):
                        n0 = k * HALF + g * GROUP
                        pe.wait_ge(s[f"pre_stats{2 * k + g}"], i + NI)
                        mm(banks[2 * k + g][:, :], w2T[:, :], z_s[:, n0 * P:(n0 + GROUP) * P],
                           start=True, stop=True).then_inc(s[f"h2_made{k}"], 1)
            for c in range(2):
                pe.wait_ge(s["bn2_row"], c + 1)
                mm(banks[4 + c][:, 0:F], ones[:, :], tmp_a[:, :], start=True, stop=True).then_inc(s["bn2_row_done"], 1)
            pe.wait_ge(s["w2s_ready"], 1)
            with pe.Fori(0, NI) as i:
                for k in range(2):
                    pe.wait_ge(s[f"z_made{k}"], i + NI + 1)
                    for g in range(2):
                        n0 = k * HALF + g * GROUP
                        pe.wait_ge(s[f"u_made{2 * k + g}"], i)
                        mm(banks[2 * k + g][:, :], ones[0:1, :], shift_row[0:1, :], start=True, stop=False)
                        for j in range(GROUP):
                            n = n0 + j
                            o = banks[2 * k + g][:, j * F:(j + 1) * F]
                            last = mm(o, z_s[:, n * P:(n + 1) * P], w2Ts[:, :], start=False, stop=(j == GROUP - 1))
                        last.then_inc(s[f"h2_made{k}"], 1)
            pe.wait_ge(s["mlp_acc"], HALF + T)
            mm(banks[0][:, 0:F], mask_pq[:, :], run[:, (BODY - 1) * F:BODY * F],
               start=True, stop=True).then_inc(s["mlp_carry"], 1)
            pe.wait_ge(s["mlp_carry_copied"], 1)
            pick("mlp")

        @block.vector
        def _(dve):
            count = {}
            v = nc.vector

            def st(ins, name="vec_step"):
                step(dve, count, ins, name)

            tt, ts, stt = v.tensor_tensor, v.tensor_scalar, v.scalar_tensor_tensor
            x_n3, h_n3, t_n3, sq3 = (a.rearrange("p (b f) -> p b f", f=F) for a in (x_n[:, :], h_n[:, :], t_n[:, :], sq_n))

            def layernorm(src_, dst_, tmp):
                st(v.tensor_reduce(mu, src_, AX.X, ALU.add))
                st(ts(mu, mu, 1.0 / F, None, ALU.mult))
                st(tt(tmp, src_, wide(mu), ALU.subtract))
                st(tt(sq3, tmp, tmp, ALU.mult))
                st(v.tensor_reduce(rs, sq3, AX.X, ALU.add))
                st(ts(rs, rs, 1.0 / F, LN_EPS, ALU.mult, ALU.add), "var_ready")
                dve.wait_ge(s["std_ready"], count["var_ready"])
                st(v.reciprocal(rs, rs))
                st(tt(dst_, tmp, wide(rs), ALU.mult))

            def gamma_beta_silu(a3, a2):
                st(tt(a3, a3, rowwise(gamma_r[:, :], NB), ALU.mult))
                st(tt(a3, a3, rowwise(beta_r[:, :], NB), ALU.add), "sig_ready")
                dve.wait_ge(s["sig_done"], count["sig_ready"])
                st(tt(a2, a2, sq_n, ALU.mult))

            st(v.memset(x_n[:, (NB - 1) * F:NB * F], 0.0), "x_clear")
            st(v.memset(dst_i, PAD), "idx_clear")
            st(v.memset(src_i[:, :], PAD), "idx_clear")
            st(v.memset(edge_i[:, :], -1), "idx_clear")
            st(v.memset(zeros, 0.0), "zero_made")
            dve.wait_ge(s["idx_loaded"], 64)
            dve.wait_ge(s["ends_loaded"], 32)
            st(v.tensor_copy(dst_f[:, 1:T + 1], dst_i[:, 0:T]))
            st(v.tensor_copy(dst_f[:, 0:1], edge_i[:, 0:1]))
            st(v.tensor_copy(dnext[:, :], edge_i[:, 1:2]))
            st(v.tensor_copy(dfirst[:, :], dst_f[:, 1:2]))
            st(v.tensor_copy(dfirst_i[:, :], dst_i[:, 0:1]))
            st(ts(hilo_i, dst_i[:, 0:T], P - 1, None, ALU.bitwise_and))
            st(v.tensor_copy(lo_b, hilo_i))
            st(ts(hilo_i, dst_i[:, 0:T], P.bit_length() - 1, None, ALU.arith_shift_right))
            st(v.tensor_copy(hi_b, hilo_i), "hilo_ready")
            st(v.memset(keep[:, T:W], 0.0))
            st(tt(keep[:, 0:T], dst_f[:, 1:T + 1], dst_f[:, 0:T], ALU.is_equal))
            st(ts(pen[:, :], keep[:, 0:T], -NEG, NEG, ALU.mult, ALU.add))
            st(tt(ends[:, :], dfirst[:, :], dnext[:, :], ALU.not_equal))
            dve.wait_ge(s["const_made"], 1)
            st(ts(d_rel, iota_f[:, 0:NB], float(-P), dfirst[:, 0:1], ALU.mult, ALU.add))
            st(ts(tmp_a[:, :], ident[:, :], dst_f[:, T:T + 1], None, ALU.mult), "mask_row")
            dve.wait_ge(s["mask_T"], 1)
            st(stt(mask_qp[:, :], banks[1][:, 0:P], dfirst[:, 0:1], low_strict[:, :], ALU.is_equal, ALU.mult),
               "mask_row")
            with dve.Fori(0, NI) as i:
                for k in range(2):
                    dve.wait_ge(s[f"hot_used{k}"], i)
                    tt(hot_hi[:, k * HALF * NB:(k + 1) * HALF * NB].rearrange("p (t m) -> p t m", m=NB),
                       hi_b[:, bass.ds(i * BODY + k * HALF, HALF)].unsqueeze(2).to_broadcast([P, HALF, NB]),
                       rowwise(iota_b[:, 0:NB], HALF), ALU.is_equal).then_inc(s[f"hot_hi_made{k}"], 1)
                    tt(hot_lo[:, k * HALF * P:(k + 1) * HALF * P].rearrange("p (t m) -> p t m", m=P),
                       lo_b[:, bass.ds(i * BODY + k * HALF, HALF)].unsqueeze(2).to_broadcast([P, HALF, P]),
                       rowwise(iota_b[:, :], HALF), ALU.is_equal).then_inc(s[f"hot_lo_made{k}"], 1)
            dve.wait_ge(s["hist_done"], 1)
            st(v.tensor_copy(deg, banks[0][:, 0:NB]), "cum_ready")
            st(ts(has, deg, 0.5, None, ALU.is_gt))
            st(ts(rs, deg, 1.0, None, ALU.add), "var_ready")
            dve.wait_ge(s["std_ready"], count["var_ready"])
            st(v.reciprocal(dinv, rs))
            dve.wait_ge(s["cum_done"], 1)
            st(v.tensor_copy(cum, banks[5][:, 0:NB]))
            st(v.tensor_copy(tot, banks[5][:, NB:2 * NB]))
            st(v.tensor_tensor_scan(scr, ones[:, 0:NB], tot, 0.0, ALU.mult, ALU.add))
            st(tt(scr, scr, tot, ALU.subtract))
            st(tt(cum, cum, scr, ALU.add))
            st(ts(last_f, cum, -1.0, 0.0, ALU.add, ALU.max))
            st(v.tensor_copy(last_i, last_f))
            st(tt(start_f, cum, deg, ALU.subtract))
            st(ts(scr, has, float(-FAR), float(FAR), ALU.mult, ALU.add))
            st(tt(start_f, start_f, scr, ALU.add))
            st(v.tensor_copy(start_i, start_f))

            dve.wait_ge(s["x_loaded"], 32)
            dve.wait_ge(s["filled"], (NI + 1) * 16)
            layernorm(x_n3, h_n3, t_n3)
            st(ts(h_n[:, :], h_n[:, :], 0.0, None, ALU.max))
            st(tt(h_n3, h_n3, wide(dinv), ALU.mult), "gcn_ready")

            def stage(c, at, prefix, with_keep):
                v.tensor_copy(stage_idx[:, c * HALF:(c + 1) * HALF],
                              src_i[:, at]).then_inc(s[prefix + "_idx"], 1)
                if with_keep:
                    v.tensor_copy(stage_keep[:, c * HALF:(c + 1) * HALF],
                                  keep[:, at]).then_inc(s[prefix + "_idx"], 1)

            def prime(acc, names_=HALF):
                for c in range(names_):
                    st(v.memset(run[:, (BODY - 1) * F + c * (F // names_):(BODY - 1) * F + (c + 1) * (F // names_)], 0.0), acc)

            def accumulate(prefix, rows, ready):
                with dve.Fori(0, NI) as i:
                    for k in range(2):
                        if prefix == "gcn":
                            dve.wait_ge(s["gcn_idx"], i * 4 + 2 * k + 2)
                        ready(i, k, 0)
                        dve.wait_ge(s[f"{prefix}_written{k}"], i * 16)
                        for j in range(HALF):
                            n = k * HALF + j
                            if j == GROUP:
                                ready(i, k, 1)
                            before = (n - 1) % BODY
                            kp = (stage_keep[:, n:n + 1] if prefix == "gcn" else keep[:, bass.ds(i * BODY + n, 1)])
                            stt(run[:, n * F:(n + 1) * F], run[:, before * F:(before + 1) * F],
                                kp, rows[:, n * F:(n + 1) * F],
                                ALU.mult, ALU.add).then_inc(s[prefix + "_acc"], 1)
                            dve.wait_ge(s[prefix + "_acc"], i * BODY + HALF + n + 1)
                        if prefix == "gcn":
                            stage(k, bass.ds(i * BODY + BODY + k * HALF, HALF), "gcn", True)

            prime("gcn_acc")
            for k in range(2):
                stage(k, slice(k * HALF, (k + 1) * HALF), "gcn", True)

            def gcn_rows_ready(i, k, g):
                if g == 0:
                    dve.wait_ge(s[f"gcn_gathered{k}"], i * (16 * HALF) + 16 * HALF)
            accumulate("gcn", G, gcn_rows_ready)

            def pick(prefix):
                def select(b):
                    st(ts(sel[:, (b % (2 * GROUP)) * P:(b % (2 * GROUP) + 1) * P], iota_f[:, :], d_rel[:, b:b + 1],
                          ends[:, 0:1], ALU.is_equal, ALU.mult), prefix + "_sel")
                for b in range(*GROUPS[0]):
                    select(b)
                for g, (b0, b1_) in enumerate(GROUPS):
                    if g + 1 < len(GROUPS):
                        if g >= 1:
                            dve.wait_ge(s[prefix + "_picked"], g)
                        for b in range(*GROUPS[g + 1]):
                            select(b)
                    dve.wait_ge(s[prefix + "_picked"], g + 1)
                    for b in range(b0, b1_):
                        st(stt(Rf[:, b * F:(b + 1) * F], Rf[:, b * F:(b + 1) * F], has[:, b:b + 1],
                               banks[2 + g % 2][:, (b - b0) * F:(b - b0 + 1) * F], ALU.mult, ALU.add),
                           prefix + "_merged")

            dve.wait_ge(s["gcn_carry"], 1)
            st(v.tensor_copy(carry_s[:, 0:F], banks[0][:, 0:F]), "gcn_carry_copied")
            dve.wait_ge(s["gcn_rows"], NB * 16)
            pick("gcn")
            st(tt(Rf, Rf, h_n[:, :], ALU.add))
            st(tt(Rf_v, Rf_v, wide(dinv), ALU.mult), "gcn_lin_ready")
            for g, (b0, b1_) in enumerate(GROUPS):
                dve.wait_ge(s["gcn_lin"], g + 1)
                st(tt(h_v[:, b0:b1_, :], banks[6 + g % 2][:, 0:(b1_ - b0) * F].rearrange("p (b f) -> p b f", f=F),
                      rowwise(gcnb_r[:, :], b1_ - b0), ALU.add), "gcn_lin_used")
            layernorm(h_n3, h_n3, t_n3)
            gamma_beta_silu(h_n3, h_n[:, :])

            for c in range(2):
                for h in range(HEADS):
                    st(tt(tmp_a[:, :], gat_w_s[:, h * F:(h + 1) * F],
                          att_row[:, (c * HEADS + h) * F:(c * HEADS + h + 1) * F], ALU.mult))
                    st(v.tensor_reduce(att_v[:, c * HEADS + h:c * HEADS + h + 1], tmp_a[:, :], AX.X, ALU.add),
                       "att_v_done")
            st(v.memset(scr, 0.0), "att_lin_ready")
            dve.wait_ge(s["att_lin"], len(GROUPS))
            st(v.tensor_copy(a4[:, :], banks[6][:, 0:4 * NB]), "att_ready")
            dve.wait_ge(s["adst_loaded"], 16)
            dve.wait_ge(s["adst_init"], 16)
            for h in range(HEADS):
                st(v.tensor_tensor_scan(adst_v[:, :, h], keep[:, 0:T], adst_v[:, :, h],
                                        q_init[:, F + HEADS + h:F + HEADS + h + 1], ALU.mult, ALU.add))
            prime("gat_acc", 2 * HALF)
            run_v = run[:, :].rearrange("p (t r) -> p t r", r=ROW_R)
            st(v.memset(run[:, (BODY - 1) * ROW_R:BODY * ROW_R], 0.0))
            m_half = [att_m[:, k * (HALF + 1) * HEADS:(k + 1) * (HALF + 1) * HEADS].rearrange("p (t h) -> p t h", h=HEADS)
                      for k in range(2)]
            s_half = [att_s[:, k * HALF * HEADS:(k + 1) * HALF * HEADS].rearrange("p (t h) -> p t h", h=HEADS)
                      for k in range(2)]
            r_half, w_half = ([att_rw[:, (2 * k + c) * HALF * HEADS:(2 * k + c + 1) * HALF * HEADS]
                               .rearrange("p (t h) -> p t h", h=HEADS) for k in range(2)] for c in range(2))
            st(v.memset(m_half[0][:, 0, :], NEG))
            for k in range(2):
                stage(k, slice(k * HALF, (k + 1) * HALF), "gat", False)
            with dve.Fori(0, NI) as i:
                for k in range(2):
                    at = bass.ds(i * BODY + k * HALF, HALF)
                    steps = [0]

                    def small_step(ins):
                        steps[0] += 1
                        ins.then_inc(s["gat_small"], 1)
                        dve.wait_ge(s["gat_small"], i * (2 * SMALL) + k * SMALL + steps[0])

                    S, M, R_, W_ = s_half[k], m_half[k], r_half[k], w_half[k]
                    g_v = G[:, k * HALF * ROW_H:(k + 1) * HALF * ROW_H].rearrange("p (t r) -> p t r", r=ROW_H)
                    dve.wait_ge(s[f"gat_gathered{k}"], i * (16 * HALF) + 16 * HALF)
                    small_step(tt(S, g_v[:, :, F:F + HEADS], adst_v[:, at, :], ALU.add))
                    small_step(stt(S, S, SLOPE, S, ALU.mult, ALU.max))
                    for h in range(HEADS):
                        small_step(v.tensor_tensor_scan(M[:, 1:HALF + 1, h], pen[:, at], S[:, :, h], M[:, 0:1, h],
                                                        ALU.add, ALU.max))
                    small_step(v.tensor_copy(m_half[1 - k][:, 0, :], M[:, HALF, :]))
                    small_step(tt(R_, M[:, 0:HALF, :], M[:, 1:HALF + 1, :], ALU.subtract))
                    small_step(tt(R_, R_, pen[:, at].unsqueeze(2).to_broadcast([P, HALF, HEADS]), ALU.add))
                    small_step(tt(W_, S, M[:, 1:HALF + 1, :], ALU.subtract))
                    dve.wait_ge(s[f"gat_written{k}"], i * 16)
                    small_step(v.tensor_copy(run_v[:, k * HALF:(k + 1) * HALF, HEADS * F + HEADS:ROW_R],
                                             M[:, 1:HALF + 1, :]))
                    dve.wait_ge(s["gat_exp"], i * 2 + k + 1)
                    before = (k * HALF - 1) % BODY
                    for h in range(HEADS):
                        small_step(v.tensor_tensor_scan(run_v[:, k * HALF:(k + 1) * HALF, HEADS * F + h],
                                                        R_[:, :, h], W_[:, :, h],
                                                        run_v[:, before:before + 1, HEADS * F + h],
                                                        ALU.mult, ALU.add))
                    assert steps[0] == SMALL
                    for j in range(HALF):
                        n = k * HALF + j
                        before = (n - 1) % BODY
                        dve.wait_ge(s["gat_weighted"], i * (2 * BODY) + 2 * n + 2)
                        dve.wait_ge(s["gat_acc"], i * (2 * BODY) + 2 * HALF + 2 * n)
                        for h in range(HEADS):
                            stt(run_v[:, n, h * F:(h + 1) * F], run_v[:, before, h * F:(h + 1) * F],
                                R_[:, j, h:h + 1], weighted[:, (n * HEADS + h) * F:(n * HEADS + h + 1) * F],
                                ALU.mult, ALU.add).then_inc(s["gat_acc"], 1)
                    dve.wait_ge(s["gat_acc"], i * (2 * BODY) + (k + 2) * 2 * HALF)
                    stage(k, bass.ds(i * BODY + BODY + k * HALF, HALF), "gat", False)

            tail = (BODY - 1) * ROW_R
            mm_w = [mask_w[:, h * P:(h + 1) * P] for h in range(HEADS)]
            for h in range(HEADS):
                at = tail + HEADS * F + HEADS + h
                if h:
                    dve.wait_ge(s["gat_mrow"], h)
                st(ts(tmp_a[:, :], ident[:, :], run[:, at:at + 1], None, ALU.mult), "gat_mrow_ready")
            dve.wait_ge(s["gat_mrow"], HEADS)
            st(ts(sel[:, 0:P], mask_qp[:, :], -NEG, NEG, ALU.mult, ALU.add))
            for h in range(HEADS):
                mc = carry_s[:, HEADS * F + HEADS + h:HEADS * F + HEADS + h + 1]
                st(tt(mm_w[h], banks[0][:, h * P:(h + 1) * P], sel[:, 0:P], ALU.add))
                st(v.tensor_reduce(mc, mm_w[h], AX.X, ALU.max))
                st(ts(mm_w[h], mm_w[h], mc, None, ALU.subtract), "gat_exp_ready2")
            for h in range(HEADS):
                dve.wait_ge(s["gat_exp2"], 1)
                st(tt(mm_w[h], mm_w[h], mask_qp[:, :], ALU.mult), "gat_wt_ready")
            dve.wait_ge(s["gat_wt_T"], HEADS)
            for h in range(HEADS):
                st(v.tensor_copy(mask_w[:, (2 + h) * P:(3 + h) * P], banks[1][:, h * P:(h + 1) * P]), "gat_wt_copied")
            dve.wait_ge(s["gat_carry"], 1)
            st(v.tensor_copy(carry_s[:, 0:HEADS * F], banks[2][:, 0:HEADS * F]))
            st(v.tensor_copy(carry_s[:, HEADS * F:HEADS * F + HEADS], banks[3][:, 0:HEADS]))
            st(v.memset(carry_s[:, HEADS * F + 4:HEADS * F + 5], 1.0), "gat_carry_copied")

            def select(b, name):
                st(ts(sel[:, (b % (2 * GROUP)) * P:(b % (2 * GROUP) + 1) * P], iota_f[:, :], d_rel[:, b:b + 1],
                      ends[:, 0:1], ALU.is_equal, ALU.mult), name)
            for g, (b0, b1_) in enumerate(GROUPS):
                if g >= 2:
                    dve.wait_ge(s["gat_tail"], g - 1)
                for b in range(b0, b1_):
                    select(b, "gat_sel")
            dve.wait_ge(s["gat_tail"], len(GROUPS))
            st(v.tensor_copy(carry5, banks[0][:, 0:5 * NB]))
            c5 = carry5.rearrange("p (b c) -> p b c", c=5)
            a4v = a4[:, :].rearrange("p (b c) -> p b c", c=4)

            def two(a):
                return a.rearrange("p (b h) -> p b h", h=HEADS)

            def heads_wide(a):
                return a.unsqueeze(2).to_broadcast([P, NB, HEADS])

            wr, wc, ws, dn, mx, ss = (two(a) for a in (wr2, wc2, ws2, dn2, mx2, ss2))
            dve.wait_ge(s["gat_rows"], NB * 16)
            st(tt(ss, a4v[:, :, 0:2], a4v[:, :, 2:4], ALU.add))
            st(stt(ss2, ss2, SLOPE, ss2, ALU.mult, ALU.max))
            st(ts(scr, has, -NEG, NEG, ALU.mult, ALU.add))
            st(tt(wr, R_v[:, :, HEADS * F + HEADS:ROW_R], heads_wide(scr), ALU.add))
            st(ts(scr, c5[:, :, 4], -NEG, NEG, ALU.mult, ALU.add))
            st(tt(wc, c5[:, :, 2:4], heads_wide(scr), ALU.add))
            st(tt(mx2, wr2, wc2, ALU.max))
            st(tt(mx2, mx2, ss2, ALU.max))
            st(tt(wr2, wr2, mx2, ALU.subtract))
            st(tt(wc2, wc2, mx2, ALU.subtract))
            st(tt(ws2, ss2, mx2, ALU.subtract), "gat_comb_ready")
            dve.wait_ge(s["gat_comb"], 1)
            st(tt(dn, wr, R_v[:, :, HEADS * F:HEADS * F + HEADS], ALU.mult))
            st(tt(mx, wc, c5[:, :, 0:2], ALU.mult))
            st(tt(dn2, dn2, mx2, ALU.add))
            st(tt(dn2, dn2, ws2, ALU.add))
            st(v.reciprocal(dn2, dn2))
            st(ts(dn2, dn2, 1.0 / HEADS, None, ALU.mult))
            for w_ in (wr2, wc2, ws2):
                st(tt(w_, w_, dn2, ALU.mult))
            for b in range(*PAIRS[0]):
                select(b, "gat_sel2")
            for g, (b0, b1_) in enumerate(PAIRS):
                if g + 1 < len(PAIRS):
                    for b in range(*PAIRS[g + 1]):
                        select(b, "gat_sel2")
                dve.wait_ge(s["gat_picked"], g + 1)
                for b in range(b0, b1_):
                    for h in range(HEADS):
                        row = arena[:, b * ROW_R + h * F:b * ROW_R + (h + 1) * F]
                        col = b * HEADS + h
                        st(ts(row, row, wr2[:, col:col + 1], None, ALU.mult))
                        st(stt(row, h_n[:, b * F:(b + 1) * F], ws2[:, col:col + 1], row, ALU.mult, ALU.add))
                        at = ((b - b0) * HEADS + h) * F
                        st(stt(row, banks[2 + g % 2][:, at:at + F], wc2[:, col:col + 1], row, ALU.mult, ALU.add),
                           "gat_merged" if h == HEADS - 1 else "vec_step")
            for g, (b0, b1_) in enumerate(PAIRS):
                dve.wait_ge(s["gat_lin"], g + 1)
                st(tt(t_v[:, b0:b1_, :], banks[6 + g % 2][:, 0:(b1_ - b0) * F].rearrange("p (b f) -> p b f", f=F),
                      rowwise(gatb_r[:, :], b1_ - b0), ALU.add), "gat_lin_used")
            layernorm(t_n3, t_n3, h_n3)
            gamma_beta_silu(t_n3, t_n[:, :])
            st(tt(x_n[:, :], x_n[:, :], t_n[:, :], ALU.add))

            layernorm(x_n3, h_n3, t_n3)
            st(ts(h_n[:, :], h_n[:, :], 0.0, None, ALU.max), "mlp_lin_ready")
            for g, (b0, b1_) in enumerate(PAIRS):
                dve.wait_ge(s["mlp_lin"], g + 1)
                pq = banks[6 + g % 2][:, 0:(b1_ - b0) * 2 * F].rearrange("p (b c f) -> p b c f", c=2, f=F)
                st(v.tensor_copy(t_v[:, b0:b1_, :], pq[:, :, 0, :]))
                st(v.tensor_copy(Rf_v[:, b0:b1_, :], pq[:, :, 1, :]), "mlp_lin_used")
            st(ts(t_n[:, (NB - 1) * F:], t_n[:, (NB - 1) * F:], real_node[:, 0:1], None, ALU.mult))
            st(ts(Rf[:, (NB - 1) * F:], Rf[:, (NB - 1) * F:], real_node[:, 0:1], None, ALU.mult), "mlp_ready")
            dve.wait_ge(s["q_scattered"], NB * 16)
            dve.wait_ge(s["mlp_tables_written"], 32)
            st(v.memset(valid[:, :], 1.0))
            st(v.memset(valid[:, ELAST:T], 0.0))
            for c in range(HALF):
                at = slice(c * (F // HALF), (c + 1) * (F // HALF))
                if c == 0:
                    dve.wait_ge(s["q_init_loaded"], 16)
                st(v.tensor_copy(q_cur[:, (BODY - 1) * F + at.start:(BODY - 1) * F + at.stop], q_init[:, at]), "q_acc")
            for k in range(2):
                stage(k, slice(k * HALF, (k + 1) * HALF), "mlp", True)
            with dve.Fori(0, NI) as i:
                for k in range(2):
                    dve.wait_ge(s["mlp_idx"], i * 4 + 2 * k + 2)
                    dve.wait_ge(s[f"q_loaded{k}"], i * 16 + 16)
                    dve.wait_ge(s[f"pre_made{k}"], i * 2)
                    for j in range(HALF):
                        n = k * HALF + j
                        before = (n - 1) % BODY
                        stt(q_cur[:, n * F:(n + 1) * F], q_cur[:, before * F:(before + 1) * F],
                            stage_keep[:, n:n + 1], q_load[:, n * F:(n + 1) * F],
                            ALU.mult, ALU.add).then_inc(s["q_acc"], 1)
                        dve.wait_ge(s["q_acc"], i * BODY + HALF + n + 1)
                    for g in range(2):
                        dve.wait_ge(s[f"pre_copied{2 * k + g}"], i + 1)
                        n0 = k * HALF + g * GROUP
                        v.bn_stats(stats[:, bass.ds(i * 24 + (2 * k + g) * 6, 6)],
                                   pre_s[:, n0 * P:(n0 + GROUP) * P]).then_inc(s[f"pre_stats{2 * k + g}"], 1)
                    stage(k, bass.ds(i * BODY + BODY + k * HALF, HALF), "mlp", True)

            sv = stats.rearrange("p (g a c) -> p (g a) c", a=2, c=3)
            NS = 2 * (T // GROUP)
            s_cm = h_n[:, 0:NS]
            s_q = h_n[:, NS:2 * NS]

            def batch_norm(c0, o0, name):
                gcol, becol, bcol = (cols[:, c0 + c:c0 + c + 1] for c in range(3))
                mean, var, scale, shift, tmp = (bn[:, c:c + 1] for c in range(o0, o0 + 5))
                st(tt(s_cm, sv[:, :, 0], sv[:, :, 1], ALU.mult))
                st(v.tensor_reduce(mean, s_cm, AX.X, ALU.add))
                st(tt(s_q, s_cm, sv[:, :, 1], ALU.mult))
                st(tt(s_q, s_q, sv[:, :, 2], ALU.add))
                st(v.tensor_reduce(var, s_q, AX.X, ALU.add))
                st(ts(mean, mean, 1.0 / E, None, ALU.mult))
                st(tt(tmp, mean, mean, ALU.mult))
                st(ts(var, var, 1.0 / E, tmp, ALU.mult, ALU.subtract))
                st(ts(var, var, 0.0, BN_EPS, ALU.max, ALU.add), "bn_var")
                dve.wait_ge(s["bn_std"], count["bn_var"])
                st(v.reciprocal(var, var))
                st(tt(scale, var, gcol, ALU.mult))
                st(tt(mean, mean, bcol, ALU.add))
                st(tt(tmp, bcol, mean, ALU.subtract))
                st(ts(shift, tmp, scale, becol, ALU.mult, ALU.add), name)

            for b_ in range(4):
                dve.wait_ge(s[f"pre_stats{b_}"], NI)
            batch_norm(0, 0, "bn1_ready")
            with dve.Fori(0, NI) as i:
                for k in range(2):
                    dve.wait_ge(s[f"z_made{k}"], i + 1)
                    zc = z_s[:, k * HALF * P:(k + 1) * HALF * P].rearrange("p (t e) -> p t e", e=P)[:, :, P - 1]
                    tt(zc, zc, valid[:, bass.ds(i * BODY + k * HALF, HALF)], ALU.mult).then_inc(s[f"z_masked{k}"], 1)
                    for g in range(2):
                        dve.wait_ge(s[f"h2_made{k}"], i * 2 + g + 1)
                        v.bn_stats(stats[:, bass.ds(i * 24 + (2 * k + g) * 6, 6)],
                                   banks[2 * k + g][:, :]).then_inc(s[f"pre_stats{2 * k + g}"], 1)
            for b_ in range(4):
                dve.wait_ge(s[f"pre_stats{b_}"], 2 * NI)
            batch_norm(3, 8, "bn2_ready")
            st(ts(tmp_a[:, :], ident[:, :], bn[:, 10:11], None, ALU.mult), "bn2_row")
            dve.wait_ge(s["bn2_row_done"], 1)
            st(tt(w2Ts[:, :], w2T[:, :], banks[4][:, 0:F], ALU.mult))
            st(ts(tmp_a[:, :], ident[:, :], bn[:, 11:12], None, ALU.mult), "bn2_row")
            dve.wait_ge(s["bn2_row_done"], 2)
            st(v.tensor_copy(shift_row[:, :].rearrange("p (g f) -> p g f", f=F),
                             rowwise(banks[5][:, 0:F], GROUP)), "w2s_ready")
            prime("mlp_acc")

            def u_ready(i, k, g):
                dve.wait_ge(s[f"u_made{2 * k + g}"], i + 1)
            accumulate("mlp", u_s, u_ready)
            dve.wait_ge(s["mlp_carry"], 1)
            st(v.tensor_copy(carry_s[:, 0:F], banks[0][:, 0:F]), "mlp_carry_copied")
            dve.wait_ge(s["mlp_rows"], NB * 16)
            pick("mlp")
            st(tt(x_n[:, :], x_n[:, :], Rf, ALU.add), "out_ready")

        @block.scalar
        def _(act):
            a = nc.scalar.activation
            count = {}

            def std(ap):
                count["std"] = count.get("std", 0) + 1
                act.wait_ge(s["var_ready"], count["std"])
                a(ap, ap, ACT.Sqrt).then_inc(s["std_ready"], 1)

            def sigmoid(src_):
                count["sig"] = count.get("sig", 0) + 1
                act.wait_ge(s["sig_ready"], count["sig"])
                a(sq_n, src_, ACT.Sigmoid).then_inc(s["sig_done"], 1)

            def wl(o, i_):
                act.dma_start(o, i_).then_inc(s["weights_loaded"], 16)
            wl(gcn_w_s[:, :], gcn_w)
            wl(gat_w_s[:, :], gat_w)
            wl(w1_s[:, :], W1)
            wl(w2_s[:, :], W2)
            wl(att_row[:, 0:2 * F], att_src.rearrange("h f -> (h f)").partition_broadcast(P))
            wl(att_row[:, 2 * F:4 * F], att_dst.rearrange("h f -> (h f)").partition_broadcast(P))
            for o, i_ in ((gcnb_r, gcn_b), (gatb_r, gat_b), (gamma_r, ln_gamma), (beta_r, ln_beta)):
                wl(o[:, :], i_.partition_broadcast(P))
            for c, i_ in enumerate((g1, be1, b1, g2, be2, b2)):
                wl(cols[:, c:c + 1], i_.rearrange("(p o) -> p o", o=1))

            act.wait_ge(s["w1_T"], 1)
            a(w1T[:, :], banks[2][:, 0:2 * F], ACT.Copy).then_inc(s["wT_copied"], 1)
            act.wait_ge(s["w2_T"], 1)
            a(w2T[:, :], banks[3][:, 0:F], ACT.Copy).then_inc(s["wT_copied"], 1)
            act.wait_ge(s["mask_T"], 2)
            a(mask_pq[:, :], banks[1][:, P:2 * P], ACT.Copy).then_inc(s["mask_copied"], 1)
            std(rs)
            std(rs)

            def copies(prefix, groups, parts=1):
                for g, (b0, b1_) in enumerate(groups):
                    act.wait_ge(s[prefix + "_T"], g + 1)
                    if g >= 2:
                        act.wait_ge(s[prefix + "_lin"], g - 1)
                    n = (b1_ - b0) * parts * P
                    a(stage_t[:, g % 2 * 512:g % 2 * 512 + n], banks[4 + g % 2][:, 0:n],
                      ACT.Copy).then_inc(s[prefix + "_T_copied"], 1)
            copies("gcn", GROUPS)
            std(rs)
            sigmoid(h_n[:, :])
            copies("att", GROUPS)
            with act.Fori(0, NI) as i:
                for k in range(2):
                    rw = att_rw[:, 2 * k * HALF * HEADS:2 * (k + 1) * HALF * HEADS]
                    w_ = att_rw[:, (2 * k + 1) * HALF * HEADS:2 * (k + 1) * HALF * HEADS]
                    act.wait_ge(s["gat_small"], i * (2 * SMALL) + k * SMALL + SMALL_LOGS)
                    a(rw, rw, ACT.Exp).then_inc(s["gat_exp"], 1)
                    act.wait_ge(s["gat_exp"], i * 2 + k + 1)
                    act.wait_ge(s["gat_acc"], i * (2 * BODY) + k * 2 * HALF)
                    for j in range(HALF):
                        n = k * HALF + j
                        for h in range(HEADS):
                            a(weighted[:, (n * HEADS + h) * F:(n * HEADS + h + 1) * F], G[:, n * ROW_H:n * ROW_H + F],
                              ACT.Copy, scale=w_[:, j * HEADS + h:j * HEADS + h + 1]).then_inc(s["gat_weighted"], 1)
            act.wait_ge(s["gat_exp_ready2"], HEADS)
            a(mask_w[:, 0:HEADS * P], mask_w[:, 0:HEADS * P], ACT.Exp).then_inc(s["gat_exp2"], 1)
            act.wait_ge(s["gat_comb_ready"], 1)
            wrcs = small[:, 21 * NB:27 * NB]
            a(wrcs, wrcs, ACT.Exp).then_inc(s["gat_comb"], 1)
            copies("gat", PAIRS, HEADS)
            std(rs)
            sigmoid(t_n[:, :])
            std(rs)
            copies("mlp", PAIRS)
            act.wait_ge(s["q_scattered"], NB * 16)
            act.wait_ge(s["mlp_tables_written"], 32)
            with act.Fori(0, NI) as i:
                for k in range(2):
                    act.wait_ge(s[f"pre_written{k}"], i * 16)
                    for g in range(2):
                        act.wait_ge(s[f"pre_stats{2 * k + g}"], i)
                        act.wait_ge(s[f"pre_made{k}"], i * 2 + g + 1)
                        n0 = k * HALF + g * GROUP
                        a(pre_s[:, n0 * P:(n0 + GROUP) * P], banks[2 * k + g][:, :],
                          ACT.Copy).then_inc(s[f"pre_copied{2 * k + g}"], 1)
                    for g in range(2):
                        act.wait_ge(s[f"pre_copied{2 * k + g}"], i + 1)
                    act.dma_start(pre_dram[i, :, k * HALF * P:(k + 1) * HALF * P],
                                  pre_s[:, k * HALF * P:(k + 1) * HALF * P]).then_inc(s[f"pre_written{k}"], 16)
            for k in range(2):
                act.wait_ge(s[f"pre_written{k}"], NI * 16)
            act.wait_ge(s["bn_var"], 1)
            a(bn[:, 1:2], bn[:, 1:2], ACT.Sqrt).then_inc(s["bn_std"], 1)
            act.wait_ge(s["bn1_ready"], 1)
            with act.Fori(0, NI) as i:
                for k in range(2):
                    act.wait_ge(s[f"pre2_loaded{k}"], i * 16 + 16)
                    act.wait_ge(s[f"h2_made{k}"], i * 2)
                    a(z_s[:, k * HALF * P:(k + 1) * HALF * P], G[:, k * HALF * P:(k + 1) * HALF * P],
                      ACT.Relu, bias=bn[:, 3:4], scale=bn[:, 2:3]).then_inc(s[f"z_made{k}"], 1)
            act.wait_ge(s["bn_var"], 2)
            a(bn[:, 9:10], bn[:, 9:10], ACT.Sqrt).then_inc(s["bn_std"], 1)
            act.wait_ge(s["w2s_ready"], 1)
            with act.Fori(0, NI) as i:
                for k in range(2):
                    act.wait_ge(s[f"pre2_loaded{k}"], i * 16 + (NI + 1) * 16)
                    act.wait_ge(s[f"h2_made{k}"], i * 2 + 2 * NI)
                    a(z_s[:, k * HALF * P:(k + 1) * HALF * P], G[:, k * HALF * P:(k + 1) * HALF * P],
                      ACT.Relu, bias=bn[:, 3:4], scale=bn[:, 2:3]).then_inc(s[f"z_made{k}"], 1)
                    act.wait_ge(s["mlp_acc"], i * BODY + k * HALF)
                    for g in range(2):
                        act.wait_ge(s[f"h2_made{k}"], i * 2 + 2 * NI + g + 1)
                        n0 = k * HALF + g * GROUP
                        a(u_s[:, n0 * P:(n0 + GROUP) * P], banks[2 * k + g][:, :],
                          ACT.Relu).then_inc(s[f"u_made{2 * k + g}"], 1)


_INS = ["x", "src", "dst", "L0_gnn_gcn_w", "L0_gnn_gcn_b", "L0_gnn_gat_w", "L0_gnn_att_src", "L0_gnn_att_dst",
        "L0_gnn_gat_b", "L0_gnn_ln_gamma", "L0_gnn_ln_beta", "L1_gnn_W1", "L1_gnn_b1", "L1_gnn_g1", "L1_gnn_be1",
        "L1_gnn_W2", "L1_gnn_b2", "L1_gnn_g2", "L1_gnn_be2"]


def kernel(**inputs):
    import numpy as _np
    import concourse.bacc as _bacc
    from concourse import mybir as _mybir
    from concourse.bass_utils import run_bass_kernel_spmd as _run

    nc = _bacc.Bacc("TRN2", target_bir_lowering=False, num_devices=1)
    arrays, args = {}, []
    for name in _INS:
        a = _np.ascontiguousarray(inputs[name])
        arrays[f"in_{name}_dram"] = a
        args.append(nc.dram_tensor(f"in_{name}_dram", a.shape, _mybir.dt.from_np(a.dtype), kind="ExternalInput").ap())
    out = nc.dram_tensor("out_dram", arrays["in_x_dram"].shape, _mybir.dt.float32, kind="ExternalOutput").ap()
    gnn_kernel(nc, *args, out)
    r = _run(nc, [arrays], core_ids=[0])
    return r.results[0]["out_dram"]
```

```python
import concourse.bass as bass
from concourse import mybir
from contextlib import ExitStack

f32 = mybir.dt.float32
bf16 = mybir.dt.bfloat16
i32 = mybir.dt.int32
ALU = mybir.AluOpType
ACT = mybir.ActivationFunctionType
AX = mybir.AxisListType

P = 128
F = 128
HEADS = 2
HALF = 8
BODY = 2 * HALF
GROUP = 4
NEG = -1e30
LN_EPS = 1e-5
BN_EPS = 1e-5
SLOPE = 0.2
ROW_H = F + 2 * HEADS
ROW_R = HEADS * F + 2 * HEADS


def gnn_kernel(nc, x, src, dst, gcn_w, gcn_b, gat_w, att_src, att_dst, gat_b, ln_gamma, ln_beta,
               W1, b1, g1, be1, W2, b2, g2, be2, out):
    N = x.shape[0]
    E = src.shape[0]
    NB = -(-N // P)
    NP = NB * P
    PAD = NP - 1
    NLAST = N - (NB - 1) * P
    T = -(-E // (P * BODY)) * BODY
    NI = T // BODY
    ELAST = E - (P - 1) * T
    assert N < NP and 0 < ELAST < T
    GROUPS = [(b, min(b + GROUP, NB)) for b in range(0, NB, GROUP)]
    PAIRS = [(b, min(b + 2, NB)) for b in range(0, NB, 2)]
    SMALL = 11
    SMALL_LOGS = 8
    FREE = 4
    SUB = 16
    NSUB = T // SUB
    assert T % SUB == 0 and NSUB <= P and FREE == GROUP
    FAR = 1 << 20

    gcn_table = nc.dram_tensor("gcn_table", (NP, F), f32).ap()
    gat_table = nc.dram_tensor("gat_table", (NP, ROW_H), f32).ap()
    p_table = nc.dram_tensor("p_table", (NP, F), f32).ap()
    q_table = nc.dram_tensor("q_table", (NP, F), f32).ap()
    q_edge = nc.dram_tensor("q_edge", (P * T, F), f32).ap()
    adst_edge = nc.dram_tensor("adst_edge", (P * T, HEADS), f32).ap()
    gcn_run = nc.dram_tensor("gcn_run", (P * T, F), f32).ap()
    gat_run = nc.dram_tensor("gat_run", (P * T, ROW_R), f32).ap()
    mlp_run = nc.dram_tensor("mlp_run", (P * T, F), f32).ap()
    pre_dram = nc.dram_tensor("pre_dram", (NI, P, BODY * P), f32).ap()
    dst_rows = nc.dram_tensor("dst_rows", (P * NSUB, SUB), f32).ap()
    dst_samples = nc.dram_tensor("dst_samples", (P, NSUB), f32).ap()
    q_edge_pt = q_edge.rearrange("(p t) f -> p t f", t=T)
    gcn_run_pt = gcn_run.rearrange("(p t) f -> p t f", t=T)
    gat_run_pt = gat_run.rearrange("(p t) f -> p t f", t=T)
    mlp_run_pt = mlp_run.rearrange("(p t) f -> p t f", t=T)

    ctx = ExitStack()
    with ctx:
        def sb(name, shape, dt=f32):
            return ctx.enter_context(nc.sbuf_tensor(name, shape, dt))

        def sem(name):
            return ctx.enter_context(nc.semaphore(name))

        src_i = sb("src_i", [P, T], i32)
        keep = sb("keep", [P, T])
        pen = sb("pen", [P, T])
        valid = pen
        adst_e = sb("adst_e", [P, T * HEADS])
        adst_v = adst_e[:, :].rearrange("p (t h) -> p t h", h=HEADS)
        x_n = sb("x_n", [P, NB * F])
        h_n = sb("h_n", [P, NB * F])
        t_n = sb("t_n", [P, NB * F])
        arena = sb("arena", [P, NB * ROW_R])
        a4 = sb("a4", [P, NB * 2 * HEADS])
        small = sb("small", [P, 30 * NB])
        has, dinv, last_f, start_f = (small[:, k * NB:(k + 1) * NB] for k in range(4))
        mu, rs, deg, cum, tot, scr = (small[:, k * NB:(k + 1) * NB] for k in range(4, 10))
        d_rel = small[:, 10 * NB:11 * NB]
        cum1 = sb("cum1", [P, NB + 1])
        degsrc = small[:, 11 * NB:12 * NB]
        carry5 = small[:, 12 * NB:17 * NB]
        mx2, ss2 = (small[:, (17 + 2 * k) * NB:(19 + 2 * k) * NB] for k in range(2))
        wr2, wc2, ws2, dn2 = (small[:, (21 + 2 * k) * NB:(23 + 2 * k) * NB] for k in range(4))
        pos_i = sb("pos_i", [P, 2 * NB], i32)
        last_i, start_i = pos_i[:, 0:NB], pos_i[:, NB:2 * NB]
        ident = sb("ident", [P, P])
        shift_in = sb("shift_in", [P, P])
        shift_across = sb("shift_across", [P, P])
        low_strict = sb("low_strict", [P, P])
        ones = sb("ones", [P, P])
        iota_f = sb("iota_f", [P, P])
        iota_i = sb("iota_i", [P, P], i32)
        node_f = sb("node_f", [P, NB])
        gcn_w_s = sb("gcn_w_s", [P, F])
        gat_w_s = sb("gat_w_s", [P, HEADS * F])
        w1_s = sb("w1_s", [P, 2 * F])
        w1T = sb("w1T", [P, 2 * F])
        w2_s = sb("w2_s", [P, F])
        w2T = sb("w2T", [P, F])
        w2Ts = sb("w2Ts", [P, F])
        att_row = sb("att_row", [P, 4 * F])
        att_v = sb("att_v", [P, 4])
        gcnb_r = sb("gcnb_r", [P, F])
        gatb_r = sb("gatb_r", [P, F])
        gamma_r = sb("gamma_r", [P, F])
        beta_r = sb("beta_r", [P, F])
        cols = sb("cols", [P, 8])
        bn = sb("bn", [P, 16])
        dfirst, dlast, dprev, dnext = (sb(n, [P, 1]) for n in ("dfirst", "dlast", "dprev", "dnext"))
        edge_i = sb("edge_i", [P, 2], i32)
        dfirst_i = sb("dfirst_i", [P, 1], i32)
        ends = sb("ends", [P, 1])
        real_node = sb("real_node", [P, 1])
        mask_qp = sb("mask_qp", [P, P])
        mask_pq = sb("mask_pq", [P, P])
        tmp_a = sb("tmp_a", [P, P])
        mask_w = sb("mask_w", [P, 4 * P])
        shift_rows = sb("shift_rows", [P, GROUP * F], bf16)
        ones_b = sb("ones_b", [P, P], bf16)
        carry_s = sb("carry_s", [P, HEADS * F + 5])
        sel = sb("sel", [P, 2 * GROUP * P])
        stage_t = sb("stage_t", [P, 2 * 512])
        q_init = sb("q_init", [P, ROW_H])
        stage_idx = sb("stage_idx", [P, 2 * HALF], i32)
        stage_keep = sb("stage_keep", [P, 2 * HALF])
        att_s = sb("att_s", [P, 8 * HALF * HEADS])
        att_rw = sb("att_rw", [P, 4 * HALF * HEADS])
        att_m = sb("att_m", [P, 2 * (HALF + 1) * HEADS])
        run = sb("run", [P, BODY * ROW_R])
        banks = [ctx.enter_context(nc.psum_tensor(f"bank{k}", [P, 512], f32)) for k in range(8)]

        def cut(at, n):
            return arena[:, at:at + n]
        G = cut(0, BODY * ROW_H)
        RAW = BODY * ROW_H
        weighted = cut(RAW, BODY * HEADS * F)
        q_load = cut(RAW, BODY * F)
        q_cur = cut(RAW + BODY * F, BODY * F)
        pre_s = cut(RAW + 2 * BODY * F, BODY * P)
        z_s = cut(RAW, BODY * P)
        u_s = cut(RAW + BODY * F, BODY * P)
        assert RAW + 3 * BODY * F <= NB * ROW_R
        dst_i = cut(0, T + 1).bitcast(i32)
        dst_f = cut(T + 8, T + 1)
        samples = cut(2 * T + 16, NSUB)
        level_a = cut(0, NB * NSUB)
        level_b = cut(NB * NSUB, NB * SUB)
        assert NB * (NSUB + SUB) <= NB * F
        zeros = t_n[:, 0:2 * T]
        assert 2 * T <= NB * F
        stats = t_n[:, 0:(T // GROUP) * 6]

        x_v = x_n[:, :].rearrange("p (b f) -> p b f", f=F)
        h_v = h_n[:, :].rearrange("p (b f) -> p b f", f=F)
        t_v = t_n[:, :].rearrange("p (b f) -> p b f", f=F)
        R_v = arena[:, :].rearrange("p (b r) -> p b r", r=ROW_R)
        Rf = arena[:, 0:NB * F]
        Rf_v = Rf.rearrange("p (b f) -> p b f", f=F)
        sq_n = arena[:, NB * F:2 * NB * F]

        def wide(a):
            return a.unsqueeze(2).to_broadcast([P, NB, F])

        def rowwise(a, n):
            return a.unsqueeze(1).to_broadcast([P, n, a.shape[-1]])

        names = """const_made x_clear idx_clear x_loaded idx_loaded ends_loaded weights_loaded
        zero_made filled pool_step vec_step
        search_ready search_written level1 level2 samples_in rows_in keep_staged slots_free mask_row mask_T mask_copied w1_T w2_T wT_copied
        cum_ready cum_done
        var_ready std_ready
        gcn_ready gcn_table_written
        gcn_idx gcn_gathered0 gcn_gathered1 gcn_acc gcn_written0 gcn_written1
        gcn_rows gcn_carry gcn_carry_copied gcn_sel gcn_picked gcn_merged gcn_lin_ready
        gcn_T gcn_T_copied gcn_lin gcn_lin_used
        sig_ready sig_done
        att_lin_ready att_T att_T_copied att_lin att_ready
        gat_table_written adst_scattered adst_loaded adst_init
        gat_idx gat_gathered0 gat_gathered1 gat_small gat_exp gat_weighted gat_acc
        gat_written0 gat_written1
        att_v_done gat_exp_ready2 gat_exp2
        gat_rows gat_mrow_ready gat_mrow gat_wt_ready gat_wt_T gat_wt_copied gat_carry
        gat_carry_copied gat_sel gat_tail gat_comb_ready gat_comb gat_sel2 gat_picked gat_merged
        gat_T gat_T_copied gat_lin gat_lin_used
        mlp_lin_ready mlp_T mlp_T_copied mlp_lin mlp_lin_used mlp_ready mlp_tables_written
        q_scattered q_init_loaded mlp_idx mlp_gathered0 mlp_gathered1
        q_loaded0 q_loaded1 q_acc pre_made0 pre_made1 pre_copied0 pre_copied1 pre_copied2 pre_copied3
        pre_stats0 pre_stats1 pre_stats2 pre_stats3 pre_written0 pre_written1
        bn_var bn_std bn1_ready bn2_ready
        pre2_loaded0 pre2_loaded1 z_made0 z_made1 z_masked0 z_masked1 h2_made0 h2_made1
        bn2_row bn2_row_done
        w2s_ready  u_made0 u_made1 u_made2 u_made3 mlp_acc mlp_written0
        mlp_written1 mlp_rows mlp_carry mlp_carry_copied mlp_sel mlp_picked mlp_merged
        out_ready out_written""".split()
        s = {n: sem(n) for n in names}

        def step(eng, count, ins, name):
            count[name] = count.get(name, 0) + 1
            ins.then_inc(s[name], 1)
            eng.wait_ge(s[name], count[name])

        def wait(eng, name, value):
            if not (isinstance(value, int) and value <= 0):
                eng.wait_ge(s[name], value)

        def bodies(eng, body):
            body(0, False)
            with eng.Fori(1, NI - 1) as i:
                body(i, False)
            body(NI - 1, True)

        block = ctx.enter_context(nc.Block())

        @block.sync
        def _(sp):
            sp.wait_ge(s["x_clear"], 1)
            sp.dma_start(x_v[:, 0:NB - 1, :],
                         x[0:(NB - 1) * P, :].rearrange("(b p) f -> p b f", p=P)).then_inc(s["x_loaded"], 16)
            sp.dma_start(x_v[0:NLAST, NB - 1, :], x[(NB - 1) * P:N, :]).then_inc(s["x_loaded"], 16)
            sp.wait_ge(s["idx_clear"], 3)
            for tile, edge in ((dst_i, dst), (src_i, src)):
                sp.dma_start(tile[0:P - 1, 0:T],
                             edge[0:(P - 1) * T].rearrange("(p t) -> p t", t=T)).then_inc(s["idx_loaded"], 16)
                sp.dma_start(tile[P - 1:P, 0:ELAST],
                             edge[(P - 1) * T:E].rearrange("(p t) -> p t", p=1)).then_inc(s["idx_loaded"], 16)
            sp.wait_ge(s["idx_loaded"], 64)
            sp.dma_start(edge_i[1:P, 0:1], dst_i[0:P - 1, T - 1:T]).then_inc(s["ends_loaded"], 16)
            sp.dma_start(edge_i[0:P - 1, 1:2], dst_i[1:P, 0:1]).then_inc(s["ends_loaded"], 16)
            sp.wait_ge(s["search_ready"], 2)
            sp.dma_start(dst_rows.rearrange("(p u) c -> p (u c)", p=P), dst_f[:, 1:T + 1]).then_inc(s["search_written"], 16)
            sp.dma_start(dst_samples, samples).then_inc(s["search_written"], 16)
            sp.wait_ge(s["gcn_ready"], 1)
            sp.dma_start(gcn_table.rearrange("(b p) f -> p b f", p=P), h_v).then_inc(s["gcn_table_written"], 16)
            def gcn_out(i, last):
                for k in range(2):
                    sp.wait_ge(s["gcn_acc"], i * BODY + (k + 2) * HALF)
                    sp.dma_start(gcn_run_pt[:, bass.ds(i * BODY + k * HALF, HALF), :],
                                 run[:, k * HALF * F:(k + 1) * HALF * F].rearrange("p (t f) -> p t f", f=F)
                                 ).then_inc(s[f"gcn_written{k}"], 16)
            bodies(sp, gcn_out)
            sp.wait_ge(s["att_ready"], 1)
            t_rows = gat_table.rearrange("(b p) f -> p b f", p=P)
            sp.dma_start(t_rows[:, :, 0:F], h_v).then_inc(s["gat_table_written"], 16)
            sp.dma_start(t_rows[:, :, F:ROW_H],
                         a4[:, :].rearrange("p (b c) -> p b c", c=4)).then_inc(s["gat_table_written"], 16)
            sp.wait_ge(s["adst_scattered"], NB * 16)
            sp.dma_start(adst_e[:, :], adst_edge.rearrange("(p t) h -> p (t h)", t=T)).then_inc(s["adst_loaded"], 16)
            def gat_out(i, last):
                for k in range(2):
                    sp.wait_ge(s["gat_acc"], i * (2 * BODY) + (k + 2) * 2 * HALF)
                    sp.dma_start(gat_run_pt[:, bass.ds(i * BODY + k * HALF, HALF), :],
                                 run[:, k * HALF * ROW_R:(k + 1) * HALF * ROW_R].rearrange("p (t f) -> p t f", f=ROW_R)
                                 ).then_inc(s[f"gat_written{k}"], 16)
            bodies(sp, gat_out)
            sp.wait_ge(s["mlp_ready"], 1)
            sp.dma_start(p_table.rearrange("(b p) f -> p b f", p=P), t_v).then_inc(s["mlp_tables_written"], 16)
            sp.dma_start(q_table.rearrange("(b p) f -> p b f", p=P), Rf_v).then_inc(s["mlp_tables_written"], 16)
            sp.wait_ge(s["q_scattered"], NB * 16)
            sp.wait_ge(s["mlp_tables_written"], 32)
            def q_in(i, last):
                for k in range(2):
                    wait(sp, "q_acc", i * BODY + k * HALF)
                    sp.dma_start(q_load[:, k * HALF * F:(k + 1) * HALF * F].rearrange("p (t f) -> p t f", f=F),
                                 q_edge_pt[:, bass.ds(i * BODY + k * HALF, HALF), :]).then_inc(s[f"q_loaded{k}"], 16)
            bodies(sp, q_in)
            sp.wait_ge(s["bn1_ready"], 1)
            def pre_in2(i, last):
                for k in range(2):
                    wait(sp, f"z_made{k}", i)
                    sp.dma_start(G[:, k * HALF * P:(k + 1) * HALF * P],
                                 pre_dram[i, :, k * HALF * P:(k + 1) * HALF * P]).then_inc(s[f"pre2_loaded{k}"], 16)
            bodies(sp, pre_in2)
            sp.wait_ge(s["w2s_ready"], 1)
            def pre_in3(i, last):
                for k in range(2):
                    wait(sp, f"z_made{k}", i + NI)
                    sp.dma_start(G[:, k * HALF * P:(k + 1) * HALF * P],
                                 pre_dram[i, :, k * HALF * P:(k + 1) * HALF * P]).then_inc(s[f"pre2_loaded{k}"], 16)
            bodies(sp, pre_in3)
            sp.wait_ge(s["out_ready"], 1)
            sp.dma_start(out[0:(NB - 1) * P, :].rearrange("(b p) f -> p b f", p=P),
                         x_v[:, 0:NB - 1, :]).then_inc(s["out_written"], 16)
            sp.dma_start(out[(NB - 1) * P:N, :], x_v[0:NLAST, NB - 1, :]).then_inc(s["out_written"], 16)
            sp.wait_ge(s["out_written"], 32)

        @block.gpsimd
        def _(pool):
            count = {}

            def st(ins):
                step(pool, count, ins, "pool_step")

            st(nc.gpsimd.iota(iota_i[:, :], pattern=[[1, P]], base=0, channel_multiplier=0))
            st(nc.gpsimd.tensor_copy(iota_f[:, :], iota_i[:, :]))
            st(nc.gpsimd.iota(iota_i[:, 0:NB], pattern=[[P, NB]], base=0, channel_multiplier=1))
            st(nc.gpsimd.tensor_copy(node_f[:, :], iota_i[:, 0:NB]))
            st(nc.gpsimd.memset(ones[:, :], 1.0))
            st(nc.gpsimd.memset(ident[:, :], 0.0))
            st(nc.gpsimd.affine_select(out=ident[:, :], in_=ident[:, :], compare_op=ALU.not_equal, fill=1.0,
                                       base=0, pattern=[[-1, P]], channel_multiplier=1))
            st(nc.gpsimd.memset(shift_in[:, :], 0.0))
            st(nc.gpsimd.affine_select(out=shift_in[:, :], in_=shift_in[:, :], compare_op=ALU.not_equal, fill=1.0,
                                       base=1, pattern=[[-1, P]], channel_multiplier=1))
            st(nc.gpsimd.memset(shift_across[:, :], 0.0))
            st(nc.gpsimd.affine_select(out=shift_across[:, :], in_=shift_across[:, :], compare_op=ALU.not_equal,
                                       fill=1.0, base=1 - P, pattern=[[-1, P]], channel_multiplier=1))
            st(nc.gpsimd.affine_select(out=low_strict[:, :], in_=ones[:, :], compare_op=ALU.is_gt, fill=0.0,
                                       base=0, pattern=[[-1, P]], channel_multiplier=1))
            nc.gpsimd.affine_select(out=real_node[:, :], in_=ones[:, 0:1], compare_op=ALU.is_gt, fill=0.0,
                                    base=NLAST, pattern=[[0, 1]], channel_multiplier=-1).then_inc(s["const_made"], 1)

            def hold():
                pool.sem_inc(s["slots_free"], 1)

            def gather(tile, table, idx):
                return pool.indirect_dma_start(out=tile, out_offset=None, in_=table,
                                               in_offset=bass.IndirectOffsetOnAxis(ap=idx, axis=0))

            def scatter(table, tile, idx):
                return pool.indirect_dma_start(out=table, out_offset=bass.IndirectOffsetOnAxis(ap=idx, axis=0),
                                               in_=tile, in_offset=None, bounds_check=P * T - 1, oob_is_err=False)

            def source_rows(table, row, prefix, rows_used):
                def body(i, last):
                    for k in range(2):
                        pool.wait_ge(s[prefix + "_idx"], i * 2 + k + 1)
                        for j in range(HALF):
                            n = k * HALF + j
                            if j % FREE == 0:
                                rows_used(i, n)
                                hold()
                            gather(G[:, n * row:(n + 1) * row], table, stage_idx[:, n:n + 1]
                                   ).then_inc(s[f"{prefix}_gathered{k}"], 16)
                bodies(pool, body)

            pool.wait_ge(s["search_written"], 32)
            pool.wait_ge(s["level1"], 1)
            for b in range(NB):
                gather(level_a[:, b * NSUB:(b + 1) * NSUB], dst_samples, last_i[:, b:b + 1]).then_inc(s["samples_in"], 16)
            pool.wait_ge(s["level2"], 1)
            for b in range(NB):
                gather(level_b[:, b * SUB:(b + 1) * SUB], dst_rows, last_i[:, b:b + 1]).then_inc(s["rows_in"], 16)

            pool.wait_ge(s["gcn_table_written"], 16)
            source_rows(gcn_table, F, "gcn", lambda i, n: wait(pool, "gcn_acc", i * BODY + n - HALF + FREE))
            for k in range(2):
                pool.wait_ge(s[f"gcn_written{k}"], NI * 16)
            for b in range(NB):
                gather(Rf[:, b * F:(b + 1) * F], gcn_run, last_i[:, b:b + 1]).then_inc(s["gcn_rows"], 16)
            pool.wait_ge(s["gat_table_written"], 32)
            pool.wait_ge(s["filled"], (NI + 1) * 16)
            for b in range(NB):
                scatter(adst_edge, a4[:, 4 * b + HEADS:4 * b + 2 * HEADS], start_i[:, b:b + 1]
                        ).then_inc(s["adst_scattered"], 16)
            gather(q_init[:, :], gat_table, dfirst_i[:, 0:1]).then_inc(s["adst_init"], 16)
            source_rows(gat_table, ROW_H, "gat",
                        lambda i, n: wait(pool, "gat_acc", i * (2 * BODY) + 2 * (n - HALF + FREE)))
            for k in range(2):
                pool.wait_ge(s[f"gat_written{k}"], NI * 16)
            for b in range(NB):
                gather(arena[:, b * ROW_R:(b + 1) * ROW_R], gat_run, last_i[:, b:b + 1]).then_inc(s["gat_rows"], 16)
            pool.wait_ge(s["mlp_tables_written"], 32)
            for b in range(NB):
                scatter(q_edge, Rf[:, b * F:(b + 1) * F], start_i[:, b:b + 1]).then_inc(s["q_scattered"], 16)
            gather(q_init[:, 0:F], q_table, dfirst_i[:, 0:1]).then_inc(s["q_init_loaded"], 16)
            pool.wait_ge(s["q_scattered"], NB * 16)
            source_rows(p_table, F, "mlp",
                        lambda i, n: wait(pool, f"pre_made{n // HALF}", i * 2 - 1 + n % HALF // GROUP))
            def mlp_out(i, last):
                for k in range(2):
                    pool.wait_ge(s["mlp_acc"], i * BODY + (k + 2) * HALF)
                    pool.dma_start(mlp_run_pt[:, bass.ds(i * BODY + k * HALF, HALF), :],
                                   run[:, k * HALF * F:(k + 1) * HALF * F].rearrange("p (t f) -> p t f", f=F)
                                   ).then_inc(s[f"mlp_written{k}"], 16)
            bodies(pool, mlp_out)
            for k in range(2):
                pool.wait_ge(s[f"mlp_written{k}"], NI * 16)
            for b in range(NB):
                gather(Rf[:, b * F:(b + 1) * F], mlp_run, last_i[:, b:b + 1]).then_inc(s["mlp_rows"], 16)

        @block.tensor
        def _(pe):
            mm = nc.tensor.matmul

            def transpose(o, a):
                return mm(o, a, ident[:, :], start=True, stop=True)

            pe.wait_ge(s["const_made"], 1)
            pe.wait_ge(s["weights_loaded"], 16 * 16)
            for c in range(2):
                last = transpose(banks[2][:, c * F:(c + 1) * F], w1_s[:, c * F:(c + 1) * F])
            last.then_inc(s["w1_T"], 1)
            transpose(banks[3][:, 0:F], w2_s[:, :]).then_inc(s["w2_T"], 1)
            pe.wait_ge(s["mask_row"], 1)
            mm(banks[1][:, 0:P], ones[:, :], tmp_a[:, :], start=True, stop=True).then_inc(s["mask_T"], 1)
            pe.wait_ge(s["mask_row"], 2)
            transpose(banks[1][:, P:2 * P], mask_qp[:, :]).then_inc(s["mask_T"], 1)
            pe.wait_ge(s["mask_row"], 3)
            mm(banks[0][:, 0:P], ones[:, :], tmp_a[:, :], start=True, stop=True).then_inc(s["mask_T"], 1)
            pe.wait_ge(s["cum_ready"], 1)
            mm(banks[5][:, 0:NB], shift_in[:, :], cum1[:, 1:NB + 1], start=True, stop=False)
            mm(banks[5][:, 0:NB], shift_across[:, :], cum1[:, 0:NB], start=False, stop=True).then_inc(s["cum_done"], 1)

            pe.wait_ge(s["gcn_acc"], HALF + T)
            mm(banks[0][:, 0:F], mask_pq[:, :], run[:, (BODY - 1) * F:BODY * F],
               start=True, stop=True).then_inc(s["gcn_carry"], 1)
            pe.wait_ge(s["gcn_carry_copied"], 1)

            def pick(prefix):
                for g, (b0, b1_) in enumerate(GROUPS):
                    pe.wait_ge(s[prefix + "_sel"], b1_)
                    if g >= 2:
                        pe.wait_ge(s[prefix + "_merged"], GROUPS[g - 2][1])
                    for b in range(b0, b1_):
                        last = mm(banks[2 + g % 2][:, (b - b0) * F:(b - b0 + 1) * F],
                                  sel[:, (b % (2 * GROUP)) * P:(b % (2 * GROUP) + 1) * P],
                                  carry_s[:, 0:F], start=True, stop=True)
                    last.then_inc(s[prefix + "_picked"], 1)
            pick("gcn")

            def linear(prefix, source, w, n_out, groups, parts=1):
                width = GROUP // parts
                for g in range(len(groups) + 1):
                    if g < len(groups):
                        b0, b1_ = groups[g]
                        if g >= 2:
                            pe.wait_ge(s[prefix + "_T_copied"], g - 1)
                        for b in range(b0, b1_):
                            for c in range(parts):
                                at = (b - b0) * parts + c
                                last = transpose(banks[4 + g % 2][:, at * P:(at + 1) * P], source(b, c))
                        last.then_inc(s[prefix + "_T"], 1)
                    if g >= 1:
                        b0, b1_ = groups[g - 1]
                        pe.wait_ge(s[prefix + "_T_copied"], g)
                        if g >= 3:
                            pe.wait_ge(s[prefix + "_lin_used"], g - 2)
                        for b in range(b0, b1_):
                            for c in range(parts):
                                at = (b - b0) * parts + c
                                o = banks[6 + (g - 1) % 2][:, (b - b0) * n_out:(b - b0 + 1) * n_out]
                                last = mm(o, stage_t[:, (g - 1) % 2 * 512 + at * P:(g - 1) % 2 * 512 + (at + 1) * P],
                                          w[:, c * n_out:(c + 1) * n_out], start=(c == 0), stop=(c == parts - 1))
                        last.then_inc(s[prefix + "_lin"], 1)

            pe.wait_ge(s["gcn_lin_ready"], 1)
            linear("gcn", lambda b, c: Rf[:, b * F:(b + 1) * F], gcn_w_s, F, GROUPS)
            pe.wait_ge(s["att_lin_ready"], 1)
            for g in range(len(GROUPS) + 1):
                if g < len(GROUPS):
                    b0, b1_ = GROUPS[g]
                    if g >= 2:
                        pe.wait_ge(s["att_T_copied"], g - 1)
                    for b in range(b0, b1_):
                        last = transpose(banks[4 + g % 2][:, (b - b0) * P:(b - b0 + 1) * P],
                                         h_n[:, b * F:(b + 1) * F])
                    last.then_inc(s["att_T"], 1)
                if g >= 1:
                    b0, b1_ = GROUPS[g - 1]
                    pe.wait_ge(s["att_T_copied"], g)
                    for b in range(b0, b1_):
                        at = (g - 1) % 2 * 512 + (b - b0) * P
                        last = mm(banks[6][:, b * 4:(b + 1) * 4], stage_t[:, at:at + P], att_v[:, :],
                                  start=True, stop=True)
                    last.then_inc(s["att_lin"], 1)

            pe.wait_ge(s["gat_acc"], 2 * (HALF + T))
            tail = (BODY - 1) * ROW_R
            for c in range(HEADS):
                pe.wait_ge(s["gat_mrow_ready"], c + 1)
                mm(banks[0][:, c * P:(c + 1) * P], ones[:, :], tmp_a[:, :],
                   start=True, stop=True).then_inc(s["gat_mrow"], 1)
            for c in range(HEADS):
                pe.wait_ge(s["gat_wt_ready"], c + 1)
                transpose(banks[1][:, c * P:(c + 1) * P], mask_w[:, c * P:(c + 1) * P]).then_inc(s["gat_wt_T"], 1)
            pe.wait_ge(s["gat_wt_copied"], HEADS)
            for c in range(HEADS):
                wt = mask_w[:, (2 + c) * P:(3 + c) * P]
                mm(banks[2][:, c * F:(c + 1) * F], wt, run[:, tail + c * F:tail + (c + 1) * F], start=True, stop=True)
                last = mm(banks[3][:, c:c + 1], wt, run[:, tail + HEADS * F + c:tail + HEADS * F + c + 1],
                          start=True, stop=True)
            last.then_inc(s["gat_carry"], 1)
            pe.wait_ge(s["gat_carry_copied"], 1)
            for g, (b0, b1_) in enumerate(GROUPS):
                pe.wait_ge(s["gat_sel"], b1_)
                for b in range(b0, b1_):
                    last = mm(banks[0][:, b * 5:(b + 1) * 5], sel[:, (b % (2 * GROUP)) * P:(b % (2 * GROUP) + 1) * P],
                              carry_s[:, HEADS * F:HEADS * F + 5], start=True, stop=True)
                last.then_inc(s["gat_tail"], 1)
            for g, (b0, b1_) in enumerate(PAIRS):
                pe.wait_ge(s["gat_sel2"], b1_)
                if g >= 2:
                    pe.wait_ge(s["gat_merged"], PAIRS[g - 2][1])
                for b in range(b0, b1_):
                    last = mm(banks[2 + g % 2][:, (b - b0) * HEADS * F:(b - b0 + 1) * HEADS * F],
                              sel[:, (b % (2 * GROUP)) * P:(b % (2 * GROUP) + 1) * P],
                              carry_s[:, 0:HEADS * F], start=True, stop=True)
                last.then_inc(s["gat_picked"], 1)
            pe.wait_ge(s["gat_merged"], NB)
            linear("gat", lambda b, c: arena[:, b * ROW_R + c * F:b * ROW_R + (c + 1) * F], gat_w_s, F, PAIRS, HEADS)
            pe.wait_ge(s["mlp_lin_ready"], 1)
            linear("mlp", lambda b, c: h_n[:, b * F:(b + 1) * F], w1T, 2 * F, PAIRS)

            def pre_body(i, last):
                for k in range(2):
                    pe.wait_ge(s[f"mlp_gathered{k}"], i * (16 * HALF) + 16 * HALF)
                    for g in range(2):
                        n0 = k * HALF + g * GROUP
                        pe.wait_ge(s["q_acc"], i * BODY + n0 + GROUP + HALF)
                        bank = banks[2 * k + g]
                        wait(pe, f"pre_copied{2 * k + g}", i)
                        for j in range(GROUP):
                            n = n0 + j
                            mm(bank[:, j * P:(j + 1) * P], G[:, n * F:(n + 1) * F], ident[:, :],
                               start=True, stop=False)
                            o = mm(bank[:, j * P:(j + 1) * P], q_cur[:, n * F:(n + 1) * F], ident[:, :],
                                      start=False, stop=True)
                        o.then_inc(s[f"pre_made{k}"], 1)
            bodies(pe, pre_body)
            def h2_body(i, last):
                for k in range(2):
                    pe.wait_ge(s[f"z_masked{k}"], i + 1)
                    for g in range(2):
                        n0 = k * HALF + g * GROUP
                        pe.wait_ge(s[f"pre_stats{2 * k + g}"], i + NI)
                        mm(banks[2 * k + g][:, :], w2T[:, :], z_s[:, n0 * P:(n0 + GROUP) * P],
                           start=True, stop=True).then_inc(s[f"h2_made{k}"], 1)
            bodies(pe, h2_body)
            for c in range(2):
                pe.wait_ge(s["bn2_row"], c + 1)
                mm(banks[4 + c][:, 0:F], ones[:, :], tmp_a[:, :], start=True, stop=True).then_inc(s["bn2_row_done"], 1)
            pe.wait_ge(s["w2s_ready"], 1)
            def h3_body(i, last):
                for k in range(2):
                    pe.wait_ge(s[f"z_made{k}"], i + NI + 1)
                    for g in range(2):
                        n0 = k * HALF + g * GROUP
                        wait(pe, f"u_made{2 * k + g}", i)
                        mm(banks[2 * k + g][:, :], ones_b[:, :], shift_rows[:, :], start=True, stop=False)
                        for j in range(GROUP):
                            n = n0 + j
                            o = banks[2 * k + g][:, j * F:(j + 1) * F]
                            m = mm(o, z_s[:, n * P:(n + 1) * P], w2Ts[:, :], start=False, stop=(j == GROUP - 1))
                        m.then_inc(s[f"h2_made{k}"], 1)
            bodies(pe, h3_body)
            pe.wait_ge(s["mlp_acc"], HALF + T)
            mm(banks[0][:, 0:F], mask_pq[:, :], run[:, (BODY - 1) * F:BODY * F],
               start=True, stop=True).then_inc(s["mlp_carry"], 1)
            pe.wait_ge(s["mlp_carry_copied"], 1)
            pick("mlp")

        @block.vector
        def _(dve):
            count = {}
            v = nc.vector

            def st(ins, name="vec_step"):
                step(dve, count, ins, name)

            tt, ts, stt = v.tensor_tensor, v.tensor_scalar, v.scalar_tensor_tensor
            x_n3, h_n3, t_n3, sq3 = (a.rearrange("p (b f) -> p b f", f=F) for a in (x_n[:, :], h_n[:, :], t_n[:, :], sq_n))

            def layernorm(src_, dst_, tmp):
                st(v.tensor_reduce(mu, src_, AX.X, ALU.add))
                st(ts(mu, mu, 1.0 / F, None, ALU.mult))
                st(tt(tmp, src_, wide(mu), ALU.subtract))
                st(tt(sq3, tmp, tmp, ALU.mult))
                st(v.tensor_reduce(rs, sq3, AX.X, ALU.add))
                st(ts(rs, rs, 1.0 / F, LN_EPS, ALU.mult, ALU.add), "var_ready")
                dve.wait_ge(s["std_ready"], count["var_ready"])
                st(v.reciprocal(rs, rs))
                st(tt(dst_, tmp, wide(rs), ALU.mult))

            def gamma_beta_silu(a3, a2):
                st(tt(a3, a3, rowwise(gamma_r[:, :], NB), ALU.mult))
                st(tt(a3, a3, rowwise(beta_r[:, :], NB), ALU.add), "sig_ready")
                dve.wait_ge(s["sig_done"], count["sig_ready"])
                st(tt(a2, a2, sq_n, ALU.mult))

            st(v.memset(x_n[:, (NB - 1) * F:NB * F], 0.0), "x_clear")
            st(v.memset(dst_i, PAD), "idx_clear")
            st(v.memset(src_i[:, :], PAD), "idx_clear")
            st(v.memset(edge_i[:, :], -1), "idx_clear")
            dve.wait_ge(s["idx_loaded"], 64)
            dve.wait_ge(s["ends_loaded"], 32)
            st(v.tensor_copy(dst_f[:, 1:T + 1], dst_i[:, 0:T]))
            st(v.tensor_copy(dst_f[:, 0:1], edge_i[:, 0:1]))
            st(v.tensor_copy(dnext[:, :], edge_i[:, 1:2]))
            st(v.tensor_copy(dfirst[:, :], dst_f[:, 1:2]))
            st(v.tensor_copy(dfirst_i[:, :], dst_i[:, 0:1]))
            st(v.tensor_copy(samples, dst_f[:, 1:T + 1].rearrange("p (u c) -> p u c", c=SUB)[:, :, 0]), "search_ready")
            dve.wait_ge(s["const_made"], 1)
            st(v.memset(ones_b[:, :], 1.0), "search_ready")
            st(tt(keep[:, 0:T], dst_f[:, 1:T + 1], dst_f[:, 0:T], ALU.is_equal))
            st(ts(pen[:, :], keep[:, 0:T], -NEG, NEG, ALU.mult, ALU.add))
            st(tt(ends[:, :], dfirst[:, :], dnext[:, :], ALU.not_equal))
            st(ts(d_rel, iota_f[:, 0:NB], float(-P), dfirst[:, 0:1], ALU.mult, ALU.add))
            st(ts(tmp_a[:, :], ident[:, :], dst_f[:, T:T + 1], None, ALU.mult), "mask_row")
            dve.wait_ge(s["mask_T"], 1)
            st(stt(mask_qp[:, :], banks[1][:, 0:P], dfirst[:, 0:1], low_strict[:, :], ALU.is_equal, ALU.mult),
               "mask_row")
            st(ts(tmp_a[:, :], ident[:, :], dfirst[:, 0:1], None, ALU.mult), "mask_row")

            def count_upto(out_, table3, n):
                hits = t_n[:, 0:NB * n].rearrange("p (b c) -> p b c", c=n)
                st(tt(hits, node_f[:, :].unsqueeze(2).to_broadcast([P, NB, n]), table3, ALU.is_ge))
                st(v.tensor_reduce(out_, hits, AX.X, ALU.add))

            dve.wait_ge(s["mask_T"], 3)
            count_upto(cum, banks[0][:, 0:P].unsqueeze(1).to_broadcast([P, NB, P]), P)
            st(ts(tot, cum, -1.0, 0.0, ALU.add, ALU.max))
            st(v.tensor_copy(last_i, tot), "level1")
            dve.wait_ge(s["x_loaded"], 32)
            layernorm(x_n3, h_n3, t_n3)
            st(ts(h_n[:, :], h_n[:, :], 0.0, None, ALU.max))
            dve.wait_ge(s["samples_in"], NB * 16)
            count_upto(cum, level_a.rearrange("p (b c) -> p b c", c=NSUB), NSUB)
            st(ts(cum, cum, -1.0, 0.0, ALU.add, ALU.max))
            st(stt(tot, tot, float(NSUB), cum, ALU.mult, ALU.add))
            st(v.tensor_copy(last_i, tot), "level2")
            dve.wait_ge(s["rows_in"], NB * 16)
            count_upto(cum, level_b.rearrange("p (b c) -> p b c", c=SUB), SUB)
            st(v.memset(cum1[:, 0:1], 0.0))
            st(stt(cum1[:, 1:NB + 1], tot, float(SUB), cum, ALU.mult, ALU.add), "cum_ready")
            dve.wait_ge(s["cum_done"], 1)
            st(v.tensor_copy(start_f, banks[5][:, 0:NB]))
            st(tt(deg, cum1[:, 1:NB + 1], start_f, ALU.subtract))
            st(ts(has, deg, 0.5, None, ALU.is_gt))
            st(ts(rs, deg, 1.0, None, ALU.add), "var_ready")
            dve.wait_ge(s["std_ready"], count["var_ready"])
            st(v.reciprocal(dinv, rs))
            st(ts(last_f, cum1[:, 1:NB + 1], -1.0, 0.0, ALU.add, ALU.max))
            st(v.tensor_copy(last_i, last_f))
            st(ts(scr, has, float(-FAR), float(FAR), ALU.mult, ALU.add))
            st(tt(start_f, start_f, scr, ALU.add))
            st(v.tensor_copy(start_i, start_f))

            st(tt(h_n3, h_n3, wide(dinv), ALU.mult), "gcn_ready")
            st(v.memset(zeros, 0.0), "zero_made")

            def stage_idx_of(prefix, i, k):
                v.tensor_copy(stage_idx[:, k * HALF:(k + 1) * HALF],
                              src_i[:, bass.ds(i * BODY + k * HALF, HALF)]).then_inc(s[prefix + "_idx"], 1)

            def stage_keep_of(i, k):
                v.tensor_copy(stage_keep[:, k * HALF:(k + 1) * HALF],
                              keep[:, bass.ds(i * BODY + k * HALF, HALF)]).then_inc(s["keep_staged"], 1)

            def keep_ready(sweep, i, k):
                dve.wait_ge(s["keep_staged"], (i + sweep * NI) * 2 + k + 1)

            def prime(acc, names_=HALF):
                for c in range(names_):
                    st(v.memset(run[:, (BODY - 1) * F + c * (F // names_):(BODY - 1) * F + (c + 1) * (F // names_)], 0.0), acc)

            def accumulate(prefix, sweep, rows, ready):
                def body(i, last):
                    for k in range(2):
                        ready(i, k, 0)
                        if prefix == "gcn" and not last:
                            stage_idx_of(prefix, i + 1, k)
                        keep_ready(sweep, i, k)
                        wait(dve, f"{prefix}_written{k}", i * 16)
                        for j in range(HALF):
                            n = k * HALF + j
                            if j == GROUP:
                                ready(i, k, 1)
                            before = (n - 1) % BODY
                            stt(run[:, n * F:(n + 1) * F], run[:, before * F:(before + 1) * F],
                                stage_keep[:, n:n + 1], rows[:, n * F:(n + 1) * F],
                                ALU.mult, ALU.add).then_inc(s[prefix + "_acc"], 1)
                            dve.wait_ge(s[prefix + "_acc"], i * BODY + HALF + n + 1)
                        if not last:
                            stage_keep_of(i + 1, k)
                bodies(dve, body)

            prime("gcn_acc")
            for k in range(2):
                stage_idx_of("gcn", 0, k)
                stage_keep_of(0, k)

            def gcn_rows_ready(i, k, g):
                if g == 0:
                    dve.wait_ge(s[f"gcn_gathered{k}"], i * (16 * HALF) + 16 * HALF)
            accumulate("gcn", 0, G, gcn_rows_ready)

            def pick(prefix):
                def select(b):
                    st(ts(sel[:, (b % (2 * GROUP)) * P:(b % (2 * GROUP) + 1) * P], iota_f[:, :], d_rel[:, b:b + 1],
                          ends[:, 0:1], ALU.is_equal, ALU.mult), prefix + "_sel")
                for b in range(*GROUPS[0]):
                    select(b)
                for g, (b0, b1_) in enumerate(GROUPS):
                    if g + 1 < len(GROUPS):
                        if g >= 1:
                            dve.wait_ge(s[prefix + "_picked"], g)
                        for b in range(*GROUPS[g + 1]):
                            select(b)
                    dve.wait_ge(s[prefix + "_picked"], g + 1)
                    for b in range(b0, b1_):
                        st(stt(Rf[:, b * F:(b + 1) * F], Rf[:, b * F:(b + 1) * F], has[:, b:b + 1],
                               banks[2 + g % 2][:, (b - b0) * F:(b - b0 + 1) * F], ALU.mult, ALU.add),
                           prefix + "_merged")

            dve.wait_ge(s["filled"], (NI + 1) * 16)
            dve.wait_ge(s["gcn_carry"], 1)
            st(v.tensor_copy(carry_s[:, 0:F], banks[0][:, 0:F]), "gcn_carry_copied")
            dve.wait_ge(s["gcn_rows"], NB * 16)
            pick("gcn")
            st(tt(Rf, Rf, h_n[:, :], ALU.add))
            st(tt(Rf_v, Rf_v, wide(dinv), ALU.mult), "gcn_lin_ready")
            for g, (b0, b1_) in enumerate(GROUPS):
                dve.wait_ge(s["gcn_lin"], g + 1)
                st(tt(h_v[:, b0:b1_, :], banks[6 + g % 2][:, 0:(b1_ - b0) * F].rearrange("p (b f) -> p b f", f=F),
                      rowwise(gcnb_r[:, :], b1_ - b0), ALU.add), "gcn_lin_used")
            layernorm(h_n3, h_n3, t_n3)
            gamma_beta_silu(h_n3, h_n[:, :])

            for c in range(2):
                for h in range(HEADS):
                    st(tt(tmp_a[:, :], gat_w_s[:, h * F:(h + 1) * F],
                          att_row[:, (c * HEADS + h) * F:(c * HEADS + h + 1) * F], ALU.mult))
                    st(v.tensor_reduce(att_v[:, c * HEADS + h:c * HEADS + h + 1], tmp_a[:, :], AX.X, ALU.add),
                       "att_v_done")
            st(v.memset(scr, 0.0), "att_lin_ready")
            dve.wait_ge(s["att_lin"], len(GROUPS))
            st(v.tensor_copy(a4[:, :], banks[6][:, 0:4 * NB]), "att_ready")
            dve.wait_ge(s["adst_loaded"], 16)
            dve.wait_ge(s["adst_init"], 16)
            for h in range(HEADS):
                st(v.tensor_tensor_scan(adst_v[:, :, h], keep[:, 0:T], adst_v[:, :, h],
                                        q_init[:, F + HEADS + h:F + HEADS + h + 1], ALU.mult, ALU.add))
            prime("gat_acc", 2 * HALF)
            run_v = run[:, :].rearrange("p (t r) -> p t r", r=ROW_R)
            st(v.memset(run[:, (BODY - 1) * ROW_R:BODY * ROW_R], 0.0))
            m_half = [att_m[:, k * (HALF + 1) * HEADS:(k + 1) * (HALF + 1) * HEADS].rearrange("p (t h) -> p t h", h=HEADS)
                      for k in range(2)]
            s_half = [att_s[:, k * HALF * HEADS:(k + 1) * HALF * HEADS].rearrange("p (t h) -> p t h", h=HEADS)
                      for k in range(2)]
            r_half, w_half = ([att_rw[:, (2 * k + c) * HALF * HEADS:(2 * k + c + 1) * HALF * HEADS]
                               .rearrange("p (t h) -> p t h", h=HEADS) for k in range(2)] for c in range(2))
            st(v.memset(m_half[0][:, 0, :], NEG))
            for k in range(2):
                stage_idx_of("gat", 0, k)
            def gat_body(i, last):
                for k in range(2):
                    at = bass.ds(i * BODY + k * HALF, HALF)
                    steps = [0]

                    def small_step(ins):
                        steps[0] += 1
                        ins.then_inc(s["gat_small"], 1)
                        dve.wait_ge(s["gat_small"], i * (2 * SMALL) + k * SMALL + steps[0])

                    S, M, R_, W_ = s_half[k], m_half[k], r_half[k], w_half[k]
                    g_v = G[:, k * HALF * ROW_H:(k + 1) * HALF * ROW_H].rearrange("p (t r) -> p t r", r=ROW_H)
                    dve.wait_ge(s[f"gat_gathered{k}"], i * (16 * HALF) + 16 * HALF)
                    if not last:
                        stage_idx_of("gat", i + 1, k)
                    small_step(tt(S, g_v[:, :, F:F + HEADS], adst_v[:, at, :], ALU.add))
                    small_step(stt(S, S, SLOPE, S, ALU.mult, ALU.max))
                    for h in range(HEADS):
                        small_step(v.tensor_tensor_scan(M[:, 1:HALF + 1, h], pen[:, at], S[:, :, h], M[:, 0:1, h],
                                                        ALU.add, ALU.max))
                    small_step(v.tensor_copy(m_half[1 - k][:, 0, :], M[:, HALF, :]))
                    small_step(tt(R_, M[:, 0:HALF, :], M[:, 1:HALF + 1, :], ALU.subtract))
                    small_step(tt(R_, R_, pen[:, at].unsqueeze(2).to_broadcast([P, HALF, HEADS]), ALU.add))
                    small_step(tt(W_, S, M[:, 1:HALF + 1, :], ALU.subtract))
                    wait(dve, f"gat_written{k}", i * 16)
                    small_step(v.tensor_copy(run_v[:, k * HALF:(k + 1) * HALF, HEADS * F + HEADS:ROW_R],
                                             M[:, 1:HALF + 1, :]))
                    dve.wait_ge(s["gat_exp"], i * 2 + k + 1)
                    before = (k * HALF - 1) % BODY
                    for h in range(HEADS):
                        small_step(v.tensor_tensor_scan(run_v[:, k * HALF:(k + 1) * HALF, HEADS * F + h],
                                                        R_[:, :, h], W_[:, :, h],
                                                        run_v[:, before:before + 1, HEADS * F + h],
                                                        ALU.mult, ALU.add))
                    assert steps[0] == SMALL
                    for j in range(HALF):
                        n = k * HALF + j
                        before = (n - 1) % BODY
                        dve.wait_ge(s["gat_weighted"], i * (2 * BODY) + 2 * n + 2)
                        dve.wait_ge(s["gat_acc"], i * (2 * BODY) + 2 * HALF + 2 * n)
                        for h in range(HEADS):
                            stt(run_v[:, n, h * F:(h + 1) * F], run_v[:, before, h * F:(h + 1) * F],
                                R_[:, j, h:h + 1], weighted[:, (n * HEADS + h) * F:(n * HEADS + h + 1) * F],
                                ALU.mult, ALU.add).then_inc(s["gat_acc"], 1)
                    dve.wait_ge(s["gat_acc"], i * (2 * BODY) + (k + 2) * 2 * HALF)
            bodies(dve, gat_body)

            tail = (BODY - 1) * ROW_R
            mm_w = [mask_w[:, h * P:(h + 1) * P] for h in range(HEADS)]
            for h in range(HEADS):
                at = tail + HEADS * F + HEADS + h
                if h:
                    dve.wait_ge(s["gat_mrow"], h)
                st(ts(tmp_a[:, :], ident[:, :], run[:, at:at + 1], None, ALU.mult), "gat_mrow_ready")
            dve.wait_ge(s["gat_mrow"], HEADS)
            st(ts(sel[:, 0:P], mask_qp[:, :], -NEG, NEG, ALU.mult, ALU.add))
            for h in range(HEADS):
                mc = carry_s[:, HEADS * F + HEADS + h:HEADS * F + HEADS + h + 1]
                st(tt(mm_w[h], banks[0][:, h * P:(h + 1) * P], sel[:, 0:P], ALU.add))
                st(v.tensor_reduce(mc, mm_w[h], AX.X, ALU.max))
                st(ts(mm_w[h], mm_w[h], mc, None, ALU.subtract), "gat_exp_ready2")
            for h in range(HEADS):
                dve.wait_ge(s["gat_exp2"], 1)
                st(tt(mm_w[h], mm_w[h], mask_qp[:, :], ALU.mult), "gat_wt_ready")
            dve.wait_ge(s["gat_wt_T"], HEADS)
            for h in range(HEADS):
                st(v.tensor_copy(mask_w[:, (2 + h) * P:(3 + h) * P], banks[1][:, h * P:(h + 1) * P]), "gat_wt_copied")
            dve.wait_ge(s["gat_carry"], 1)
            st(v.tensor_copy(carry_s[:, 0:HEADS * F], banks[2][:, 0:HEADS * F]))
            st(v.tensor_copy(carry_s[:, HEADS * F:HEADS * F + HEADS], banks[3][:, 0:HEADS]))
            st(v.memset(carry_s[:, HEADS * F + 4:HEADS * F + 5], 1.0), "gat_carry_copied")

            def select(b, name):
                st(ts(sel[:, (b % (2 * GROUP)) * P:(b % (2 * GROUP) + 1) * P], iota_f[:, :], d_rel[:, b:b + 1],
                      ends[:, 0:1], ALU.is_equal, ALU.mult), name)
            for g, (b0, b1_) in enumerate(GROUPS):
                if g >= 2:
                    dve.wait_ge(s["gat_tail"], g - 1)
                for b in range(b0, b1_):
                    select(b, "gat_sel")
            dve.wait_ge(s["gat_tail"], len(GROUPS))
            st(v.tensor_copy(carry5, banks[0][:, 0:5 * NB]))
            c5 = carry5.rearrange("p (b c) -> p b c", c=5)
            a4v = a4[:, :].rearrange("p (b c) -> p b c", c=4)

            def two(a):
                return a.rearrange("p (b h) -> p b h", h=HEADS)

            def heads_wide(a):
                return a.unsqueeze(2).to_broadcast([P, NB, HEADS])

            wr, wc, ws, dn, mx, ss = (two(a) for a in (wr2, wc2, ws2, dn2, mx2, ss2))
            dve.wait_ge(s["gat_rows"], NB * 16)
            st(tt(ss, a4v[:, :, 0:2], a4v[:, :, 2:4], ALU.add))
            st(stt(ss2, ss2, SLOPE, ss2, ALU.mult, ALU.max))
            st(ts(scr, has, -NEG, NEG, ALU.mult, ALU.add))
            st(tt(wr, R_v[:, :, HEADS * F + HEADS:ROW_R], heads_wide(scr), ALU.add))
            st(ts(scr, c5[:, :, 4], -NEG, NEG, ALU.mult, ALU.add))
            st(tt(wc, c5[:, :, 2:4], heads_wide(scr), ALU.add))
            st(tt(mx2, wr2, wc2, ALU.max))
            st(tt(mx2, mx2, ss2, ALU.max))
            st(tt(wr2, wr2, mx2, ALU.subtract))
            st(tt(wc2, wc2, mx2, ALU.subtract))
            st(tt(ws2, ss2, mx2, ALU.subtract), "gat_comb_ready")
            dve.wait_ge(s["gat_comb"], 1)
            st(tt(dn, wr, R_v[:, :, HEADS * F:HEADS * F + HEADS], ALU.mult))
            st(tt(mx, wc, c5[:, :, 0:2], ALU.mult))
            st(tt(dn2, dn2, mx2, ALU.add))
            st(tt(dn2, dn2, ws2, ALU.add))
            st(v.reciprocal(dn2, dn2))
            st(ts(dn2, dn2, 1.0 / HEADS, None, ALU.mult))
            for w_ in (wr2, wc2, ws2):
                st(tt(w_, w_, dn2, ALU.mult))
            for b in range(*PAIRS[0]):
                select(b, "gat_sel2")
            for g, (b0, b1_) in enumerate(PAIRS):
                if g + 1 < len(PAIRS):
                    for b in range(*PAIRS[g + 1]):
                        select(b, "gat_sel2")
                dve.wait_ge(s["gat_picked"], g + 1)
                for b in range(b0, b1_):
                    for h in range(HEADS):
                        row = arena[:, b * ROW_R + h * F:b * ROW_R + (h + 1) * F]
                        col = b * HEADS + h
                        st(ts(row, row, wr2[:, col:col + 1], None, ALU.mult))
                        st(stt(row, h_n[:, b * F:(b + 1) * F], ws2[:, col:col + 1], row, ALU.mult, ALU.add))
                        at = ((b - b0) * HEADS + h) * F
                        st(stt(row, banks[2 + g % 2][:, at:at + F], wc2[:, col:col + 1], row, ALU.mult, ALU.add),
                           "gat_merged" if h == HEADS - 1 else "vec_step")
            for g, (b0, b1_) in enumerate(PAIRS):
                dve.wait_ge(s["gat_lin"], g + 1)
                st(tt(t_v[:, b0:b1_, :], banks[6 + g % 2][:, 0:(b1_ - b0) * F].rearrange("p (b f) -> p b f", f=F),
                      rowwise(gatb_r[:, :], b1_ - b0), ALU.add), "gat_lin_used")
            layernorm(t_n3, t_n3, h_n3)
            gamma_beta_silu(t_n3, t_n[:, :])
            st(tt(x_n[:, :], x_n[:, :], t_n[:, :], ALU.add))

            layernorm(x_n3, h_n3, t_n3)
            st(ts(h_n[:, :], h_n[:, :], 0.0, None, ALU.max), "mlp_lin_ready")
            for g, (b0, b1_) in enumerate(PAIRS):
                dve.wait_ge(s["mlp_lin"], g + 1)
                pq = banks[6 + g % 2][:, 0:(b1_ - b0) * 2 * F].rearrange("p (b c f) -> p b c f", c=2, f=F)
                st(v.tensor_copy(t_v[:, b0:b1_, :], pq[:, :, 0, :]))
                st(v.tensor_copy(Rf_v[:, b0:b1_, :], pq[:, :, 1, :]), "mlp_lin_used")
            st(ts(t_n[:, (NB - 1) * F:], t_n[:, (NB - 1) * F:], real_node[:, 0:1], None, ALU.mult))
            st(ts(Rf[:, (NB - 1) * F:], Rf[:, (NB - 1) * F:], real_node[:, 0:1], None, ALU.mult), "mlp_ready")
            dve.wait_ge(s["q_scattered"], NB * 16)
            dve.wait_ge(s["mlp_tables_written"], 32)
            st(v.memset(valid[:, :], 1.0))
            st(v.memset(valid[:, ELAST:T], 0.0))
            for c in range(HALF):
                at = slice(c * (F // HALF), (c + 1) * (F // HALF))
                if c == 0:
                    dve.wait_ge(s["q_init_loaded"], 16)
                st(v.tensor_copy(q_cur[:, (BODY - 1) * F + at.start:(BODY - 1) * F + at.stop], q_init[:, at]), "q_acc")
            for k in range(2):
                stage_idx_of("mlp", 0, k)
                stage_keep_of(0, k)
            def q_chain(i, k):
                keep_ready(1, i, k)
                dve.wait_ge(s[f"q_loaded{k}"], i * 16 + 16)
                wait(dve, f"pre_made{k}", i * 2)
                for j in range(HALF):
                    n = k * HALF + j
                    before = (n - 1) % BODY
                    stt(q_cur[:, n * F:(n + 1) * F], q_cur[:, before * F:(before + 1) * F],
                        stage_keep[:, n:n + 1], q_load[:, n * F:(n + 1) * F],
                        ALU.mult, ALU.add).then_inc(s["q_acc"], 1)
                    dve.wait_ge(s["q_acc"], i * BODY + HALF + n + 1)

            def q_chain_and_stage(i, k, last):
                q_chain(i, k)
                if not last:
                    stage_keep_of(i + 1, k)

            q_chain_and_stage(0, 0, False)

            def mlp_body(i, last, next_last=False):
                for k in range(2):
                    if k == 0:
                        q_chain_and_stage(i, 1, last)
                    elif not last:
                        q_chain_and_stage(i + 1, 0, next_last)
                    if not last:
                        dve.wait_ge(s[f"mlp_gathered{k}"], i * (16 * HALF) + 16 * HALF)
                        stage_idx_of("mlp", i + 1, k)
                    for g in range(2):
                        dve.wait_ge(s[f"pre_copied{2 * k + g}"], i + 1)
                        n0 = k * HALF + g * GROUP
                        v.bn_stats(stats[:, bass.ds(i * 24 + (2 * k + g) * 6, 6)],
                                   pre_s[:, n0 * P:(n0 + GROUP) * P]).then_inc(s[f"pre_stats{2 * k + g}"], 1)
            mlp_body(0, False)
            with dve.Fori(1, NI - 2) as i:
                mlp_body(i, False)
            mlp_body(NI - 2, False, True)
            mlp_body(NI - 1, True)

            sv = stats.rearrange("p (g a c) -> p (g a) c", a=2, c=3)
            NS = 2 * (T // GROUP)
            s_cm = h_n[:, 0:NS]
            s_q = h_n[:, NS:2 * NS]

            def batch_norm(c0, o0, name):
                gcol, becol, bcol = (cols[:, c0 + c:c0 + c + 1] for c in range(3))
                mean, var, scale, shift, tmp = (bn[:, c:c + 1] for c in range(o0, o0 + 5))
                st(tt(s_cm, sv[:, :, 0], sv[:, :, 1], ALU.mult))
                st(v.tensor_reduce(mean, s_cm, AX.X, ALU.add))
                st(tt(s_q, s_cm, sv[:, :, 1], ALU.mult))
                st(tt(s_q, s_q, sv[:, :, 2], ALU.add))
                st(v.tensor_reduce(var, s_q, AX.X, ALU.add))
                st(ts(mean, mean, 1.0 / E, None, ALU.mult))
                st(tt(tmp, mean, mean, ALU.mult))
                st(ts(var, var, 1.0 / E, tmp, ALU.mult, ALU.subtract))
                st(ts(var, var, 0.0, BN_EPS, ALU.max, ALU.add), "bn_var")
                dve.wait_ge(s["bn_std"], count["bn_var"])
                st(v.reciprocal(var, var))
                st(tt(scale, var, gcol, ALU.mult))
                st(tt(mean, mean, bcol, ALU.add))
                st(tt(tmp, bcol, mean, ALU.subtract))
                st(ts(shift, tmp, scale, becol, ALU.mult, ALU.add), name)

            for b_ in range(4):
                dve.wait_ge(s[f"pre_stats{b_}"], NI)
            batch_norm(0, 0, "bn1_ready")
            def z_mask(i, k):
                dve.wait_ge(s[f"z_made{k}"], i + 1)
                zc = z_s[:, k * HALF * P:(k + 1) * HALF * P].rearrange("p (t e) -> p t e", e=P)[:, :, P - 1]
                tt(zc, zc, valid[:, bass.ds(i * BODY + k * HALF, HALF)], ALU.mult).then_inc(s[f"z_masked{k}"], 1)

            z_mask(0, 0)

            def h2_stats_body(i, last):
                for k in range(2):
                    if k == 0:
                        z_mask(i, 1)
                    elif not last:
                        z_mask(i + 1, 0)
                    for g in range(2):
                        dve.wait_ge(s[f"h2_made{k}"], i * 2 + g + 1)
                        v.bn_stats(stats[:, bass.ds(i * 24 + (2 * k + g) * 6, 6)],
                                   banks[2 * k + g][:, :]).then_inc(s[f"pre_stats{2 * k + g}"], 1)
            bodies(dve, h2_stats_body)
            for b_ in range(4):
                dve.wait_ge(s[f"pre_stats{b_}"], 2 * NI)
            batch_norm(3, 8, "bn2_ready")
            st(ts(tmp_a[:, :], ident[:, :], bn[:, 10:11], None, ALU.mult), "bn2_row")
            dve.wait_ge(s["bn2_row_done"], 1)
            st(tt(w2Ts[:, :], w2T[:, :], banks[4][:, 0:F], ALU.mult))
            st(ts(tmp_a[:, :], ident[:, :], bn[:, 11:12], None, ALU.mult), "bn2_row")
            dve.wait_ge(s["bn2_row_done"], 2)
            st(v.tensor_copy(tmp_a[:, :], banks[5][:, 0:F]))
            parts_b = ones_b[:, :]
            total = carry_s[:, 0:F]
            st(v.memset(total, 0.0))
            for c in range(3):
                st(v.tensor_copy(parts_b, tmp_a[:, :]))
                st(stt(total, parts_b, ident[:, c:c + 1], total, ALU.mult, ALU.add))
                st(tt(tmp_a[:, :], tmp_a[:, :], parts_b, ALU.subtract))
            st(v.memset(ones_b[:, :], 1.0))
            st(v.tensor_copy(shift_rows[:, :].rearrange("p (g f) -> p g f", f=F), rowwise(total, GROUP)),
               "w2s_ready")
            prime("mlp_acc")

            def u_ready(i, k, g):
                dve.wait_ge(s[f"u_made{2 * k + g}"], i + 1)

            for k in range(2):
                stage_keep_of(0, k)
            accumulate("mlp", 2, u_s, u_ready)
            dve.wait_ge(s["mlp_carry"], 1)
            st(v.tensor_copy(carry_s[:, 0:F], banks[0][:, 0:F]), "mlp_carry_copied")
            dve.wait_ge(s["mlp_rows"], NB * 16)
            pick("mlp")
            st(tt(x_n[:, :], x_n[:, :], Rf, ALU.add), "out_ready")

        @block.scalar
        def _(act):
            a = nc.scalar.activation
            count = {}

            def std(ap):
                count["std"] = count.get("std", 0) + 1
                act.wait_ge(s["var_ready"], count["std"])
                a(ap, ap, ACT.Sqrt).then_inc(s["std_ready"], 1)

            def sigmoid(src_):
                count["sig"] = count.get("sig", 0) + 1
                act.wait_ge(s["sig_ready"], count["sig"])
                a(sq_n, src_, ACT.Sigmoid).then_inc(s["sig_done"], 1)

            def wl(o, i_):
                act.dma_start(o, i_).then_inc(s["weights_loaded"], 16)
            wl(gcn_w_s[:, :], gcn_w)
            wl(gat_w_s[:, :], gat_w)
            wl(w1_s[:, :], W1)
            wl(w2_s[:, :], W2)
            wl(att_row[:, 0:2 * F], att_src.rearrange("h f -> (h f)").partition_broadcast(P))
            wl(att_row[:, 2 * F:4 * F], att_dst.rearrange("h f -> (h f)").partition_broadcast(P))
            for o, i_ in ((gcnb_r, gcn_b), (gatb_r, gat_b), (gamma_r, ln_gamma), (beta_r, ln_beta)):
                wl(o[:, :], i_.partition_broadcast(P))
            for c, i_ in enumerate((g1, be1, b1, g2, be2, b2)):
                wl(cols[:, c:c + 1], i_.rearrange("(p o) -> p o", o=1))

            act.wait_ge(s["w1_T"], 1)
            a(w1T[:, :], banks[2][:, 0:2 * F], ACT.Copy).then_inc(s["wT_copied"], 1)
            act.wait_ge(s["w2_T"], 1)
            a(w2T[:, :], banks[3][:, 0:F], ACT.Copy).then_inc(s["wT_copied"], 1)
            act.wait_ge(s["mask_T"], 2)
            a(mask_pq[:, :], banks[1][:, P:2 * P], ACT.Copy).then_inc(s["mask_copied"], 1)
            std(rs)
            std(rs)
            act.wait_ge(s["zero_made"], 1)
            act.dma_start(adst_edge.rearrange("(p t) h -> p (t h)", t=T), zeros).then_inc(s["filled"], 16)

            def fill(i, last):
                wait(act, "gcn_acc", i * BODY)
                act.dma_start(q_edge_pt[:, bass.ds(i * BODY, BODY), :],
                              zeros[:, 0:BODY * F].rearrange("p (t f) -> p t f", f=F)).then_inc(s["filled"], 16)
            bodies(act, fill)

            def copies(prefix, groups, parts=1):
                for g, (b0, b1_) in enumerate(groups):
                    act.wait_ge(s[prefix + "_T"], g + 1)
                    if g >= 2:
                        act.wait_ge(s[prefix + "_lin"], g - 1)
                    n = (b1_ - b0) * parts * P
                    a(stage_t[:, g % 2 * 512:g % 2 * 512 + n], banks[4 + g % 2][:, 0:n],
                      ACT.Copy).then_inc(s[prefix + "_T_copied"], 1)
            copies("gcn", GROUPS)
            std(rs)
            sigmoid(h_n[:, :])
            copies("att", GROUPS)
            def gat_act(i, last):
                for k in range(2):
                    rw = att_rw[:, 2 * k * HALF * HEADS:2 * (k + 1) * HALF * HEADS]
                    w_ = att_rw[:, (2 * k + 1) * HALF * HEADS:2 * (k + 1) * HALF * HEADS]
                    act.wait_ge(s["gat_small"], i * (2 * SMALL) + k * SMALL + SMALL_LOGS)
                    a(rw, rw, ACT.Exp).then_inc(s["gat_exp"], 1)
                    act.wait_ge(s["gat_exp"], i * 2 + k + 1)
                    wait(act, "gat_acc", i * (2 * BODY) + k * 2 * HALF)
                    for j in range(HALF):
                        n = k * HALF + j
                        for h in range(HEADS):
                            a(weighted[:, (n * HEADS + h) * F:(n * HEADS + h + 1) * F], G[:, n * ROW_H:n * ROW_H + F],
                              ACT.Copy, scale=w_[:, j * HEADS + h:j * HEADS + h + 1]).then_inc(s["gat_weighted"], 1)
            bodies(act, gat_act)
            act.wait_ge(s["gat_exp_ready2"], HEADS)
            a(mask_w[:, 0:HEADS * P], mask_w[:, 0:HEADS * P], ACT.Exp).then_inc(s["gat_exp2"], 1)
            act.wait_ge(s["gat_comb_ready"], 1)
            wrcs = small[:, 21 * NB:27 * NB]
            a(wrcs, wrcs, ACT.Exp).then_inc(s["gat_comb"], 1)
            copies("gat", PAIRS, HEADS)
            std(rs)
            sigmoid(t_n[:, :])
            std(rs)
            copies("mlp", PAIRS)
            act.wait_ge(s["q_scattered"], NB * 16)
            act.wait_ge(s["mlp_tables_written"], 32)
            def pre_out(i, last):
                for k in range(2):
                    wait(act, f"pre_written{k}", i * 16)
                    for g in range(2):
                        wait(act, f"pre_stats{2 * k + g}", i)
                        act.wait_ge(s[f"pre_made{k}"], i * 2 + g + 1)
                        n0 = k * HALF + g * GROUP
                        a(pre_s[:, n0 * P:(n0 + GROUP) * P], banks[2 * k + g][:, :],
                          ACT.Copy).then_inc(s[f"pre_copied{2 * k + g}"], 1)
                    for g in range(2):
                        act.wait_ge(s[f"pre_copied{2 * k + g}"], i + 1)
                    act.dma_start(pre_dram[i, :, k * HALF * P:(k + 1) * HALF * P],
                                  pre_s[:, k * HALF * P:(k + 1) * HALF * P]).then_inc(s[f"pre_written{k}"], 16)
            bodies(act, pre_out)
            for k in range(2):
                act.wait_ge(s[f"pre_written{k}"], NI * 16)
            act.wait_ge(s["bn_var"], 1)
            a(bn[:, 1:2], bn[:, 1:2], ACT.Sqrt).then_inc(s["bn_std"], 1)
            act.wait_ge(s["bn1_ready"], 1)

            def z_of(i, k, sweep):
                act.wait_ge(s[f"pre2_loaded{k}"], i * 16 + (sweep * NI + 1) * 16)
                wait(act, f"h2_made{k}", (i + sweep * NI) * 2)
                a(z_s[:, k * HALF * P:(k + 1) * HALF * P], G[:, k * HALF * P:(k + 1) * HALF * P],
                  ACT.Relu, bias=bn[:, 3:4], scale=bn[:, 2:3]).then_inc(s[f"z_made{k}"], 1)

            def z_body(i, last):
                for k in range(2):
                    z_of(i, k, 0)
            bodies(act, z_body)
            act.wait_ge(s["bn_var"], 2)
            a(bn[:, 9:10], bn[:, 9:10], ACT.Sqrt).then_inc(s["bn_std"], 1)
            act.wait_ge(s["w2s_ready"], 1)
            z_of(0, 0, 1)

            def u_body(i, last):
                for k in range(2):
                    if k == 0:
                        z_of(i, 1, 1)
                    elif not last:
                        z_of(i + 1, 0, 1)
                    wait(act, "mlp_acc", i * BODY + k * HALF)
                    for g in range(2):
                        act.wait_ge(s[f"h2_made{k}"], i * 2 + 2 * NI + g + 1)
                        n0 = k * HALF + g * GROUP
                        a(u_s[:, n0 * P:(n0 + GROUP) * P], banks[2 * k + g][:, :],
                          ACT.Relu).then_inc(s[f"u_made{2 * k + g}"], 1)
            bodies(act, u_body)


_INS = ["x", "src", "dst", "L0_gnn_gcn_w", "L0_gnn_gcn_b", "L0_gnn_gat_w", "L0_gnn_att_src", "L0_gnn_att_dst",
        "L0_gnn_gat_b", "L0_gnn_ln_gamma", "L0_gnn_ln_beta", "L1_gnn_W1", "L1_gnn_b1", "L1_gnn_g1", "L1_gnn_be1",
        "L1_gnn_W2", "L1_gnn_b2", "L1_gnn_g2", "L1_gnn_be2"]


def kernel(**inputs):
    import numpy as _np
    import concourse.bacc as _bacc
    from concourse import mybir as _mybir
    from concourse.bass_utils import run_bass_kernel_spmd as _run

    nc = _bacc.Bacc("TRN2", target_bir_lowering=False, num_devices=1)
    arrays, args = {}, []
    for name in _INS:
        a = _np.ascontiguousarray(inputs[name])
        arrays[f"in_{name}_dram"] = a
        args.append(nc.dram_tensor(f"in_{name}_dram", a.shape, _mybir.dt.from_np(a.dtype), kind="ExternalInput").ap())
    out = nc.dram_tensor("out_dram", arrays["in_x_dram"].shape, _mybir.dt.float32, kind="ExternalOutput").ap()
    gnn_kernel(nc, *args, out)
    r = _run(nc, [arrays], core_ids=[0])
    return r.results[0]["out_dram"]
```

```python
import concourse.bass as bass
from concourse import mybir
from contextlib import ExitStack

f32 = mybir.dt.float32
bf16 = mybir.dt.bfloat16
i32 = mybir.dt.int32
ALU = mybir.AluOpType
ACT = mybir.ActivationFunctionType
AX = mybir.AxisListType

P = 128
F = 128
HEADS = 2
HALF = 8
BODY = 2 * HALF
GROUP = 4
NEG = -1e30
LN_EPS = 1e-5
BN_EPS = 1e-5
SLOPE = 0.2
ROW_H = F + 2 * HEADS
ROW_R = HEADS * F + 2 * HEADS


def gnn_kernel(nc, x, src, dst, gcn_w, gcn_b, gat_w, att_src, att_dst, gat_b, ln_gamma, ln_beta,
               W1, b1, g1, be1, W2, b2, g2, be2, out):
    N = x.shape[0]
    E = src.shape[0]
    NB = -(-N // P)
    NP = NB * P
    PAD = NP - 1
    NLAST = N - (NB - 1) * P
    T = -(-E // (P * BODY)) * BODY
    NI = T // BODY
    ELAST = E - (P - 1) * T
    assert N < NP and 0 < ELAST < T
    GROUPS = [(b, min(b + GROUP, NB)) for b in range(0, NB, GROUP)]
    PAIRS = [(b, min(b + 2, NB)) for b in range(0, NB, 2)]
    LN_CUT = NB * 3 // 8
    PIECES = [(c * 3 * GROUP, (c + 1) * 3 * GROUP) for c in range(3)] + [(9 * GROUP, NB)]
    assert 9 * GROUP < NB
    PIECE_PAIRS = [b0 // 2 for b0, _ in PIECES]

    def piece_of(b):
        return sum(b >= end for _, end in PIECES)
    GAT_TABLE = 16 * (len(PIECES) + 1)
    SMALL = 11
    SMALL_LOGS = 8
    FREE = 4
    SUB = 16
    NSUB = T // SUB
    assert T % SUB == 0 and NSUB <= P and FREE == GROUP
    FAR = 1 << 20

    gcn_table = nc.dram_tensor("gcn_table", (NP, F), f32).ap()
    gat_table = nc.dram_tensor("gat_table", (NP, ROW_H), f32).ap()
    p_table = nc.dram_tensor("p_table", (NP, F), f32).ap()
    q_table = nc.dram_tensor("q_table", (NP, F), f32).ap()
    q_edge = nc.dram_tensor("q_edge", (P * T, F), f32).ap()
    adst_edge = nc.dram_tensor("adst_edge", (P * T, HEADS), f32).ap()
    gcn_run = nc.dram_tensor("gcn_run", (P * T, F), f32).ap()
    gat_run = nc.dram_tensor("gat_run", (P * T, ROW_R), f32).ap()
    mlp_run = nc.dram_tensor("mlp_run", (P * T, F), f32).ap()
    pre_dram = nc.dram_tensor("pre_dram", (NI, P, BODY * P), f32).ap()
    dst_rows = nc.dram_tensor("dst_rows", (P * NSUB, SUB), f32).ap()
    dst_samples = nc.dram_tensor("dst_samples", (P, NSUB), f32).ap()
    q_edge_pt = q_edge.rearrange("(p t) f -> p t f", t=T)
    gcn_run_pt = gcn_run.rearrange("(p t) f -> p t f", t=T)
    gat_run_pt = gat_run.rearrange("(p t) f -> p t f", t=T)
    mlp_run_pt = mlp_run.rearrange("(p t) f -> p t f", t=T)

    ctx = ExitStack()
    with ctx:
        def sb(name, shape, dt=f32):
            return ctx.enter_context(nc.sbuf_tensor(name, shape, dt))

        def sem(name):
            return ctx.enter_context(nc.semaphore(name))

        src_i = sb("src_i", [P, T], i32)
        keep = sb("keep", [P, T])
        pen = sb("pen", [P, T])
        valid = pen
        adst_e = sb("adst_e", [P, T * HEADS])
        adst_v = adst_e[:, :].rearrange("p (t h) -> p t h", h=HEADS)
        x_n = sb("x_n", [P, NB * F])
        h_n = sb("h_n", [P, NB * F])
        t_n = sb("t_n", [P, NB * F])
        arena = sb("arena", [P, NB * ROW_R])
        a4 = sb("a4", [P, NB * 2 * HEADS])
        small = sb("small", [P, 30 * NB])
        has, dinv, last_f, start_f = (small[:, k * NB:(k + 1) * NB] for k in range(4))
        mu, rs, deg, cum, tot, scr = (small[:, k * NB:(k + 1) * NB] for k in range(4, 10))
        d_rel = small[:, 10 * NB:11 * NB]
        cum1 = sb("cum1", [P, NB + 1])
        nbias = small[:, 11 * NB:12 * NB]
        ln_s = sb("ln_s", [P, 6 * NB])
        carry5 = small[:, 12 * NB:17 * NB]
        mx2, ss2 = (small[:, (17 + 2 * k) * NB:(19 + 2 * k) * NB] for k in range(2))
        wr2, wc2, ws2, dn2 = (small[:, (21 + 2 * k) * NB:(23 + 2 * k) * NB] for k in range(4))
        pos_i = sb("pos_i", [P, 2 * NB], i32)
        last_i, start_i = pos_i[:, 0:NB], pos_i[:, NB:2 * NB]
        ident = sb("ident", [P, P])
        shift_in = sb("shift_in", [P, P])
        shift_across = sb("shift_across", [P, P])
        low_strict = sb("low_strict", [P, P])
        ones = sb("ones", [P, P])
        iota_f = sb("iota_f", [P, P])
        iota_i = sb("iota_i", [P, P], i32)
        node_f = sb("node_f", [P, NB])
        gcn_w_s = sb("gcn_w_s", [P, F])
        gat_w_s = sb("gat_w_s", [P, HEADS * F])
        w1_s = sb("w1_s", [P, 2 * F])
        w1T = sb("w1T", [P, 2 * F])
        w2_s = sb("w2_s", [P, F])
        w2T = sb("w2T", [P, F])
        w2Ts = sb("w2Ts", [P, F])
        att_row = sb("att_row", [P, 4 * F])
        att_v = sb("att_v", [P, 4])
        gcnb_r = sb("gcnb_r", [P, F])
        gatb_r = sb("gatb_r", [P, F])
        gamma_r = sb("gamma_r", [P, F])
        beta_r = sb("beta_r", [P, F])
        cols = sb("cols", [P, 8])
        bn = sb("bn", [P, 16])
        dfirst, dlast, dprev, dnext = (sb(n, [P, 1]) for n in ("dfirst", "dlast", "dprev", "dnext"))
        edge_i = sb("edge_i", [P, 2], i32)
        dfirst_i = sb("dfirst_i", [P, 1], i32)
        ends = sb("ends", [P, 1])
        real_node = sb("real_node", [P, 1])
        mask_qp = sb("mask_qp", [P, P])
        mask_pq = sb("mask_pq", [P, P])
        tmp_a = sb("tmp_a", [P, P])
        mask_w = sb("mask_w", [P, 4 * P])
        shift_rows = sb("shift_rows", [P, GROUP * F], bf16)
        ones_b = sb("ones_b", [P, P], bf16)
        carry_s = sb("carry_s", [P, HEADS * F + 5])
        sel = sb("sel", [P, 2 * GROUP * P])
        stage_t = sb("stage_t", [P, 2 * 512])
        q_init = sb("q_init", [P, ROW_H])
        stage_idx = sb("stage_idx", [P, 2 * HALF], i32)
        stage_keep = sb("stage_keep", [P, 2 * HALF])
        att_s = sb("att_s", [P, 8 * HALF * HEADS])
        att_rw = sb("att_rw", [P, 4 * HALF * HEADS])
        att_m = sb("att_m", [P, 2 * (HALF + 1) * HEADS])
        run = sb("run", [P, BODY * ROW_R])
        banks = [ctx.enter_context(nc.psum_tensor(f"bank{k}", [P, 512], f32)) for k in range(8)]

        def cut(at, n):
            return arena[:, at:at + n]
        G = cut(0, BODY * ROW_H)
        RAW = BODY * ROW_H
        weighted = cut(RAW, BODY * HEADS * F)
        q_load = cut(RAW, BODY * F)
        q_cur = cut(RAW + BODY * F, BODY * F)
        pre_s = cut(RAW + 2 * BODY * F, BODY * P)
        z_s = cut(RAW, BODY * P)
        u_s = cut(RAW + BODY * F, BODY * P)
        assert RAW + 3 * BODY * F <= NB * ROW_R
        dst_i = cut(0, T + 1).bitcast(i32)
        dst_f = cut(T + 8, T + 1)
        samples = cut(2 * T + 16, NSUB)
        level_a = cut(0, NB * NSUB)
        level_b = cut(NB * NSUB, NB * SUB)
        assert NB * (NSUB + SUB) <= NB * F
        zeros = t_n[:, 0:2 * T]
        assert 2 * T <= NB * F
        stats = t_n[:, 0:(T // GROUP) * 6]

        x_v = x_n[:, :].rearrange("p (b f) -> p b f", f=F)
        h_v = h_n[:, :].rearrange("p (b f) -> p b f", f=F)
        t_v = t_n[:, :].rearrange("p (b f) -> p b f", f=F)
        R_v = arena[:, :].rearrange("p (b r) -> p b r", r=ROW_R)
        Rf = arena[:, 0:NB * F]
        Rf_v = Rf.rearrange("p (b f) -> p b f", f=F)
        sq_n = arena[:, NB * F:2 * NB * F]

        def rowwise(a, n):
            return a.unsqueeze(1).to_broadcast([P, n, a.shape[-1]])

        names = """const_made x_clear idx_clear x_loaded idx_loaded ends_loaded weights_loaded zero_made filled
        pool_step vec_step search_ready search_written level1 level2 keep_staged slots_free
        mask_row mask_T mask_copied w1_T w2_T wT_copied cum_ready cum_done var_ready std_ready
        gcn_ready gcn_table_written gcn_idx gcn_gathered0 gcn_gathered1 gcn_acc gcn_written0
        gcn_written1 node_rows0 node_rows1 node_rows2 node_rows3 gcn_corr gcn_summed gcn_carry
        gcn_carry_copied gcn_sel gcn_picked gcn_merged gcn_lin_ready gcn_T gcn_T_copied gcn_lin
        gcn_lin_used sig_ready sig_done ln_stats ln_half ln_ready ln_applied gamma_done
        silu_made x_added att_v_made att_T att_T_copied att_lin att_ready gat_table_written
        adst_scattered adst_loaded adst_init gat_idx gat_gathered0 gat_gathered1 gat_small
        gat_exp gat_weighted gat_acc gat_written0 gat_written1 gat_exp_ready2 gat_exp2
        gat_mrow_ready gat_mrow gat_wt_ready gat_wt_T gat_wt_copied gat_carry gat_carry_copied
        gat_sel gat_tail gat_comb_ready gat_comb gat_weights gat_scaled gat_own_added gat_picked
        gat_merged gat_T gat_T_copied gat_lin gat_lin_used mlp_lin_ready mlp_T mlp_T_copied
        mlp_lin mlp_lin_used mlp_ready mlp_tables_written q_scattered q_init_loaded mlp_idx
        mlp_gathered0 mlp_gathered1 q_loaded0 q_loaded1 q_acc pre_made0 pre_made1 pre_copied0
        pre_copied1 pre_copied2 pre_copied3 stats_made pre_written0 pre_written1 bn_var bn_std
        bn1_ready bn2_ready pre2_loaded0 pre2_loaded1 pre2_loaded2 pre2_loaded3 z_made z_masked
        h2_made bn2_row bn2_row_done w2s_ready u_made mlp_acc mlp_written0 mlp_written1
        mlp_written2 mlp_written3 mlp_corr mlp_carry mlp_carry_copied mlp_sel mlp_picked
        mlp_merged out_ready out_written""".split()
        s = {n: sem(n) for n in names}

        def step(eng, count, ins, name):
            count[name] = count.get(name, 0) + 1
            ins.then_inc(s[name], 1)
            eng.wait_ge(s[name], count[name])

        def wait(eng, name, value):
            if not (isinstance(value, int) and value <= 0):
                eng.wait_ge(s[name], value)

        def bodies(eng, body, unroll=1):
            first = 1 + (NI - 2) % unroll
            for i in range(first):
                body(i, False)
            with eng.Fori(first, NI - unroll, unroll) as i:
                for c in range(unroll):
                    body(i + c, False)
            body(NI - 1, True)

        block = ctx.enter_context(nc.Block())

        @block.sync
        def _(sp):
            sp.wait_ge(s["x_clear"], 1)
            sp.dma_start(x_v[:, 0:NB - 1, :],
                         x[0:(NB - 1) * P, :].rearrange("(b p) f -> p b f", p=P)).then_inc(s["x_loaded"], 16)
            sp.dma_start(x_v[0:NLAST, NB - 1, :], x[(NB - 1) * P:N, :]).then_inc(s["x_loaded"], 16)
            sp.wait_ge(s["idx_clear"], 3)
            for tile, edge in ((dst_i, dst), (src_i, src)):
                sp.dma_start(tile[0:P - 1, 0:T],
                             edge[0:(P - 1) * T].rearrange("(p t) -> p t", t=T)).then_inc(s["idx_loaded"], 16)
                sp.dma_start(tile[P - 1:P, 0:ELAST],
                             edge[(P - 1) * T:E].rearrange("(p t) -> p t", p=1)).then_inc(s["idx_loaded"], 16)
            sp.wait_ge(s["idx_loaded"], 64)
            sp.dma_start(edge_i[1:P, 0:1], dst_i[0:P - 1, T - 1:T]).then_inc(s["ends_loaded"], 16)
            sp.dma_start(edge_i[0:P - 1, 1:2], dst_i[1:P, 0:1]).then_inc(s["ends_loaded"], 16)
            sp.wait_ge(s["search_ready"], 2)
            sp.dma_start(dst_rows.rearrange("(p u) c -> p (u c)", p=P), dst_f[:, 1:T + 1]).then_inc(s["search_written"], 16)
            sp.dma_start(dst_samples, samples).then_inc(s["search_written"], 16)
            for c, (b0, b1_) in enumerate(PIECES):
                sp.wait_ge(s["gcn_ready"], c + 1)
                sp.dma_start(gcn_table.rearrange("(b p) f -> p b f", p=P)[:, b0:b1_, :],
                             h_v[:, b0:b1_, :]).then_inc(s["gcn_table_written"], 16)
            def gcn_out(i, last):
                for k in range(2):
                    sp.wait_ge(s["gcn_acc"], i * BODY + (k + 2) * HALF)
                    sp.dma_start(gcn_run_pt[:, bass.ds(i * BODY + k * HALF, HALF), :],
                                 run[:, k * HALF * F:(k + 1) * HALF * F].rearrange("p (t f) -> p t f", f=F)
                                 ).then_inc(s[f"gcn_written{k}"], 16)
            bodies(sp, gcn_out)
            t_rows = gat_table.rearrange("(b p) f -> p b f", p=P)
            for c, (b0, b1_) in enumerate(PIECES):
                sp.wait_ge(s["silu_made"], c + 1)
                sp.dma_start(t_rows[:, b0:b1_, 0:F], h_v[:, b0:b1_, :]).then_inc(s["gat_table_written"], 16)
            sp.wait_ge(s["att_ready"], 1)
            sp.dma_start(t_rows[:, :, F:ROW_H],
                         a4[:, :].rearrange("p (b c) -> p b c", c=4)).then_inc(s["gat_table_written"], 16)
            sp.wait_ge(s["adst_scattered"], NB * 16)
            sp.dma_start(adst_e[:, :], adst_edge.rearrange("(p t) h -> p (t h)", t=T)).then_inc(s["adst_loaded"], 16)
            def gat_out(i, last):
                for k in range(2):
                    sp.wait_ge(s["gat_acc"], i * (2 * BODY) + (k + 2) * 2 * HALF)
                    sp.dma_start(gat_run_pt[:, bass.ds(i * BODY + k * HALF, HALF), :],
                                 run[:, k * HALF * ROW_R:(k + 1) * HALF * ROW_R].rearrange("p (t f) -> p t f", f=ROW_R)
                                 ).then_inc(s[f"gat_written{k}"], 16)
            bodies(sp, gat_out)
            for table, rows in ((q_table, Rf_v), (p_table, t_v)):
                for b0, b1_ in PIECES:
                    if b1_ < NB:
                        sp.wait_ge(s["mlp_lin_used"], 2 * b1_ // 2)
                    else:
                        sp.wait_ge(s["mlp_ready"], 1)
                    sp.dma_start(table.rearrange("(b p) f -> p b f", p=P)[:, b0:b1_, :],
                                 rows[:, b0:b1_, :]).then_inc(s["mlp_tables_written"], 16)
            sp.wait_ge(s["q_scattered"], NB * 16)
            sp.wait_ge(s["mlp_tables_written"], 2 * len(PIECES) * 16)
            def q_in(i, last):
                for k in range(2):
                    wait(sp, "q_acc", i * BODY + k * HALF)
                    sp.dma_start(q_load[:, k * HALF * F:(k + 1) * HALF * F].rearrange("p (t f) -> p t f", f=F),
                                 q_edge_pt[:, bass.ds(i * BODY + k * HALF, HALF), :]).then_inc(s[f"q_loaded{k}"], 16)
            bodies(sp, q_in)
            def pre_in(i, q, sweep):
                wait(sp, "z_made", (i + sweep * NI) * 4 + q - 3)
                sp.dma_start(G[:, q * GROUP * P:(q + 1) * GROUP * P],
                             pre_dram[i, :, q * GROUP * P:(q + 1) * GROUP * P]).then_inc(s[f"pre2_loaded{q}"], 16)

            sp.wait_ge(s["bn1_ready"], 1)
            def second(i, last):
                for q in range(4):
                    pre_in(i, q, 0)
            bodies(sp, second, 2)

            for c in range(6):
                pre_in(c // 4, c % 4, 1)

            def third(i, left):
                for q in range(4):
                    if left > (q + 2) // 4:
                        pre_in(i + 1 + (q + 2) // 4, (q + 2) % 4, 1)
                    sp.wait_ge(s["mlp_acc"], i * BODY + (q + 1) * GROUP + HALF)
                    sp.dma_start(mlp_run_pt[:, bass.ds(i * BODY + q * GROUP, GROUP), :],
                                 run[:, q * GROUP * F:(q + 1) * GROUP * F].rearrange("p (t f) -> p t f", f=F)
                                 ).then_inc(s[f"mlp_written{q}"], 16)
            third(0, NI - 1)
            with sp.Fori(1, NI - 2) as i:
                third(i, 2)
            third(NI - 2, 1)
            third(NI - 1, 0)
            for c, (b0, b1_) in enumerate(PIECES):
                sp.wait_ge(s["out_ready"], c + 1)
                whole = min(b1_, NB - 1)
                sp.dma_start(out[b0 * P:whole * P, :].rearrange("(b p) f -> p b f", p=P),
                             x_v[:, b0:whole, :]).then_inc(s["out_written"], 16)
            sp.dma_start(out[(NB - 1) * P:N, :], x_v[0:NLAST, NB - 1, :]).then_inc(s["out_written"], 16)
            sp.wait_ge(s["out_written"], (len(PIECES) + 1) * 16)

        @block.gpsimd
        def _(pool):
            count = {}

            def st(ins):
                step(pool, count, ins, "pool_step")

            st(nc.gpsimd.iota(iota_i[:, :], pattern=[[1, P]], base=0, channel_multiplier=0))
            st(nc.gpsimd.tensor_copy(iota_f[:, :], iota_i[:, :]))
            st(nc.gpsimd.iota(iota_i[:, 0:NB], pattern=[[P, NB]], base=0, channel_multiplier=1))
            st(nc.gpsimd.tensor_copy(node_f[:, :], iota_i[:, 0:NB]))
            st(nc.gpsimd.memset(ones[:, :], 1.0))
            st(nc.gpsimd.memset(ident[:, :], 0.0))
            st(nc.gpsimd.affine_select(out=ident[:, :], in_=ident[:, :], compare_op=ALU.not_equal, fill=1.0,
                                       base=0, pattern=[[-1, P]], channel_multiplier=1))
            st(nc.gpsimd.memset(shift_in[:, :], 0.0))
            st(nc.gpsimd.affine_select(out=shift_in[:, :], in_=shift_in[:, :], compare_op=ALU.not_equal, fill=1.0,
                                       base=1, pattern=[[-1, P]], channel_multiplier=1))
            st(nc.gpsimd.memset(shift_across[:, :], 0.0))
            st(nc.gpsimd.affine_select(out=shift_across[:, :], in_=shift_across[:, :], compare_op=ALU.not_equal,
                                       fill=1.0, base=1 - P, pattern=[[-1, P]], channel_multiplier=1))
            st(nc.gpsimd.affine_select(out=low_strict[:, :], in_=ones[:, :], compare_op=ALU.is_gt, fill=0.0,
                                       base=0, pattern=[[-1, P]], channel_multiplier=1))
            nc.gpsimd.affine_select(out=real_node[:, :], in_=ones[:, 0:1], compare_op=ALU.is_gt, fill=0.0,
                                    base=NLAST, pattern=[[0, 1]], channel_multiplier=-1).then_inc(s["const_made"], 1)

            def hold():
                pool.sem_inc(s["slots_free"], 1)

            def gather(tile, table, idx):
                return pool.indirect_dma_start(out=tile, out_offset=None, in_=table,
                                               in_offset=bass.IndirectOffsetOnAxis(ap=idx, axis=0))

            def scatter(table, tile, idx):
                return pool.indirect_dma_start(out=table, out_offset=bass.IndirectOffsetOnAxis(ap=idx, axis=0),
                                               in_=tile, in_offset=None, bounds_check=P * T - 1, oob_is_err=False)

            def source_rows(table, row, prefix, rows_used):
                def body(i, last):
                    for k in range(2):
                        pool.wait_ge(s[prefix + "_idx"], i * 2 + k + 1)
                        for j in range(HALF):
                            n = k * HALF + j
                            if j % FREE == 0:
                                rows_used(i, n)
                                hold()
                            gather(G[:, n * row:(n + 1) * row], table, stage_idx[:, n:n + 1]
                                   ).then_inc(s[f"{prefix}_gathered{k}"], 16)
                bodies(pool, body)

            pool.wait_ge(s["search_written"], 32)
            for level, table, rows, n in (("level1", dst_samples, level_a, NSUB), ("level2", dst_rows, level_b, SUB)):
                for c, (b0, b1_) in enumerate(PIECES):
                    pool.wait_ge(s[level], c + 1)
                    for b in range(b0, b1_):
                        gather(rows[:, b * n:(b + 1) * n], table, last_i[:, b:b + 1]).then_inc(s[f"node_rows{c}"], 16)

            pool.wait_ge(s["gcn_table_written"], len(PIECES) * 16)
            source_rows(gcn_table, F, "gcn", lambda i, n: wait(pool, "gcn_acc", i * BODY + n - HALF + FREE))
            for k in range(2):
                pool.wait_ge(s[f"gcn_written{k}"], NI * 16)
            for b in range(NB):
                gather(Rf[:, b * F:(b + 1) * F], gcn_run, last_i[:, b:b + 1]
                       ).then_inc(s[f"node_rows{piece_of(b)}"], 16)
            pool.wait_ge(s["filled"], (NI + 1) * 16)
            pool.wait_ge(s["att_ready"], 1)
            for b in range(NB):
                scatter(adst_edge, a4[:, 4 * b + HEADS:4 * b + 2 * HEADS], start_i[:, b:b + 1]
                        ).then_inc(s["adst_scattered"], 16)
            pool.wait_ge(s["gat_table_written"], GAT_TABLE)
            gather(q_init[:, :], gat_table, dfirst_i[:, 0:1]).then_inc(s["adst_init"], 16)
            source_rows(gat_table, ROW_H, "gat",
                        lambda i, n: wait(pool, "gat_weighted", i * (2 * BODY) + 2 * (n - BODY + FREE)))
            for k in range(2):
                pool.wait_ge(s[f"gat_written{k}"], NI * 16)
            for b in range(NB):
                gather(arena[:, b * ROW_R:(b + 1) * ROW_R], gat_run, last_i[:, b:b + 1]
                       ).then_inc(s[f"node_rows{piece_of(b)}"], 16)
            for b in range(NB):
                if b == NB - 1:
                    pool.wait_ge(s["mlp_ready"], 1)
                elif b % 2 == 0:
                    pool.wait_ge(s["mlp_lin_used"], b + 2)
                scatter(q_edge, Rf[:, b * F:(b + 1) * F], start_i[:, b:b + 1]).then_inc(s["q_scattered"], 16)
            pool.wait_ge(s["mlp_tables_written"], 2 * len(PIECES) * 16)
            gather(q_init[:, 0:F], q_table, dfirst_i[:, 0:1]).then_inc(s["q_init_loaded"], 16)
            pool.wait_ge(s["q_scattered"], NB * 16)
            source_rows(p_table, F, "mlp",
                        lambda i, n: wait(pool, f"pre_made{n // HALF}", i * 2 - 1 + n % HALF // GROUP))
            for q in range(4):
                pool.wait_ge(s[f"mlp_written{q}"], NI * 16)
            for b in range(NB):
                gather(Rf[:, b * F:(b + 1) * F], mlp_run, last_i[:, b:b + 1]
                       ).then_inc(s[f"node_rows{piece_of(b)}"], 16)

        @block.tensor
        def _(pe):
            mm = nc.tensor.matmul

            def transpose(o, a):
                return mm(o, a, ident[:, :], start=True, stop=True)

            pe.wait_ge(s["const_made"], 1)
            pe.wait_ge(s["weights_loaded"], 16 * 16)
            for c in range(2):
                last = transpose(banks[2][:, c * F:(c + 1) * F], w1_s[:, c * F:(c + 1) * F])
            last.then_inc(s["w1_T"], 1)
            transpose(banks[3][:, 0:F], w2_s[:, :]).then_inc(s["w2_T"], 1)
            pe.wait_ge(s["mask_row"], 1)
            mm(banks[1][:, 0:P], ones[:, :], tmp_a[:, :], start=True, stop=True).then_inc(s["mask_T"], 1)
            pe.wait_ge(s["mask_row"], 2)
            transpose(banks[1][:, P:2 * P], mask_qp[:, :]).then_inc(s["mask_T"], 1)
            pe.wait_ge(s["mask_row"], 3)
            mm(banks[0][:, 0:P], ones[:, :], tmp_a[:, :], start=True, stop=True).then_inc(s["mask_T"], 1)
            pe.wait_ge(s["cum_ready"], 1)
            mm(banks[5][:, 0:NB], shift_in[:, :], cum1[:, 1:NB + 1], start=True, stop=False)
            mm(banks[5][:, 0:NB], shift_across[:, :], cum1[:, 0:NB], start=False, stop=True).then_inc(s["cum_done"], 1)

            pe.wait_ge(s["gcn_acc"], HALF + T)
            mm(banks[0][:, 0:F], mask_pq[:, :], run[:, (BODY - 1) * F:BODY * F],
               start=True, stop=True).then_inc(s["gcn_carry"], 1)
            pe.wait_ge(s["gcn_carry_copied"], 1)

            def pick(prefix):
                for g, (b0, b1_) in enumerate(GROUPS):
                    pe.wait_ge(s[prefix + "_sel"], b1_)
                    if g >= 2:
                        pe.wait_ge(s[prefix + "_corr"], g - 1)
                    for b in range(b0, b1_):
                        last = mm(banks[2 + g % 2][:, (b - b0) * F:(b - b0 + 1) * F],
                                  sel[:, (b % (2 * GROUP)) * P:(b % (2 * GROUP) + 1) * P],
                                  carry_s[:, 0:F], start=True, stop=True)
                    last.then_inc(s[prefix + "_picked"], 1)
            pick("gcn")

            def linear(prefix, source, w, n_out, groups, parts=1, ahead=None, uses=1):
                width = GROUP // parts
                for g in range(len(groups) + 1):
                    if g < len(groups):
                        b0, b1_ = groups[g]
                        if ahead:
                            ahead(g)
                        if g >= 2:
                            pe.wait_ge(s[prefix + "_T_copied"], g - 1)
                        for b in range(b0, b1_):
                            for c in range(parts):
                                at = (b - b0) * parts + c
                                last = transpose(banks[4 + g % 2][:, at * P:(at + 1) * P], source(b, c))
                        last.then_inc(s[prefix + "_T"], 1)
                    if g >= 1:
                        b0, b1_ = groups[g - 1]
                        pe.wait_ge(s[prefix + "_T_copied"], g)
                        if g >= 3:
                            pe.wait_ge(s[prefix + "_lin_used"], (g - 2) * uses)
                        for b in range(b0, b1_):
                            for c in range(parts):
                                at = (b - b0) * parts + c
                                o = banks[6 + (g - 1) % 2][:, (b - b0) * n_out:(b - b0 + 1) * n_out]
                                last = mm(o, stage_t[:, (g - 1) % 2 * 512 + at * P:(g - 1) % 2 * 512 + (at + 1) * P],
                                          w[:, c * n_out:(c + 1) * n_out], start=(c == 0), stop=(c == parts - 1))
                        last.then_inc(s[prefix + "_lin"], 1)

            linear("gcn", lambda b, c: Rf[:, b * F:(b + 1) * F], gcn_w_s, F, GROUPS,
                   ahead=lambda g: pe.wait_ge(s["gcn_lin_ready"], 1 + piece_of(GROUPS[g][0])))
            pe.wait_ge(s["att_v_made"], 1)
            for g in range(len(GROUPS) + 1):
                if g < len(GROUPS):
                    b0, b1_ = GROUPS[g]
                    pe.wait_ge(s["silu_made"], 1 + piece_of(b0))
                    if g >= 2:
                        pe.wait_ge(s["att_T_copied"], g - 1)
                    for b in range(b0, b1_):
                        last = transpose(banks[4 + g % 2][:, (b - b0) * P:(b - b0 + 1) * P],
                                         h_n[:, b * F:(b + 1) * F])
                    last.then_inc(s["att_T"], 1)
                if g >= 1:
                    b0, b1_ = GROUPS[g - 1]
                    pe.wait_ge(s["att_T_copied"], g)
                    for b in range(b0, b1_):
                        at = (g - 1) % 2 * 512 + (b - b0) * P
                        last = mm(banks[6][:, b * 4:(b + 1) * 4], stage_t[:, at:at + P], att_v[:, :],
                                  start=True, stop=True)
                    last.then_inc(s["att_lin"], 1)

            pe.wait_ge(s["gat_acc"], 2 * (HALF + T))
            tail = (BODY - 1) * ROW_R
            for c in range(HEADS):
                pe.wait_ge(s["gat_mrow_ready"], c + 1)
                mm(banks[0][:, c * P:(c + 1) * P], ones[:, :], tmp_a[:, :],
                   start=True, stop=True).then_inc(s["gat_mrow"], 1)
            for c in range(HEADS):
                pe.wait_ge(s["gat_wt_ready"], c + 1)
                transpose(banks[1][:, c * P:(c + 1) * P], mask_w[:, c * P:(c + 1) * P]).then_inc(s["gat_wt_T"], 1)
            pe.wait_ge(s["gat_wt_copied"], HEADS)
            for c in range(HEADS):
                wt = mask_w[:, (2 + c) * P:(3 + c) * P]
                mm(banks[2][:, c * F:(c + 1) * F], wt, run[:, tail + c * F:tail + (c + 1) * F], start=True, stop=True)
                last = mm(banks[3][:, c:c + 1], wt, run[:, tail + HEADS * F + c:tail + HEADS * F + c + 1],
                          start=True, stop=True)
            last.then_inc(s["gat_carry"], 1)
            pe.wait_ge(s["gat_carry_copied"], 1)
            for g, (b0, b1_) in enumerate(GROUPS):
                pe.wait_ge(s["gat_sel"], b1_)
                for b in range(b0, b1_):
                    last = mm(banks[0][:, b * 5:(b + 1) * 5], t_n[:, b * P:(b + 1) * P],
                              carry_s[:, HEADS * F:HEADS * F + 5], start=True, stop=True)
                last.then_inc(s["gat_tail"], 1)
            def gat_pick(g):
                b0, b1_ = PAIRS[g]
                if g >= 2:
                    pe.wait_ge(s["gat_merged"], PAIRS[g - 2][1])
                for b in range(b0, b1_):
                    last = mm(banks[2 + g % 2][:, (b - b0) * HEADS * F:(b - b0 + 1) * HEADS * F],
                              t_n[:, b * P:(b + 1) * P], carry_s[:, 0:HEADS * F], start=True, stop=True)
                last.then_inc(s["gat_picked"], 1)

            def gat_ahead(g):
                pe.wait_ge(s["gat_merged"], PAIRS[g][1])
                if g + 2 < len(PAIRS):
                    gat_pick(g + 2)
            gat_pick(0)
            gat_pick(1)
            linear("gat", lambda b, c: arena[:, b * ROW_R + c * F:b * ROW_R + (c + 1) * F], gat_w_s, F, PAIRS, HEADS,
                   gat_ahead)
            pe.wait_ge(s["mlp_lin_ready"], 1)
            linear("mlp", lambda b, c: h_n[:, b * F:(b + 1) * F], w1T, 2 * F, PAIRS, uses=2)

            def pre_body(i, last):
                for k in range(2):
                    pe.wait_ge(s[f"mlp_gathered{k}"], i * (16 * HALF) + 16 * HALF)
                    for g in range(2):
                        n0 = k * HALF + g * GROUP
                        pe.wait_ge(s["q_acc"], i * BODY + n0 + GROUP + HALF)
                        bank = banks[2 * k + g]
                        wait(pe, f"pre_copied{2 * k + g}", i)
                        for j in range(GROUP):
                            n = n0 + j
                            mm(bank[:, j * P:(j + 1) * P], G[:, n * F:(n + 1) * F], ident[:, :],
                               start=True, stop=False)
                            o = mm(bank[:, j * P:(j + 1) * P], q_cur[:, n * F:(n + 1) * F], ident[:, :],
                                      start=False, stop=True)
                        o.then_inc(s[f"pre_made{k}"], 1)
            bodies(pe, pre_body)
            def h2_body(i, last):
                for q in range(4):
                    pe.wait_ge(s["z_masked"], i * 4 + q + 1)
                    pe.wait_ge(s["stats_made"], (i + NI) * 4 + q - 3)
                    mm(banks[q][:, :], w2T[:, :], z_s[:, q * GROUP * P:(q + 1) * GROUP * P],
                       start=True, stop=True).then_inc(s["h2_made"], 1)
            bodies(pe, h2_body, 2)
            for c in range(2):
                pe.wait_ge(s["bn2_row"], c + 1)
                mm(banks[4 + c][:, 0:F], ones[:, :], tmp_a[:, :], start=True, stop=True).then_inc(s["bn2_row_done"], 1)
            pe.wait_ge(s["w2s_ready"], 1)
            def h3_body(i, last):
                for q in range(4):
                    pe.wait_ge(s["z_made"], (i + NI) * 4 + q + 1)
                    wait(pe, "u_made", i * 4 + q - 3)
                    mm(banks[q][:, :], ones_b[:, :], shift_rows[:, :], start=True, stop=False)
                    for j in range(GROUP):
                        n = q * GROUP + j
                        m = mm(banks[q][:, j * F:(j + 1) * F], z_s[:, n * P:(n + 1) * P], w2Ts[:, :],
                               start=False, stop=(j == GROUP - 1))
                    m.then_inc(s["h2_made"], 1)
            bodies(pe, h3_body, 2)
            pe.wait_ge(s["mlp_acc"], HALF + T)
            mm(banks[0][:, 0:F], mask_pq[:, :], run[:, (BODY - 1) * F:BODY * F],
               start=True, stop=True).then_inc(s["mlp_carry"], 1)
            pe.wait_ge(s["mlp_carry_copied"], 1)
            pick("mlp")

        @block.vector
        def _(dve):
            count = {}
            v = nc.vector

            def st(ins, name="vec_step"):
                step(dve, count, ins, name)

            tt, ts, stt = v.tensor_tensor, v.tensor_scalar, v.scalar_tensor_tensor
            x_n3, h_n3, t_n3, sq3 = (a.rearrange("p (b f) -> p b f", f=F) for a in (x_n[:, :], h_n[:, :], t_n[:, :], sq_n))

            def ln_stats_of(src_, b0, b1_):
                for b in range(b0, b1_):
                    v.bn_stats(ln_s[:, 6 * b:6 * b + 6], src_[:, b, :]).then_inc(s["ln_stats"], 1)

            def layernorm(src_, dst_, relu=False, tail=0):
                count["ln"] = count.get("ln", 0) + 1
                ln_stats_of(src_, tail, NB)
                dve.wait_ge(s["ln_stats"], NB * count["ln"])
                lv = ln_s[:, :].rearrange("p (b c) -> p b c", c=6)
                st(tt(mu, lv[:, :, 1], lv[:, :, 4], ALU.add))
                st(ts(mu, mu, 0.5, None, ALU.mult))
                st(tt(scr, lv[:, :, 1], mu, ALU.subtract))
                st(tt(scr, scr, scr, ALU.mult))
                st(tt(rs, lv[:, :, 2], lv[:, :, 5], ALU.add))
                st(stt(rs, scr, float(F), rs, ALU.mult, ALU.add))
                st(ts(rs, rs, 1.0 / F, LN_EPS, ALU.mult, ALU.add), "var_ready")
                dve.wait_ge(s["std_ready"], count["var_ready"])
                st(v.reciprocal(rs, rs))
                st(stt(nbias, mu, -1.0, rs, ALU.mult, ALU.mult), "ln_ready")
                for b in range(LN_CUT, NB):
                    ts(dst_[:, b, :], src_[:, b, :], mu[:, b:b + 1], rs[:, b:b + 1],
                       ALU.subtract, ALU.mult).then_inc(s["ln_half"], 1)
                dve.wait_ge(s["ln_half"], (NB - LN_CUT) * count["ln"])
                if relu:
                    st(ts(dst_[:, LN_CUT:NB, :], dst_[:, LN_CUT:NB, :], 0.0, None, ALU.max))
                dve.wait_ge(s["ln_applied"], LN_CUT * count["ln"])

            def gamma_beta_silu(a3):
                count["silu"] = count.get("silu", 0) + 1
                base = len(PIECES) * (count["silu"] - 1)
                for b0, b1_ in PIECES:
                    tt(a3[:, b0:b1_, :], a3[:, b0:b1_, :], rowwise(gamma_r[:, :], b1_ - b0),
                       ALU.mult).then_inc(s["gamma_done"], 1)
                for c, (b0, b1_) in enumerate(PIECES):
                    dve.wait_ge(s["gamma_done"], base + c + 1)
                    tt(a3[:, b0:b1_, :], a3[:, b0:b1_, :], rowwise(beta_r[:, :], b1_ - b0),
                       ALU.add).then_inc(s["sig_ready"], 1)
                for c, (b0, b1_) in enumerate(PIECES):
                    dve.wait_ge(s["sig_done"], base + c + 1)
                    dve.wait_ge(s["sig_ready"], base + c + 1)
                    tt(a3[:, b0:b1_, :], a3[:, b0:b1_, :], sq3[:, b0:b1_, :], ALU.mult).then_inc(s["silu_made"], 1)
                dve.wait_ge(s["silu_made"], base + len(PIECES))

            st(v.memset(x_n[:, (NB - 1) * F:NB * F], 0.0), "x_clear")
            st(v.memset(dst_i, PAD), "idx_clear")
            st(v.memset(src_i[:, :], PAD), "idx_clear")
            st(v.memset(edge_i[:, :], -1), "idx_clear")
            dve.wait_ge(s["idx_loaded"], 64)
            dve.wait_ge(s["ends_loaded"], 32)
            st(v.tensor_copy(dst_f[:, 1:T + 1], dst_i[:, 0:T]))
            st(v.tensor_copy(dst_f[:, 0:1], edge_i[:, 0:1]))
            st(v.tensor_copy(dnext[:, :], edge_i[:, 1:2]))
            st(v.tensor_copy(dfirst[:, :], dst_f[:, 1:2]))
            st(v.tensor_copy(dfirst_i[:, :], dst_i[:, 0:1]))
            st(v.tensor_copy(samples, dst_f[:, 1:T + 1].rearrange("p (u c) -> p u c", c=SUB)[:, :, 0]), "search_ready")
            dve.wait_ge(s["const_made"], 1)
            st(v.memset(ones_b[:, :], 1.0), "search_ready")
            st(tt(keep[:, 0:T], dst_f[:, 1:T + 1], dst_f[:, 0:T], ALU.is_equal))
            st(ts(pen[:, :], keep[:, 0:T], -NEG, NEG, ALU.mult, ALU.add))
            st(tt(ends[:, :], dfirst[:, :], dnext[:, :], ALU.not_equal))
            st(ts(d_rel, iota_f[:, 0:NB], float(-P), dfirst[:, 0:1], ALU.mult, ALU.add))
            st(ts(tmp_a[:, :], ident[:, :], dst_f[:, T:T + 1], None, ALU.mult), "mask_row")
            dve.wait_ge(s["mask_T"], 1)
            st(stt(mask_qp[:, :], banks[1][:, 0:P], dfirst[:, 0:1], low_strict[:, :], ALU.is_equal, ALU.mult),
               "mask_row")
            st(ts(tmp_a[:, :], ident[:, :], dfirst[:, 0:1], None, ALU.mult), "mask_row")

            def count_upto(out_, table3, n, b0, b1_):
                hits = t_n[:, b0 * n:b1_ * n].rearrange("p (b c) -> p b c", c=n)
                st(tt(hits, node_f[:, b0:b1_].unsqueeze(2).to_broadcast([P, b1_ - b0, n]), table3, ALU.is_ge))
                st(v.tensor_reduce(out_, hits, AX.X, ALU.add))

            dve.wait_ge(s["mask_T"], 3)
            for b0, b1_ in PIECES:
                at = slice(b0, b1_)
                count_upto(cum[:, at], banks[0][:, 0:P].unsqueeze(1).to_broadcast([P, b1_ - b0, P]), P, b0, b1_)
                st(ts(tot[:, at], cum[:, at], -1.0, 0.0, ALU.add, ALU.max))
                st(v.tensor_copy(last_i[:, at], tot[:, at]), "level1")
            dve.wait_ge(s["x_loaded"], 32)
            layernorm(x_n3, h_n3, relu=True)
            for c, (b0, b1_) in enumerate(PIECES):
                at = slice(b0, b1_)
                dve.wait_ge(s[f"node_rows{c}"], (b1_ - b0) * 16)
                count_upto(cum[:, at], level_a.rearrange("p (b c) -> p b c", c=NSUB)[:, at, :], NSUB, b0, b1_)
                st(ts(cum[:, at], cum[:, at], -1.0, 0.0, ALU.add, ALU.max))
                st(stt(tot[:, at], tot[:, at], float(NSUB), cum[:, at], ALU.mult, ALU.add))
                st(v.tensor_copy(last_i[:, at], tot[:, at]), "level2")
            for c, (b0, b1_) in enumerate(PIECES):
                dve.wait_ge(s[f"node_rows{c}"], (b1_ - b0) * 16 * 2)
                count_upto(cum[:, b0:b1_], level_b.rearrange("p (b c) -> p b c", c=SUB)[:, b0:b1_, :], SUB, b0, b1_)
            st(v.memset(cum1[:, 0:1], 0.0))
            st(stt(cum1[:, 1:NB + 1], tot, float(SUB), cum, ALU.mult, ALU.add), "cum_ready")
            dve.wait_ge(s["cum_done"], 1)
            st(v.tensor_copy(start_f, banks[5][:, 0:NB]))
            st(tt(deg, cum1[:, 1:NB + 1], start_f, ALU.subtract))
            st(ts(has, deg, 0.5, None, ALU.is_gt))
            st(ts(rs, deg, 1.0, None, ALU.add), "var_ready")
            dve.wait_ge(s["std_ready"], count["var_ready"])
            st(v.reciprocal(dinv, rs))
            st(ts(last_f, cum1[:, 1:NB + 1], -1.0, 0.0, ALU.add, ALU.max))
            st(v.tensor_copy(last_i, last_f))
            st(ts(scr, has, float(-FAR), float(FAR), ALU.mult, ALU.add))
            st(tt(start_f, start_f, scr, ALU.add))
            st(v.tensor_copy(start_i, start_f))

            for b0, b1_ in PIECES:
                tt(h_n3[:, b0:b1_, :], h_n3[:, b0:b1_, :], dinv[:, b0:b1_].unsqueeze(2).to_broadcast([P, b1_ - b0, F]),
                   ALU.mult).then_inc(s["gcn_ready"], 1)
            dve.wait_ge(s["gcn_ready"], len(PIECES))
            st(v.memset(zeros, 0.0), "zero_made")

            def stage_idx_of(prefix, i, k):
                v.tensor_copy(stage_idx[:, k * HALF:(k + 1) * HALF],
                              src_i[:, bass.ds(i * BODY + k * HALF, HALF)]).then_inc(s[prefix + "_idx"], 1)

            def stage_keep_of(i, k):
                v.tensor_copy(stage_keep[:, k * HALF:(k + 1) * HALF],
                              keep[:, bass.ds(i * BODY + k * HALF, HALF)]).then_inc(s["keep_staged"], 1)

            def keep_col(n):
                return stage_keep[:, n:n + 1]

            def keep_ready(sweep, i, k):
                dve.wait_ge(s["keep_staged"], (i + sweep * NI) * 2 + k + 1)

            def prime(acc, names_=HALF):
                for c in range(names_):
                    st(v.memset(run[:, (BODY - 1) * F + c * (F // names_):(BODY - 1) * F + (c + 1) * (F // names_)], 0.0), acc)

            def chain(prefix, i, n0, n_tiles, rows, between=None):
                for n in range(n0, n0 + n_tiles):
                    before = (n - 1) % BODY
                    stt(run[:, n * F:(n + 1) * F], run[:, before * F:(before + 1) * F],
                        keep_col(n), rows[:, n * F:(n + 1) * F], ALU.mult, ALU.add).then_inc(s[prefix + "_acc"], 1)
                    if n == n0 and between:
                        between()
                    dve.wait_ge(s[prefix + "_acc"], i * BODY + HALF + n + 1)

            def gcn_sums(i, last):
                for k in range(2):
                    dve.wait_ge(s[f"gcn_gathered{k}"], i * (16 * HALF) + 16 * HALF)
                    if not last:
                        stage_idx_of("gcn", i + 1, k)
                    keep_ready(0, i, k)
                    wait(dve, f"gcn_written{k}", i * 16)
                    chain("gcn", i, k * HALF, HALF, G)
                    if not last:
                        stage_keep_of(i + 1, k)

            prime("gcn_acc")
            for k in range(2):
                stage_idx_of("gcn", 0, k)
                stage_keep_of(0, k)
            bodies(dve, gcn_sums)

            for c in range(2):
                for h in range(HEADS):
                    st(tt(tmp_a[:, :], gat_w_s[:, h * F:(h + 1) * F],
                          att_row[:, (c * HEADS + h) * F:(c * HEADS + h + 1) * F], ALU.mult))
                    st(v.tensor_reduce(att_v[:, c * HEADS + h:c * HEADS + h + 1], tmp_a[:, :], AX.X, ALU.add))
            st(v.memset(scr, 0.0), "att_v_made")

            def pick(prefix):
                def select(b):
                    ts(sel[:, (b % (2 * GROUP)) * P:(b % (2 * GROUP) + 1) * P], iota_f[:, :], d_rel[:, b:b + 1],
                       ends[:, 0:1], ALU.is_equal, ALU.mult).then_inc(s[prefix + "_sel"], 1)
                for b in range(*GROUPS[0]):
                    select(b)
                for g, (b0, b1_) in enumerate(GROUPS):
                    if g + 1 < len(GROUPS):
                        if g >= 1:
                            dve.wait_ge(s[prefix + "_picked"], g)
                        for b in range(*GROUPS[g + 1]):
                            select(b)
                    dve.wait_ge(s[prefix + "_picked"], g + 1)
                    v.tensor_copy(t_n[:, b0 * F:b1_ * F],
                                  banks[2 + g % 2][:, 0:(b1_ - b0) * F]).then_inc(s[prefix + "_corr"], 1)
                dve.wait_ge(s[prefix + "_corr"], len(GROUPS))

            def merge_piece(prefix, c):
                b0, b1_ = PIECES[c]
                dve.wait_ge(s[f"node_rows{c}"], (b1_ - b0) * 16 * (3 if prefix == "gcn" else 5))
                for b in range(b0, b1_):
                    stt(Rf[:, b * F:(b + 1) * F], Rf[:, b * F:(b + 1) * F], has[:, b:b + 1],
                        t_n[:, b * F:(b + 1) * F], ALU.mult, ALU.add).then_inc(s[prefix + "_merged"], 1)
                dve.wait_ge(s[prefix + "_merged"], b1_)

            dve.wait_ge(s["filled"], (NI + 1) * 16)
            dve.wait_ge(s["gcn_carry"], 1)
            st(v.tensor_copy(carry_s[:, 0:F], banks[0][:, 0:F]), "gcn_carry_copied")
            pick("gcn")
            lin_groups = [[g for g, (b0, _) in enumerate(GROUPS) if piece_of(b0) == c] for c in range(len(PIECES))]
            for c in range(len(PIECES) + 1):
                if c < len(PIECES):
                    merge_piece("gcn", c)
                    b0, b1_ = PIECES[c]
                    r_, h_ = Rf_v[:, b0:b1_, :], h_v[:, b0:b1_, :]
                    tt(r_, r_, h_, ALU.add).then_inc(s["gcn_summed"], 1)
                    dve.wait_ge(s["gcn_summed"], c + 1)
                    tt(r_, r_, dinv[:, b0:b1_].unsqueeze(2).to_broadcast([P, b1_ - b0, F]),
                       ALU.mult).then_inc(s["gcn_lin_ready"], 1)
                for g in lin_groups[c - 1] if c >= 1 else []:
                    b0, b1_ = GROUPS[g]
                    dve.wait_ge(s["gcn_lin"], g + 1)
                    tt(h_v[:, b0:b1_, :], banks[6 + g % 2][:, 0:(b1_ - b0) * F].rearrange("p (b f) -> p b f", f=F),
                       rowwise(gcnb_r[:, :], b1_ - b0), ALU.add).then_inc(s["gcn_lin_used"], 1)
                    if g >= 1:
                        dve.wait_ge(s["gcn_lin_used"], g)
                        ln_stats_of(h_n3, *GROUPS[g - 1])
            dve.wait_ge(s["gcn_lin_used"], len(GROUPS))
            layernorm(h_n3, h_n3, tail=GROUPS[-1][0])
            gamma_beta_silu(h_n3)

            dve.wait_ge(s["att_lin"], len(GROUPS))
            st(v.tensor_copy(a4[:, :], banks[6][:, 0:4 * NB]), "att_ready")
            dve.wait_ge(s["adst_loaded"], 16)
            dve.wait_ge(s["adst_init"], 16)
            for h in range(HEADS):
                st(v.tensor_tensor_scan(adst_v[:, :, h], keep[:, 0:T], adst_v[:, :, h],
                                        q_init[:, F + HEADS + h:F + HEADS + h + 1], ALU.mult, ALU.add))
            prime("gat_acc", 2 * HALF)
            run_v = run[:, :].rearrange("p (t r) -> p t r", r=ROW_R)
            st(v.memset(run[:, (BODY - 1) * ROW_R:BODY * ROW_R], 0.0))
            m_half = [att_m[:, k * (HALF + 1) * HEADS:(k + 1) * (HALF + 1) * HEADS].rearrange("p (t h) -> p t h", h=HEADS)
                      for k in range(2)]
            s_half = [att_s[:, k * HALF * HEADS:(k + 1) * HALF * HEADS].rearrange("p (t h) -> p t h", h=HEADS)
                      for k in range(2)]
            r_half, w_half = ([att_rw[:, (2 * k + c) * HALF * HEADS:(2 * k + c + 1) * HALF * HEADS]
                               .rearrange("p (t h) -> p t h", h=HEADS) for k in range(2)] for c in range(2))
            st(v.memset(m_half[0][:, 0, :], NEG))
            for k in range(2):
                stage_idx_of("gat", 0, k)
            def gat_body(i, last):
                for k in range(2):
                    at = bass.ds(i * BODY + k * HALF, HALF)
                    steps = [0]

                    def small_step(ins):
                        steps[0] += 1
                        ins.then_inc(s["gat_small"], 1)
                        dve.wait_ge(s["gat_small"], i * (2 * SMALL) + k * SMALL + steps[0])

                    S, M, R_, W_ = s_half[k], m_half[k], r_half[k], w_half[k]
                    g_v = G[:, k * HALF * ROW_H:(k + 1) * HALF * ROW_H].rearrange("p (t r) -> p t r", r=ROW_H)
                    dve.wait_ge(s[f"gat_gathered{k}"], i * (16 * HALF) + 16 * HALF)
                    if not last:
                        stage_idx_of("gat", i + 1, k)
                    small_step(tt(S, g_v[:, :, F:F + HEADS], adst_v[:, at, :], ALU.add))
                    small_step(stt(S, S, SLOPE, S, ALU.mult, ALU.max))
                    for h in range(HEADS):
                        small_step(v.tensor_tensor_scan(M[:, 1:HALF + 1, h], pen[:, at], S[:, :, h], M[:, 0:1, h],
                                                        ALU.add, ALU.max))
                    small_step(v.tensor_copy(m_half[1 - k][:, 0, :], M[:, HALF, :]))
                    small_step(tt(R_, M[:, 0:HALF, :], M[:, 1:HALF + 1, :], ALU.subtract))
                    small_step(tt(R_, R_, pen[:, at].unsqueeze(2).to_broadcast([P, HALF, HEADS]), ALU.add))
                    small_step(tt(W_, S, M[:, 1:HALF + 1, :], ALU.subtract))
                    wait(dve, f"gat_written{k}", i * 16)
                    small_step(v.tensor_copy(run_v[:, k * HALF:(k + 1) * HALF, HEADS * F + HEADS:ROW_R],
                                             M[:, 1:HALF + 1, :]))
                    dve.wait_ge(s["gat_exp"], i * 2 + k + 1)
                    before = (k * HALF - 1) % BODY
                    for h in range(HEADS):
                        small_step(v.tensor_tensor_scan(run_v[:, k * HALF:(k + 1) * HALF, HEADS * F + h],
                                                        R_[:, :, h], W_[:, :, h],
                                                        run_v[:, before:before + 1, HEADS * F + h],
                                                        ALU.mult, ALU.add))
                    assert steps[0] == SMALL
                    for j in range(HALF):
                        n = k * HALF + j
                        before = (n - 1) % BODY
                        dve.wait_ge(s["gat_weighted"], i * (2 * BODY) + 2 * n + 2)
                        for h in range(HEADS):
                            dve.wait_ge(s["gat_acc"], i * (2 * BODY) + 2 * HALF + 2 * n - 1 + h)
                            stt(run_v[:, n, h * F:(h + 1) * F], run_v[:, before, h * F:(h + 1) * F],
                                R_[:, j, h:h + 1], weighted[:, (n * HEADS + h) * F:(n * HEADS + h + 1) * F],
                                ALU.mult, ALU.add).then_inc(s["gat_acc"], 1)
                    dve.wait_ge(s["gat_acc"], i * (2 * BODY) + (k + 2) * 2 * HALF)
            bodies(dve, gat_body)

            tail = (BODY - 1) * ROW_R
            mm_w = [mask_w[:, h * P:(h + 1) * P] for h in range(HEADS)]
            for h in range(HEADS):
                at = tail + HEADS * F + HEADS + h
                if h:
                    dve.wait_ge(s["gat_mrow"], h)
                st(ts(tmp_a[:, :], ident[:, :], run[:, at:at + 1], None, ALU.mult), "gat_mrow_ready")
            dve.wait_ge(s["gat_mrow"], HEADS)
            st(ts(sel[:, 0:P], mask_qp[:, :], -NEG, NEG, ALU.mult, ALU.add))
            for h in range(HEADS):
                mc = carry_s[:, HEADS * F + HEADS + h:HEADS * F + HEADS + h + 1]
                st(tt(mm_w[h], banks[0][:, h * P:(h + 1) * P], sel[:, 0:P], ALU.add))
                st(v.tensor_reduce(mc, mm_w[h], AX.X, ALU.max))
                st(ts(mm_w[h], mm_w[h], mc, None, ALU.subtract), "gat_exp_ready2")
            for h in range(HEADS):
                dve.wait_ge(s["gat_exp2"], 1)
                st(tt(mm_w[h], mm_w[h], mask_qp[:, :], ALU.mult), "gat_wt_ready")
            dve.wait_ge(s["gat_wt_T"], HEADS)
            for h in range(HEADS):
                st(v.tensor_copy(mask_w[:, (2 + h) * P:(3 + h) * P], banks[1][:, h * P:(h + 1) * P]), "gat_wt_copied")
            dve.wait_ge(s["gat_carry"], 1)
            st(v.tensor_copy(carry_s[:, 0:HEADS * F], banks[2][:, 0:HEADS * F]))
            st(v.tensor_copy(carry_s[:, HEADS * F:HEADS * F + HEADS], banks[3][:, 0:HEADS]))
            st(v.memset(carry_s[:, HEADS * F + 4:HEADS * F + 5], 1.0), "gat_carry_copied")

            for b in range(NB):
                ts(t_n[:, b * P:(b + 1) * P], iota_f[:, :], d_rel[:, b:b + 1], ends[:, 0:1],
                   ALU.is_equal, ALU.mult).then_inc(s["gat_sel"], 1)
            dve.wait_ge(s["gat_tail"], len(GROUPS))
            st(v.tensor_copy(carry5, banks[0][:, 0:5 * NB]))
            c5 = carry5.rearrange("p (b c) -> p b c", c=5)
            a4v = a4[:, :].rearrange("p (b c) -> p b c", c=4)

            def two(a):
                return a.rearrange("p (b h) -> p b h", h=HEADS)

            def heads_wide(a):
                return a.unsqueeze(2).to_broadcast([P, NB, HEADS])

            wr, wc, ws, dn, mx, ss = (two(a) for a in (wr2, wc2, ws2, dn2, mx2, ss2))
            st(tt(ss, a4v[:, :, 0:2], a4v[:, :, 2:4], ALU.add))
            st(stt(ss2, ss2, SLOPE, ss2, ALU.mult, ALU.max))
            st(ts(scr, c5[:, :, 4], -NEG, NEG, ALU.mult, ALU.add))
            st(tt(wc, c5[:, :, 2:4], heads_wide(scr), ALU.add))
            st(ts(scr, has, -NEG, NEG, ALU.mult, ALU.add))

            def cut2(a, c):
                return a[:, HEADS * PIECES[c][0]:HEADS * PIECES[c][1]]

            def logs_of(c):
                b0, b1_ = PIECES[c]
                dve.wait_ge(s[f"node_rows{c}"], (b1_ - b0) * 16 * 4)
                wr_, wc_, ws_, mx_, ss_ = (cut2(a, c) for a in (wr2, wc2, ws2, mx2, ss2))
                st(tt(wr[:, b0:b1_, :], R_v[:, b0:b1_, HEADS * F + HEADS:ROW_R],
                      scr[:, b0:b1_].unsqueeze(2).to_broadcast([P, b1_ - b0, HEADS]), ALU.add))
                st(tt(mx_, wr_, wc_, ALU.max))
                st(tt(mx_, mx_, ss_, ALU.max))
                st(tt(wr_, wr_, mx_, ALU.subtract))
                st(tt(wc_, wc_, mx_, ALU.subtract))
                st(tt(ws_, ss_, mx_, ALU.subtract), "gat_comb_ready")

            def weights_of(c):
                b0, b1_ = PIECES[c]
                wr_, wc_, ws_, mx_, dn_ = (cut2(a, c) for a in (wr2, wc2, ws2, mx2, dn2))
                dve.wait_ge(s["gat_comb"], c + 1)
                st(tt(dn[:, b0:b1_, :], wr[:, b0:b1_, :], R_v[:, b0:b1_, HEADS * F:HEADS * F + HEADS], ALU.mult))
                st(tt(mx[:, b0:b1_, :], wc[:, b0:b1_, :], c5[:, b0:b1_, 0:2], ALU.mult))
                st(tt(dn_, dn_, mx_, ALU.add))
                st(tt(dn_, dn_, ws_, ALU.add))
                st(v.reciprocal(dn_, dn_))
                st(ts(dn_, dn_, 1.0 / HEADS, None, ALU.mult))
                for w_ in (wr_, wc_, ws_):
                    st(tt(w_, w_, dn_, ALU.mult), "gat_weights")
            logs_of(0)
            weights_of(0)

            def merge(g):
                b0, b1_ = PAIRS[g]
                dve.wait_ge(s["gat_scaled"], HEADS * b1_)
                for b in range(b0, b1_):
                    for h in range(HEADS):
                        row = arena[:, b * ROW_R + h * F:b * ROW_R + (h + 1) * F]
                        stt(row, h_n[:, b * F:(b + 1) * F], ws2[:, b * HEADS + h:b * HEADS + h + 1], row,
                            ALU.mult, ALU.add).then_inc(s["gat_own_added"], 1)
                dve.wait_ge(s["gat_picked"], g + 1)
                for b in range(b0, b1_):
                    for h in range(HEADS):
                        row = arena[:, b * ROW_R + h * F:b * ROW_R + (h + 1) * F]
                        at = ((b - b0) * HEADS + h) * F
                        dve.wait_ge(s["gat_own_added"], b * HEADS + h + 1)
                        m = stt(row, banks[2 + g % 2][:, at:at + F], wc2[:, b * HEADS + h:b * HEADS + h + 1], row,
                                ALU.mult, ALU.add)
                    m.then_inc(s["gat_merged"], 1)

            for g in range(len(PAIRS) + 2):
                if g < len(PAIRS):
                    merge(g)
                if g >= 2:
                    b0, b1_ = PAIRS[g - 2]
                    dve.wait_ge(s["gat_lin"], g - 1)
                    tt(t_v[:, b0:b1_, :], banks[6 + g % 2][:, 0:(b1_ - b0) * F].rearrange("p (b f) -> p b f", f=F),
                       rowwise(gatb_r[:, :], b1_ - b0), ALU.add).then_inc(s["gat_lin_used"], 1)
                if g >= 3:
                    dve.wait_ge(s["gat_lin_used"], g - 2)
                    ln_stats_of(t_n3, *PAIRS[g - 3])
                if g + 5 in PIECE_PAIRS:
                    logs_of(PIECE_PAIRS.index(g + 5))
                if g + 4 in PIECE_PAIRS:
                    weights_of(PIECE_PAIRS.index(g + 4))
            dve.wait_ge(s["gat_lin_used"], len(PAIRS))
            layernorm(t_n3, t_n3, tail=PAIRS[-1][0])
            gamma_beta_silu(t_n3)
            for c, (b0, b1_) in enumerate(PIECES):
                tt(x_n3[:, b0:b1_, :], x_n3[:, b0:b1_, :], t_n3[:, b0:b1_, :], ALU.add).then_inc(s["x_added"], 1)
                if c >= 1:
                    dve.wait_ge(s["x_added"], c)
                    ln_stats_of(x_n3, *PIECES[c - 1])
            dve.wait_ge(s["x_added"], len(PIECES))

            layernorm(x_n3, h_n3, relu=True, tail=PIECES[-1][0])
            st(v.memset(scr, 0.0), "mlp_lin_ready")
            for g, (b0, b1_) in enumerate(PAIRS):
                dve.wait_ge(s["mlp_lin"], g + 1)
                pq = banks[6 + g % 2][:, 0:(b1_ - b0) * 2 * F].rearrange("p (b c f) -> p b c f", c=2, f=F)
                v.tensor_copy(t_v[:, b0:b1_, :], pq[:, :, 0, :]).then_inc(s["mlp_lin_used"], 1)
                v.tensor_copy(Rf_v[:, b0:b1_, :], pq[:, :, 1, :]).then_inc(s["mlp_lin_used"], 1)
            dve.wait_ge(s["mlp_lin_used"], 2 * len(PAIRS))
            st(ts(t_n[:, (NB - 1) * F:], t_n[:, (NB - 1) * F:], real_node[:, 0:1], None, ALU.mult))
            st(ts(Rf[:, (NB - 1) * F:], Rf[:, (NB - 1) * F:], real_node[:, 0:1], None, ALU.mult), "mlp_ready")
            dve.wait_ge(s["q_scattered"], NB * 16)
            dve.wait_ge(s["mlp_tables_written"], 2 * len(PIECES) * 16)
            st(v.memset(valid[:, :], 1.0))
            st(v.memset(valid[:, ELAST:T], 0.0))
            for c in range(HALF):
                at = slice(c * (F // HALF), (c + 1) * (F // HALF))
                if c == 0:
                    dve.wait_ge(s["q_init_loaded"], 16)
                st(v.tensor_copy(q_cur[:, (BODY - 1) * F + at.start:(BODY - 1) * F + at.stop], q_init[:, at]), "q_acc")
            for k in range(2):
                stage_idx_of("mlp", 0, k)
                stage_keep_of(0, k)
            def q_chain(i, k):
                keep_ready(1, i, k)
                dve.wait_ge(s[f"q_loaded{k}"], i * 16 + 16)
                wait(dve, f"pre_made{k}", i * 2)
                for j in range(HALF):
                    n = k * HALF + j
                    before = (n - 1) % BODY
                    stt(q_cur[:, n * F:(n + 1) * F], q_cur[:, before * F:(before + 1) * F],
                        keep_col(n), q_load[:, n * F:(n + 1) * F],
                        ALU.mult, ALU.add).then_inc(s["q_acc"], 1)
                    dve.wait_ge(s["q_acc"], i * BODY + HALF + n + 1)

            def q_chain_and_stage(i, k, last):
                q_chain(i, k)
                if not last:
                    stage_keep_of(i + 1, k)

            q_chain_and_stage(0, 0, False)

            def mlp_body(i, last, next_last=False):
                for k in range(2):
                    if k == 0:
                        q_chain_and_stage(i, 1, last)
                    elif not last:
                        q_chain_and_stage(i + 1, 0, next_last)
                    if not last:
                        dve.wait_ge(s[f"mlp_gathered{k}"], i * (16 * HALF) + 16 * HALF)
                        stage_idx_of("mlp", i + 1, k)
                    for g in range(2):
                        dve.wait_ge(s[f"pre_copied{2 * k + g}"], i + 1)
                        n0 = k * HALF + g * GROUP
                        v.bn_stats(stats[:, bass.ds(i * 24 + (2 * k + g) * 6, 6)],
                                   pre_s[:, n0 * P:(n0 + GROUP) * P]).then_inc(s["stats_made"], 1)
            mlp_body(0, False)
            with dve.Fori(1, NI - 2) as i:
                mlp_body(i, False)
            mlp_body(NI - 2, False, True)
            mlp_body(NI - 1, True)

            sv = stats.rearrange("p (g a c) -> p (g a) c", a=2, c=3)
            NS = 2 * (T // GROUP)
            s_cm = h_n[:, 0:NS]
            s_q = h_n[:, NS:2 * NS]

            def batch_norm(c0, o0, name):
                gcol, becol, bcol = (cols[:, c0 + c:c0 + c + 1] for c in range(3))
                mean, var, scale, shift, tmp = (bn[:, c:c + 1] for c in range(o0, o0 + 5))
                st(tt(s_cm, sv[:, :, 0], sv[:, :, 1], ALU.mult))
                st(v.tensor_reduce(mean, s_cm, AX.X, ALU.add))
                st(tt(s_q, s_cm, sv[:, :, 1], ALU.mult))
                st(tt(s_q, s_q, sv[:, :, 2], ALU.add))
                st(v.tensor_reduce(var, s_q, AX.X, ALU.add))
                st(ts(mean, mean, 1.0 / E, None, ALU.mult))
                st(tt(tmp, mean, mean, ALU.mult))
                st(ts(var, var, 1.0 / E, tmp, ALU.mult, ALU.subtract))
                st(ts(var, var, 0.0, BN_EPS, ALU.max, ALU.add), "bn_var")
                dve.wait_ge(s["bn_std"], count["bn_var"])
                st(v.reciprocal(var, var))
                st(tt(scale, var, gcol, ALU.mult))
                st(tt(mean, mean, bcol, ALU.add))
                st(tt(tmp, bcol, mean, ALU.subtract))
                st(ts(shift, tmp, scale, becol, ALU.mult, ALU.add), name)

            dve.wait_ge(s["stats_made"], 4 * NI)
            batch_norm(0, 0, "bn1_ready")
            def z_mask(i, q):
                dve.wait_ge(s["z_made"], i * 4 + q + 1)
                zc = z_s[:, q * GROUP * P:(q + 1) * GROUP * P].rearrange("p (t e) -> p t e", e=P)[:, :, P - 1]
                tt(zc, zc, valid[:, bass.ds(i * BODY + q * GROUP, GROUP)], ALU.mult).then_inc(s["z_masked"], 1)

            for q in range(2):
                z_mask(0, q)

            def h2_stats_body(i, last):
                for q in range(4):
                    if q < 2:
                        z_mask(i, q + 2)
                    elif not last:
                        z_mask(i + 1, q - 2)
                    dve.wait_ge(s["h2_made"], i * 4 + q + 1)
                    v.bn_stats(stats[:, bass.ds(i * 24 + q * 6, 6)], banks[q][:, :]).then_inc(s["stats_made"], 1)
            bodies(dve, h2_stats_body, 2)
            dve.wait_ge(s["stats_made"], 8 * NI)
            batch_norm(3, 8, "bn2_ready")
            st(ts(tmp_a[:, :], ident[:, :], bn[:, 10:11], None, ALU.mult), "bn2_row")
            dve.wait_ge(s["bn2_row_done"], 1)
            st(tt(w2Ts[:, :], w2T[:, :], banks[4][:, 0:F], ALU.mult))
            st(ts(tmp_a[:, :], ident[:, :], bn[:, 11:12], None, ALU.mult), "bn2_row")
            dve.wait_ge(s["bn2_row_done"], 2)
            st(v.tensor_copy(tmp_a[:, :], banks[5][:, 0:F]))
            parts_b = ones_b[:, :]
            total = carry_s[:, 0:F]
            st(v.memset(total, 0.0))
            for c in range(3):
                st(v.tensor_copy(parts_b, tmp_a[:, :]))
                st(stt(total, parts_b, ident[:, c:c + 1], total, ALU.mult, ALU.add))
                st(tt(tmp_a[:, :], tmp_a[:, :], parts_b, ALU.subtract))
            st(v.memset(ones_b[:, :], 1.0))
            st(v.tensor_copy(shift_rows[:, :].rearrange("p (g f) -> p g f", f=F), rowwise(total, GROUP)),
               "w2s_ready")
            prime("mlp_acc")

            stage_keep_of(0, 0)
            def mlp_sums(i, last):
                for q in range(4):
                    def restage():
                        if q == 0:
                            stage_keep_of(i, 1)
                        elif q == 2 and not last:
                            stage_keep_of(i + 1, 0)
                    if q % 2 == 0:
                        keep_ready(2, i, q // 2)
                    else:
                        restage = None
                    wait(dve, f"mlp_written{q}", i * 16)
                    dve.wait_ge(s["u_made"], i * 4 + q + 1)
                    chain("mlp", i, q * GROUP, GROUP, u_s, restage)
            bodies(dve, mlp_sums, 2)
            dve.wait_ge(s["mlp_carry"], 1)
            st(v.tensor_copy(carry_s[:, 0:F], banks[0][:, 0:F]), "mlp_carry_copied")
            pick("mlp")
            for c, (b0, b1_) in enumerate(PIECES):
                merge_piece("mlp", c)
                tt(x_v[:, b0:b1_, :], x_v[:, b0:b1_, :], Rf_v[:, b0:b1_, :], ALU.add).then_inc(s["out_ready"], 1)

        @block.scalar
        def _(act):
            a = nc.scalar.activation
            count = {}

            def std(ap):
                count["std"] = count.get("std", 0) + 1
                act.wait_ge(s["var_ready"], count["std"])
                a(ap, ap, ACT.Sqrt).then_inc(s["std_ready"], 1)

            def sigmoid(src_):
                for b0, b1_ in PIECES:
                    count["sig"] = count.get("sig", 0) + 1
                    act.wait_ge(s["sig_ready"], count["sig"])
                    a(sq_n[:, b0 * F:b1_ * F], src_[:, b0 * F:b1_ * F], ACT.Sigmoid).then_inc(s["sig_done"], 1)

            def ln_apply(src_, dst_, func):
                std(rs)
                count["ln"] = count.get("ln", 0) + 1
                act.wait_ge(s["ln_ready"], count["ln"])
                for b in range(LN_CUT):
                    a(dst_[:, b * F:(b + 1) * F], src_[:, b * F:(b + 1) * F], func, bias=nbias[:, b:b + 1],
                      scale=rs[:, b:b + 1]).then_inc(s["ln_applied"], 1)

            def wl(o, i_):
                act.dma_start(o, i_).then_inc(s["weights_loaded"], 16)
            wl(gcn_w_s[:, :], gcn_w)
            wl(gat_w_s[:, :], gat_w)
            wl(w1_s[:, :], W1)
            wl(w2_s[:, :], W2)
            wl(att_row[:, 0:2 * F], att_src.rearrange("h f -> (h f)").partition_broadcast(P))
            wl(att_row[:, 2 * F:4 * F], att_dst.rearrange("h f -> (h f)").partition_broadcast(P))
            for o, i_ in ((gcnb_r, gcn_b), (gatb_r, gat_b), (gamma_r, ln_gamma), (beta_r, ln_beta)):
                wl(o[:, :], i_.partition_broadcast(P))
            for c, i_ in enumerate((g1, be1, b1, g2, be2, b2)):
                wl(cols[:, c:c + 1], i_.rearrange("(p o) -> p o", o=1))

            act.wait_ge(s["w1_T"], 1)
            a(w1T[:, :], banks[2][:, 0:2 * F], ACT.Copy).then_inc(s["wT_copied"], 1)
            act.wait_ge(s["w2_T"], 1)
            a(w2T[:, :], banks[3][:, 0:F], ACT.Copy).then_inc(s["wT_copied"], 1)
            act.wait_ge(s["mask_T"], 2)
            a(mask_pq[:, :], banks[1][:, P:2 * P], ACT.Copy).then_inc(s["mask_copied"], 1)
            ln_apply(x_n, h_n, ACT.Relu)
            std(rs)
            act.wait_ge(s["zero_made"], 1)
            act.dma_start(adst_edge.rearrange("(p t) h -> p (t h)", t=T), zeros).then_inc(s["filled"], 16)

            def fill(i, last):
                wait(act, "gcn_acc", i * BODY)
                act.dma_start(q_edge_pt[:, bass.ds(i * BODY, BODY), :],
                              zeros[:, 0:BODY * F].rearrange("p (t f) -> p t f", f=F)).then_inc(s["filled"], 16)
            bodies(act, fill)

            def copies(prefix, groups, parts=1, ahead=None):
                for g, (b0, b1_) in enumerate(groups):
                    if ahead:
                        ahead(g)
                    act.wait_ge(s[prefix + "_T"], g + 1)
                    if g >= 2:
                        act.wait_ge(s[prefix + "_lin"], g - 1)
                    n = (b1_ - b0) * parts * P
                    a(stage_t[:, g % 2 * 512:g % 2 * 512 + n], banks[4 + g % 2][:, 0:n],
                      ACT.Copy).then_inc(s[prefix + "_T_copied"], 1)
            copies("gcn", GROUPS)
            ln_apply(h_n, h_n, ACT.Identity)
            sigmoid(h_n)
            copies("att", GROUPS)
            def gat_act(i, last):
                for k in range(2):
                    rw = att_rw[:, 2 * k * HALF * HEADS:2 * (k + 1) * HALF * HEADS]
                    w_ = att_rw[:, (2 * k + 1) * HALF * HEADS:2 * (k + 1) * HALF * HEADS]
                    act.wait_ge(s["gat_small"], i * (2 * SMALL) + k * SMALL + SMALL_LOGS)
                    a(rw, rw, ACT.Exp).then_inc(s["gat_exp"], 1)
                    act.wait_ge(s["gat_exp"], i * 2 + k + 1)
                    wait(act, "gat_acc", i * (2 * BODY) + k * 2 * HALF)
                    for j in range(HALF):
                        n = k * HALF + j
                        for h in range(HEADS):
                            a(weighted[:, (n * HEADS + h) * F:(n * HEADS + h + 1) * F], G[:, n * ROW_H:n * ROW_H + F],
                              ACT.Copy, scale=w_[:, j * HEADS + h:j * HEADS + h + 1]).then_inc(s["gat_weighted"], 1)
            bodies(act, gat_act)
            act.wait_ge(s["gat_exp_ready2"], HEADS)
            a(mask_w[:, 0:HEADS * P], mask_w[:, 0:HEADS * P], ACT.Exp).then_inc(s["gat_exp2"], 1)
            wrcs = small[:, 21 * NB:27 * NB].rearrange("p (k c) -> p k c", k=3)

            def weights_exp(c):
                b0, b1_ = PIECES[c]
                act.wait_ge(s["gat_comb_ready"], c + 1)
                w_ = wrcs[:, :, HEADS * b0:HEADS * b1_]
                a(w_, w_, ACT.Exp).then_inc(s["gat_comb"], 1)

            def scale_rows(g):
                if g in PIECE_PAIRS:
                    act.wait_ge(s["gat_weights"], 3 * (PIECE_PAIRS.index(g) + 1))
                for b in range(*PAIRS[g]):
                    for h in range(HEADS):
                        row = arena[:, b * ROW_R + h * F:b * ROW_R + (h + 1) * F]
                        a(row, row, ACT.Copy, scale=wr2[:, b * HEADS + h:b * HEADS + h + 1]).then_inc(s["gat_scaled"], 1)

            def scale_ahead(g):
                if g + 4 in PIECE_PAIRS:
                    weights_exp(PIECE_PAIRS.index(g + 4))
                if g + 3 < len(PAIRS):
                    scale_rows(g + 3)
            weights_exp(0)
            for g in range(3):
                scale_rows(g)
            copies("gat", PAIRS, HEADS, scale_ahead)
            ln_apply(t_n, t_n, ACT.Identity)
            sigmoid(t_n)
            ln_apply(x_n, h_n, ACT.Relu)
            copies("mlp", PAIRS)
            act.wait_ge(s["q_scattered"], NB * 16)
            act.wait_ge(s["mlp_tables_written"], 2 * len(PIECES) * 16)
            def pre_out(i, last):
                for k in range(2):
                    wait(act, f"pre_written{k}", i * 16)
                    for g in range(2):
                        wait(act, "stats_made", i * 4 + 2 * k + g - 3)
                        act.wait_ge(s[f"pre_made{k}"], i * 2 + g + 1)
                        n0 = k * HALF + g * GROUP
                        a(pre_s[:, n0 * P:(n0 + GROUP) * P], banks[2 * k + g][:, :],
                          ACT.Copy).then_inc(s[f"pre_copied{2 * k + g}"], 1)
                    for g in range(2):
                        act.wait_ge(s[f"pre_copied{2 * k + g}"], i + 1)
                    act.dma_start(pre_dram[i, :, k * HALF * P:(k + 1) * HALF * P],
                                  pre_s[:, k * HALF * P:(k + 1) * HALF * P]).then_inc(s[f"pre_written{k}"], 16)
            bodies(act, pre_out)
            for k in range(2):
                act.wait_ge(s[f"pre_written{k}"], NI * 16)
            act.wait_ge(s["bn_var"], 1)
            a(bn[:, 1:2], bn[:, 1:2], ACT.Sqrt).then_inc(s["bn_std"], 1)
            act.wait_ge(s["bn1_ready"], 1)

            def z_of(i, q, sweep):
                act.wait_ge(s[f"pre2_loaded{q}"], i * 16 + (sweep * NI + 1) * 16)
                wait(act, "h2_made", (i + sweep * NI) * 4 + q - 3)
                a(z_s[:, q * GROUP * P:(q + 1) * GROUP * P], G[:, q * GROUP * P:(q + 1) * GROUP * P],
                  ACT.Relu, bias=bn[:, 3:4], scale=bn[:, 2:3]).then_inc(s["z_made"], 1)

            def z_body(i, last):
                for q in range(4):
                    z_of(i, q, 0)
            bodies(act, z_body, 2)
            act.wait_ge(s["bn_var"], 2)
            a(bn[:, 9:10], bn[:, 9:10], ACT.Sqrt).then_inc(s["bn_std"], 1)
            act.wait_ge(s["w2s_ready"], 1)
            for q in range(2):
                z_of(0, q, 1)

            def u_body(i, last):
                for q in range(4):
                    if q < 2:
                        z_of(i, q + 2, 1)
                    elif not last:
                        z_of(i + 1, q - 2, 1)
                    wait(act, "mlp_acc", i * BODY + (q - 1) * GROUP)
                    act.wait_ge(s["h2_made"], (i + NI) * 4 + q + 1)
                    a(u_s[:, q * GROUP * P:(q + 1) * GROUP * P], banks[q][:, :], ACT.Relu).then_inc(s["u_made"], 1)
            bodies(act, u_body, 2)


_INS = ["x", "src", "dst", "L0_gnn_gcn_w", "L0_gnn_gcn_b", "L0_gnn_gat_w", "L0_gnn_att_src", "L0_gnn_att_dst",
        "L0_gnn_gat_b", "L0_gnn_ln_gamma", "L0_gnn_ln_beta", "L1_gnn_W1", "L1_gnn_b1", "L1_gnn_g1", "L1_gnn_be1",
        "L1_gnn_W2", "L1_gnn_b2", "L1_gnn_g2", "L1_gnn_be2"]


def kernel(**inputs):
    import numpy as _np
    import concourse.bacc as _bacc
    from concourse import mybir as _mybir
    from concourse.bass_utils import run_bass_kernel_spmd as _run

    nc = _bacc.Bacc("TRN2", target_bir_lowering=False, num_devices=1)
    arrays, args = {}, []
    for name in _INS:
        a = _np.ascontiguousarray(inputs[name])
        arrays[f"in_{name}_dram"] = a
        args.append(nc.dram_tensor(f"in_{name}_dram", a.shape, _mybir.dt.from_np(a.dtype), kind="ExternalInput").ap())
    out = nc.dram_tensor("out_dram", arrays["in_x_dram"].shape, _mybir.dt.float32, kind="ExternalOutput").ap()
    gnn_kernel(nc, *args, out)
    r = _run(nc, [arrays], core_ids=[0])
    return r.results[0]["out_dram"]
```
